# Optimizing a Trainium2 kernel written in Bass

```python
import numpy as np
import jax
import jax.numpy as jnp

def _softmax(x, axis=-1):
    return jax.nn.softmax(x, axis=axis)

def _gelu(x):
    return jax.nn.gelu(x, approximate=True)

def _silu(x):
    return jax.nn.silu(x)

def _sigmoid(x):
    return jax.nn.sigmoid(x)

def _layernorm(x, axis=-1, eps=1e-05):
    m = jnp.mean(x, axis=axis, keepdims=True)
    v = jnp.var(x, axis=axis, keepdims=True)
    return (x - m) / jnp.sqrt(v + eps)

def _scatter_add(tgt, idx, src, axis=0):
    return tgt.at[idx].add(src)

def _segment_sum(src, seg, n):
    return jax.ops.segment_sum(src, seg, n)
kernel_name = 'mk_xattn_ffn_d4_seqx_r8_46470b'

def setup_inputs(seed: int=0):
    np.random.seed(seed)
    _w = jnp.asarray

    def _rec_inputs():
        import jax
        import jax.numpy as jnp
        _rk = jax.random.key(seed)
        x = -0.0002928 + 1 * jax.random.normal(jax.random.fold_in(_rk, 1), (8, 256, 128), jnp.float32)
        _lenS = 256 - jax.random.randint(jax.random.fold_in(_rk, 7), (8,), 0, max(1, 256 // 4) + 1, jnp.int32)
        _lenS2 = 512 - jax.random.randint(jax.random.fold_in(_rk, 8), (8,), 0, max(1, 512 // 4) + 1, jnp.int32)
        _ctx_1024P = jax.random.normal(jax.random.fold_in(_rk, 11), (8, 16, 128), jnp.float32)
        _ctx_1024c = jax.random.dirichlet(jax.random.fold_in(_rk, 511), 0.3 * jnp.ones((16,), jnp.float32), (8, 512))
        _ctx_1024t = jnp.einsum('bsk,bkd->bsd', _ctx_1024c, _ctx_1024P)
        _ctx_1024t = _ctx_1024t * jax.lax.rsqrt(jnp.mean(jnp.square(_ctx_1024t)) + 1e-12) * 0.953939
        ctx_1024 = 2.81802e-05 + 1.00001 * (_ctx_1024t + 0.3 * jax.random.normal(jax.random.fold_in(_rk, 611), (8, 512, 128), jnp.float32))
        _validS = jnp.arange(256)[None, :] < _lenS[:, None]
        _validS2 = jnp.arange(512)[None, :] < _lenS2[:, None]
        _causal = jnp.tril(jnp.ones((256, 256), dtype=bool))
        mask_BxS2_ff1 = jnp.where(jnp.ones((8, 512), dtype=bool), 1.0, 0.0).astype(jnp.float32)
        mask_BxS2_bf1 = jnp.ones((8, 512), dtype=bool)
        return (x, ctx_1024, mask_BxS2_ff1, mask_BxS2_bf1)
    x, ctx_1024, mask_BxS2_ff1, mask_BxS2_bf1 = _rec_inputs()

    def _L0_xattn_setup():
        import jax, jax.numpy as jnp
        import numpy as np
        DIM_Q = 128
        DIM_V = 128
        NUM_HEADS = 8
        LN_EPS = 1e-05

        def _layernorm(x, gamma, beta):
            mu = jnp.mean(x, axis=-1, keepdims=True)
            var = jnp.mean((x - mu) ** 2, axis=-1, keepdims=True)
            return (x - mu) * jax.lax.rsqrt(var + LN_EPS) * gamma + beta
        key = jax.random.key(seed)
        ks = jax.random.split(key, 12)
        B, NQ, NK = (4, 128, 512)
        s_in = 1.0 / np.sqrt(DIM_Q)
        s_v = 1.0 / np.sqrt(DIM_V)
        return {'Q': jax.random.normal(ks[0], (B, NQ, DIM_Q), dtype=jnp.float32), 'K': jax.random.normal(ks[1], (B, NK, DIM_Q), dtype=jnp.float32), 'Wq': jax.random.uniform(ks[2], (DIM_V, DIM_Q), jnp.float32, -s_in, s_in), 'bq': jax.random.uniform(ks[3], (DIM_V,), jnp.float32, -s_in, s_in), 'Wk': jax.random.uniform(ks[4], (DIM_V, DIM_Q), jnp.float32, -s_in, s_in), 'bk': jax.random.uniform(ks[5], (DIM_V,), jnp.float32, -s_in, s_in), 'Wv': jax.random.uniform(ks[6], (DIM_V, DIM_Q), jnp.float32, -s_in, s_in), 'bv': jax.random.uniform(ks[7], (DIM_V,), jnp.float32, -s_in, s_in), 'Wo': jax.random.uniform(ks[8], (DIM_V, DIM_V), jnp.float32, -s_v, s_v), 'bo': jax.random.uniform(ks[9], (DIM_V,), jnp.float32, -s_v, s_v), 'g0': jnp.ones((DIM_V,), jnp.float32), 'b0': jnp.zeros((DIM_V,), jnp.float32), 'g1': jnp.ones((DIM_V,), jnp.float32), 'b1': jnp.zeros((DIM_V,), jnp.float32)}
    _L0_xattn_all = _L0_xattn_setup()
    _L0_xattn_in = {k: v for k, v in _L0_xattn_all.items() if k in ('Wq', 'bq', 'Wk', 'bk', 'Wv', 'bv', 'Wo', 'bo', 'g0', 'b0', 'g1', 'b1')}
    del _L0_xattn_all

    def _L0_ffn_setup():
        import jax, jax.numpy as jnp
        import numpy as np
        DIM = 128
        DEPTH = 2
        HEADS = 8
        DIM_HEAD = 64
        WINDOW = 64
        INNER = HEADS * DIM_HEAD
        HID = int(DIM * 4 * 2 / 3)
        B, N = (2, 1024)
        QK_SCALE = 8.0

        def shift_token(t):
            t1, t2 = jnp.split(t, 2, axis=-1)
            t2 = jnp.pad(t2, ((0, 0), (1, 0), (0, 0)))[:, :-1]
            return jnp.concatenate([t1, t2], axis=-1)

        def l2norm(t):
            return t / jnp.clip(jnp.linalg.norm(t, axis=-1, keepdims=True), 1e-12)

        def rotate_half(x):
            x1, x2 = jnp.split(x, 2, axis=-1)
            return jnp.concatenate([-x2, x1], axis=-1)

        def rotary_xpos(q, k):
            n = q.shape[-2]
            half_idx = jnp.arange(0, DIM_HEAD, 2, dtype=jnp.float32)
            inv_freq = 1.0 / 10000.0 ** (half_idx / DIM_HEAD)
            t = jnp.arange(n, dtype=jnp.float32)
            freqs = t[:, None] * inv_freq[None, :]
            freqs = jnp.concatenate([freqs, freqs], axis=-1)
            base = (half_idx + 0.4 * DIM_HEAD) / (1.4 * DIM_HEAD)
            power = (t - n // 2) / float(WINDOW // 2)
            scale = base[None, :] ** power[:, None]
            scale = jnp.concatenate([scale, scale], axis=-1)
            cos, sin = (jnp.cos(freqs), jnp.sin(freqs))
            q = q * cos * scale + rotate_half(q) * sin * scale
            k = k * cos / scale + rotate_half(k) * sin / scale
            return (q, k)

        def local_attention(q, k, v):
            b, h, n, d = q.shape
            w = n // WINDOW
            bq = q.reshape(b, h, w, WINDOW, d) * QK_SCALE
            bk = k.reshape(b, h, w, WINDOW, d)
            bv = v.reshape(b, h, w, WINDOW, d)

            def look_around(t):
                p = jnp.pad(t, ((0, 0), (0, 0), (1, 0), (0, 0), (0, 0)))
                return jnp.concatenate([p[:, :, :w], p[:, :, 1:]], axis=3)
            bk, bv = (look_around(bk), look_around(bv))
            bt = jnp.arange(n).reshape(w, WINDOW)
            btp = jnp.pad(bt, ((1, 0), (0, 0)), constant_values=-1)
            btk = jnp.concatenate([btp[:w], btp[1:]], axis=1)
            sim = jnp.einsum('bhwid,bhwjd->bhwij', bq, bk)
            i = bt[:, :, None]
            j = btk[:, None, :]
            mask = (i < j) | (i > j + WINDOW) | (j == -1)
            sim = jnp.where(mask, -jnp.finfo(sim.dtype).max, sim)
            attn = jax.nn.softmax(sim, axis=-1)
            out = jnp.einsum('bhwij,bhwjd->bhwid', attn, bv)
            return out.reshape(b, h, n, d)

        def _layer(x, wqkv, qs, ksc, wo, lg, lb, w1, b1, w2, b2):
            b, n, _ = x.shape
            h = shift_token(x)
            qkv = h @ wqkv
            q, k, v = jnp.split(qkv, 3, axis=-1)
            to_heads = lambda t: t.reshape(b, n, HEADS, DIM_HEAD).transpose(0, 2, 1, 3)
            q, k, v = (to_heads(q), to_heads(k), to_heads(v))
            q = l2norm(q) * qs
            k = l2norm(k) * ksc
            q, k = rotary_xpos(q, k)
            o = local_attention(q, k, v)
            o = o.transpose(0, 2, 1, 3).reshape(b, n, INNER)
            x = x + o @ wo
            h = shift_token(x)
            mu = h.mean(-1, keepdims=True)
            var = h.var(-1, keepdims=True)
            h = (h - mu) / jnp.sqrt(var + 1e-05) * lg + lb
            h = h @ w1 + b1
            a, g = jnp.split(h, 2, axis=-1)
            h = a * jax.nn.gelu(g, approximate=False)
            x = x + h @ w2 + b2
            return x
        key = jax.random.key(seed)
        ks = jax.random.split(key, 6)
        return {'x': jax.random.normal(ks[0], (B, N, DIM), jnp.float32), 'wqkv': jax.random.normal(ks[1], (DEPTH, DIM, 3 * INNER), jnp.float32) * 0.02, 'q_scale': jnp.ones((DEPTH, DIM_HEAD), jnp.float32), 'k_scale': jnp.ones((DEPTH, DIM_HEAD), jnp.float32), 'wo': jax.random.normal(ks[2], (DEPTH, INNER, DIM), jnp.float32) * 0.02, 'ln_g': jnp.ones((DEPTH, DIM), jnp.float32), 'ln_b': jnp.zeros((DEPTH, DIM), jnp.float32), 'w1': jax.random.normal(ks[3], (DEPTH, DIM, 2 * HID), jnp.float32) * 0.02, 'b1': jnp.zeros((DEPTH, 2 * HID), jnp.float32), 'w2': jax.random.normal(ks[4], (DEPTH, HID, DIM), jnp.float32) * 0.02, 'b2': jnp.zeros((DEPTH, DIM), jnp.float32)}
    _L0_ffn_all = _L0_ffn_setup()
    _L0_ffn_in = {k: v for k, v in _L0_ffn_all.items() if k in ('wqkv', 'q_scale', 'k_scale', 'wo', 'ln_g', 'ln_b', 'w1', 'b1', 'w2', 'b2')}
    del _L0_ffn_all

    def _L1_xattn_setup():
        import jax, jax.numpy as jnp
        import numpy as np
        H = 128
        NH = 16
        HD = H // NH
        B, S = (4, 256)

        def _split_heads(x):
            b, s, _ = x.shape
            return x.reshape(b, s, NH, HD).transpose(0, 2, 1, 3)
        key = jax.random.key(seed)
        ks = jax.random.split(key, 12)
        sc = 1.0 / np.sqrt(H)
        inp = {'query': jax.random.normal(ks[0], (B, S, H), jnp.float32), 'key_': jax.random.normal(ks[1], (B, S, H), jnp.float32), 'value': jax.random.normal(ks[2], (B, S, H), jnp.float32), 'attention_mask': jnp.ones((B, S), jnp.float32), 'Wq': jax.random.normal(ks[3], (H, H), jnp.float32) * sc, 'bq': jnp.zeros((H,), jnp.float32), 'Wk': jax.random.normal(ks[4], (H, H), jnp.float32) * sc, 'bk': jnp.zeros((H,), jnp.float32), 'Wv': jax.random.normal(ks[5], (H, H), jnp.float32) * sc, 'bv': jnp.zeros((H,), jnp.float32), 'Wo': jax.random.normal(ks[6], (H, H), jnp.float32) * sc, 'bo': jnp.zeros((H,), jnp.float32)}
        return inp
    _L1_xattn_all = _L1_xattn_setup()
    _L1_xattn_in = {k: v for k, v in _L1_xattn_all.items() if k in ('Wq', 'bq', 'Wk', 'bk', 'Wv', 'bv', 'Wo', 'bo')}
    del _L1_xattn_all

    def _L1_ffn_setup():
        import jax, jax.numpy as jnp
        import numpy as np
        H, I, E_ROUTED, TOP_K = (128, 352, 7, 2)
        B, S = (4, 256)

        def _expert(h, g, u, d):
            return jnp.einsum('...i,hi->...h', jax.nn.silu(h @ g.T) * (h @ u.T), d)
        key = jax.random.key(seed)
        ks = jax.random.split(key, 10)
        sc = 0.02
        return {'x': jax.random.normal(ks[0], (B, S, H), dtype=jnp.float32), 'sg': jax.random.normal(ks[1], (I, H), dtype=jnp.float32) * sc, 'su': jax.random.normal(ks[2], (I, H), dtype=jnp.float32) * sc, 'sd': jax.random.normal(ks[3], (H, I), dtype=jnp.float32) * sc, 'rg': jax.random.normal(ks[4], (E_ROUTED, I, H), dtype=jnp.float32) * sc, 'ru': jax.random.normal(ks[5], (E_ROUTED, I, H), dtype=jnp.float32) * sc, 'rd': jax.random.normal(ks[6], (E_ROUTED, H, I), dtype=jnp.float32) * sc, 'wr': jax.random.normal(ks[7], (E_ROUTED, H), dtype=jnp.float32) * sc, 'rb': jnp.zeros((E_ROUTED,), dtype=jnp.float32)}
    _L1_ffn_all = _L1_ffn_setup()
    _L1_ffn_in = {k: v for k, v in _L1_ffn_all.items() if k in ('sg', 'su', 'sd', 'rg', 'ru', 'rd', 'wr', 'rb')}
    del _L1_ffn_all

    def _L2_xattn_setup():
        import jax, jax.numpy as jnp
        import numpy as np
        NUM_HEADS = 16
        CAPACITY = 64
        ROPE_BASE = 10000.0

        def _rope_factor(positions, dim):
            freqs = jnp.exp(jnp.linspace(0.0, -1.0, dim // 2) * jnp.log(jnp.float32(ROPE_BASE)))
            angles = positions[..., None] * freqs
            return jnp.concatenate([jnp.sin(angles), jnp.cos(angles)], axis=-1)
        key = jax.random.key(seed)
        ks = jax.random.split(key, 6)
        B, Sq, Skv, D = (4, 512, 512, 128)
        return {'query_seq': jax.random.normal(ks[0], (B, Sq, D), jnp.float32), 'value_seq': jax.random.normal(ks[1], (B, Skv, D), jnp.float32), 'router_w': jax.random.normal(ks[2], (1, D), jnp.float32) * 0.02, 'q_w': jax.random.normal(ks[3], (D, D), jnp.float32) * 0.02, 'kv_w': jax.random.normal(ks[4], (2 * D, D), jnp.float32) * 0.02, 'out_w': jax.random.normal(ks[5], (D, D), jnp.float32) * 0.02}
    _L2_xattn_all = _L2_xattn_setup()
    _L2_xattn_in = {k: v for k, v in _L2_xattn_all.items() if k in ('router_w', 'q_w', 'kv_w', 'out_w')}
    del _L2_xattn_all

    def _L2_ffn_setup():
        import jax, jax.numpy as jnp
        import numpy as np
        TOP_K = 2
        EPS = 1e-20
        key = jax.random.key(seed)
        ks = jax.random.split(key, 8)
        B, S, H, E, D = (4, 256, 128, 8, 256)
        s = 0.02
        return {'x': jax.random.normal(ks[0], (B, S, H), dtype=jnp.float32), 'Wr': jax.random.normal(ks[1], (H, E), dtype=jnp.float32) * s, 'Wg': jax.random.normal(ks[2], (E, H, D), dtype=jnp.float32) * s, 'Wu': jax.random.normal(ks[3], (E, H, D), dtype=jnp.float32) * s, 'Wd': jax.random.normal(ks[4], (E, D, H), dtype=jnp.float32) * s, 'Sg': jax.random.normal(ks[5], (H, D), dtype=jnp.float32) * s, 'Su': jax.random.normal(ks[6], (H, D), dtype=jnp.float32) * s, 'Sd': jax.random.normal(ks[7], (D, H), dtype=jnp.float32) * s}
    _L2_ffn_all = _L2_ffn_setup()
    _L2_ffn_in = {k: v for k, v in _L2_ffn_all.items() if k in ('Wr', 'Wg', 'Wu', 'Wd', 'Sg', 'Su', 'Sd')}
    del _L2_ffn_all

    def _L3_xattn_setup():
        import jax, jax.numpy as jnp
        import numpy as np
        HEADS, QSIZE, KSIZE = (16, 64, 64)
        key = jax.random.key(seed)
        ks = jax.random.split(key, 8)
        B, S, D = (4, 256, 128)
        sd = 1.0 / np.sqrt(D)
        return {'q_in': jax.random.normal(ks[0], (B, S, D), jnp.float32), 'k_in': jax.random.normal(ks[1], (B, S, D), jnp.float32), 'v_in': jax.random.normal(ks[2], (B, S, D), jnp.float32), 'key_mask': jnp.ones((B, S), dtype=bool), 'Wq': jax.random.normal(ks[3], (D, HEADS * QSIZE), jnp.float32) * sd, 'bq': jnp.zeros((HEADS * QSIZE,), jnp.float32), 'Wk': jax.random.normal(ks[4], (D, HEADS * QSIZE), jnp.float32) * sd, 'bk': jnp.zeros((HEADS * QSIZE,), jnp.float32), 'Wv': jax.random.normal(ks[5], (D, HEADS * KSIZE), jnp.float32) * sd, 'bv': jnp.zeros((HEADS * KSIZE,), jnp.float32), 'Wo': jax.random.normal(ks[6], (HEADS * KSIZE, D), jnp.float32) * sd, 'bo': jnp.zeros((D,), jnp.float32)}
    _L3_xattn_all = _L3_xattn_setup()
    _L3_xattn_in = {k: v for k, v in _L3_xattn_all.items() if k in ('Wq', 'bq', 'Wk', 'bk', 'Wv', 'bv', 'Wo', 'bo')}
    del _L3_xattn_all

    def _L3_ffn_setup():
        import jax, jax.numpy as jnp
        import numpy as np
        EPS = 1e-05

        def _layernorm(x, w, b):
            mu = jnp.mean(x, axis=-1, keepdims=True)
            var = jnp.mean((x - mu) ** 2, axis=-1, keepdims=True)
            return (x - mu) * jax.lax.rsqrt(var + EPS) * w + b

        def _rope_tables(T, D, base=10000.0):
            inv_freq = 1.0 / base ** (jnp.arange(0, D, 2, dtype=jnp.float32) / D)
            t = jnp.arange(T, dtype=jnp.float32)
            freqs = jnp.einsum('i,j->ij', t, inv_freq)
            emb = jnp.concatenate([freqs, freqs], axis=-1)
            return (jnp.cos(emb), jnp.sin(emb))

        def _rotate_half(x):
            x1, x2 = (x[..., :x.shape[-1] // 2], x[..., x.shape[-1] // 2:])
            return jnp.concatenate([-x2, x1], axis=-1)

        def _attn(x, ln_w, ln_b, conv_w, attn_w, proj_w, n_head):
            B, T, C = x.shape
            D = C // n_head
            h = _layernorm(x, ln_w, ln_b)
            hc = jnp.transpose(h, (0, 2, 1))
            hc = jnp.pad(hc, ((0, 0), (0, 0), (2, 0)))
            hc = jax.lax.conv_general_dilated(hc, conv_w, window_strides=(1,), padding='VALID', dimension_numbers=('NCH', 'OIH', 'NCH'), feature_group_count=C)
            h = jnp.transpose(hc, (0, 2, 1))
            qkv = h @ attn_w
            q, k, v = jnp.split(qkv, 3, axis=-1)
            q = q.reshape(B, T, n_head, D)
            k = k.reshape(B, T, n_head, D)
            v = v.reshape(B, T, n_head, D)
            cos, sin = _rope_tables(T, D)
            cos = cos[None, :, None, :]
            sin = sin[None, :, None, :]
            q = q * cos + _rotate_half(q) * sin
            k = k * cos + _rotate_half(k) * sin
            scores = jnp.einsum('bqhd,bkhd->bhqk', q, k) / jnp.sqrt(jnp.float32(D))
            causal = jnp.tril(jnp.ones((T, T), dtype=bool))
            scores = jnp.where(causal, scores, jnp.float32(-1e+30))
            p = jax.nn.softmax(scores, axis=-1)
            y = jnp.einsum('bhqk,bkhd->bqhd', p, v).reshape(B, T, C)
            return y @ proj_w

        def _moe(x, ln_w, ln_b, router_w, expert_wv, expert_proj):
            h = _layernorm(x, ln_w, ln_b)
            logits = h @ router_w
            expert_idx = jnp.argmax(logits, axis=-1)
            E = router_w.shape[-1]
            out = jnp.zeros_like(x)
            for e in range(E):
                gv = h @ expert_wv[e]
                gate_raw, value = jnp.split(gv, 2, axis=-1)
                y = gate_raw * jax.nn.sigmoid(gate_raw) * value @ expert_proj[e]
                out = out + jnp.where((expert_idx == e)[..., None], y, 0.0)
            return out
        C, H, E, B, T = (128, 16, 4, 4, 128)
        Dff = 4 * C
        key = jax.random.key(seed)
        ks = jax.random.split(key, 8)
        s = 0.02
        return {'x': jax.random.normal(ks[0], (B, T, C), dtype=jnp.float32), 'ln1_w': jnp.ones((C,), jnp.float32), 'ln1_b': jnp.zeros((C,), jnp.float32), 'ln2_w': jnp.ones((C,), jnp.float32), 'ln2_b': jnp.zeros((C,), jnp.float32), 'conv_w': jax.random.normal(ks[1], (C, 1, 3), dtype=jnp.float32) * 0.1, 'attn_w': jax.random.normal(ks[2], (C, 3 * C), dtype=jnp.float32) * s, 'proj_w': jax.random.normal(ks[3], (C, C), dtype=jnp.float32) * s, 'router_w': jax.random.normal(ks[4], (C, E), dtype=jnp.float32) * s, 'expert_wv': jax.random.normal(ks[5], (E, C, 2 * Dff), dtype=jnp.float32) * s, 'expert_proj': jax.random.normal(ks[6], (E, Dff, C), dtype=jnp.float32) * s}
    _L3_ffn_all = _L3_ffn_setup()
    _L3_ffn_in = {k: v for k, v in _L3_ffn_all.items() if k in ('ln1_w', 'ln1_b', 'ln2_w', 'ln2_b', 'conv_w', 'attn_w', 'proj_w', 'router_w', 'expert_wv', 'expert_proj')}
    del _L3_ffn_all
    return {'x': x, 'ctx_1024': ctx_1024, 'mask_BxS2_ff1': mask_BxS2_ff1, 'mask_BxS2_bf1': mask_BxS2_bf1, 'L0_xattn_Wq': _L0_xattn_in['Wq'], 'L0_xattn_bq': _L0_xattn_in['bq'], 'L0_xattn_Wk': _L0_xattn_in['Wk'], 'L0_xattn_bk': _L0_xattn_in['bk'], 'L0_xattn_Wv': _L0_xattn_in['Wv'], 'L0_xattn_bv': _L0_xattn_in['bv'], 'L0_xattn_Wo': _L0_xattn_in['Wo'], 'L0_xattn_bo': _L0_xattn_in['bo'], 'L0_xattn_g0': _L0_xattn_in['g0'], 'L0_xattn_b0': _L0_xattn_in['b0'], 'L0_xattn_g1': _L0_xattn_in['g1'], 'L0_xattn_b1': _L0_xattn_in['b1'], 'L0_ffn_wqkv': _L0_ffn_in['wqkv'], 'L0_ffn_q_scale': _L0_ffn_in['q_scale'], 'L0_ffn_k_scale': _L0_ffn_in['k_scale'], 'L0_ffn_wo': _L0_ffn_in['wo'], 'L0_ffn_ln_g': _L0_ffn_in['ln_g'], 'L0_ffn_ln_b': _L0_ffn_in['ln_b'], 'L0_ffn_w1': _L0_ffn_in['w1'], 'L0_ffn_b1': _L0_ffn_in['b1'], 'L0_ffn_w2': _L0_ffn_in['w2'], 'L0_ffn_b2': _L0_ffn_in['b2'], 'L1_xattn_Wq': _L1_xattn_in['Wq'], 'L1_xattn_bq': _L1_xattn_in['bq'], 'L1_xattn_Wk': _L1_xattn_in['Wk'], 'L1_xattn_bk': _L1_xattn_in['bk'], 'L1_xattn_Wv': _L1_xattn_in['Wv'], 'L1_xattn_bv': _L1_xattn_in['bv'], 'L1_xattn_Wo': _L1_xattn_in['Wo'], 'L1_xattn_bo': _L1_xattn_in['bo'], 'L1_ffn_sg': _L1_ffn_in['sg'], 'L1_ffn_su': _L1_ffn_in['su'], 'L1_ffn_sd': _L1_ffn_in['sd'], 'L1_ffn_rg': _L1_ffn_in['rg'], 'L1_ffn_ru': _L1_ffn_in['ru'], 'L1_ffn_rd': _L1_ffn_in['rd'], 'L1_ffn_wr': _L1_ffn_in['wr'], 'L1_ffn_rb': _L1_ffn_in['rb'], 'L2_xattn_router_w': _L2_xattn_in['router_w'], 'L2_xattn_q_w': _L2_xattn_in['q_w'], 'L2_xattn_kv_w': _L2_xattn_in['kv_w'], 'L2_xattn_out_w': _L2_xattn_in['out_w'], 'L2_ffn_Wr': _L2_ffn_in['Wr'], 'L2_ffn_Wg': _L2_ffn_in['Wg'], 'L2_ffn_Wu': _L2_ffn_in['Wu'], 'L2_ffn_Wd': _L2_ffn_in['Wd'], 'L2_ffn_Sg': _L2_ffn_in['Sg'], 'L2_ffn_Su': _L2_ffn_in['Su'], 'L2_ffn_Sd': _L2_ffn_in['Sd'], 'L3_xattn_Wq': _L3_xattn_in['Wq'], 'L3_xattn_bq': _L3_xattn_in['bq'], 'L3_xattn_Wk': _L3_xattn_in['Wk'], 'L3_xattn_bk': _L3_xattn_in['bk'], 'L3_xattn_Wv': _L3_xattn_in['Wv'], 'L3_xattn_bv': _L3_xattn_in['bv'], 'L3_xattn_Wo': _L3_xattn_in['Wo'], 'L3_xattn_bo': _L3_xattn_in['bo'], 'L3_ffn_ln1_w': _L3_ffn_in['ln1_w'], 'L3_ffn_ln1_b': _L3_ffn_in['ln1_b'], 'L3_ffn_ln2_w': _L3_ffn_in['ln2_w'], 'L3_ffn_ln2_b': _L3_ffn_in['ln2_b'], 'L3_ffn_conv_w': _L3_ffn_in['conv_w'], 'L3_ffn_attn_w': _L3_ffn_in['attn_w'], 'L3_ffn_proj_w': _L3_ffn_in['proj_w'], 'L3_ffn_router_w': _L3_ffn_in['router_w'], 'L3_ffn_expert_wv': _L3_ffn_in['expert_wv'], 'L3_ffn_expert_proj': _L3_ffn_in['expert_proj']}

def reference(x, ctx_1024, mask_BxS2_ff1, mask_BxS2_bf1, L0_xattn_Wq, L0_xattn_bq, L0_xattn_Wk, L0_xattn_bk, L0_xattn_Wv, L0_xattn_bv, L0_xattn_Wo, L0_xattn_bo, L0_xattn_g0, L0_xattn_b0, L0_xattn_g1, L0_xattn_b1, L0_ffn_wqkv, L0_ffn_q_scale, L0_ffn_k_scale, L0_ffn_wo, L0_ffn_ln_g, L0_ffn_ln_b, L0_ffn_w1, L0_ffn_b1, L0_ffn_w2, L0_ffn_b2, L1_xattn_Wq, L1_xattn_bq, L1_xattn_Wk, L1_xattn_bk, L1_xattn_Wv, L1_xattn_bv, L1_xattn_Wo, L1_xattn_bo, L1_ffn_sg, L1_ffn_su, L1_ffn_sd, L1_ffn_rg, L1_ffn_ru, L1_ffn_rd, L1_ffn_wr, L1_ffn_rb, L2_xattn_router_w, L2_xattn_q_w, L2_xattn_kv_w, L2_xattn_out_w, L2_ffn_Wr, L2_ffn_Wg, L2_ffn_Wu, L2_ffn_Wd, L2_ffn_Sg, L2_ffn_Su, L2_ffn_Sd, L3_xattn_Wq, L3_xattn_bq, L3_xattn_Wk, L3_xattn_bk, L3_xattn_Wv, L3_xattn_bv, L3_xattn_Wo, L3_xattn_bo, L3_ffn_ln1_w, L3_ffn_ln1_b, L3_ffn_ln2_w, L3_ffn_ln2_b, L3_ffn_conv_w, L3_ffn_attn_w, L3_ffn_proj_w, L3_ffn_router_w, L3_ffn_expert_wv, L3_ffn_expert_proj):
    import jax
    import jax.numpy as jnp

    def _L0_xattn_ref(Q, K, Wq, bq, Wk, bk, Wv, bv, Wo, bo, g0, b0, g1, b1):
        import jax, jax.numpy as jnp
        import numpy as np
        DIM_Q = 128
        DIM_V = 128
        NUM_HEADS = 8
        LN_EPS = 1e-05

        def _layernorm(x, gamma, beta):
            mu = jnp.mean(x, axis=-1, keepdims=True)
            var = jnp.mean((x - mu) ** 2, axis=-1, keepdims=True)
            return (x - mu) * jax.lax.rsqrt(var + LN_EPS) * gamma + beta
        B, NQ, _ = Q.shape
        NK = K.shape[1]
        H = NUM_HEADS
        dh = DIM_V // H
        q = Q @ Wq.T + bq
        k = K @ Wk.T + bk
        v = K @ Wv.T + bv
        qh = q.reshape(B, NQ, H, dh)
        kh = k.reshape(B, NK, H, dh)
        vh = v.reshape(B, NK, H, dh)
        scores = jnp.einsum('bqhd,bkhd->bhqk', qh, kh) / np.sqrt(DIM_V).astype(np.float32)
        A = jax.nn.softmax(scores, axis=-1)
        oh = qh + jnp.einsum('bhqk,bkhd->bqhd', A, vh)
        O = oh.reshape(B, NQ, DIM_V)
        O = _layernorm(O, g0, b0)
        O = O + jax.nn.relu(O @ Wo.T + bo)
        O = _layernorm(O, g1, b1)
        return O

    def _L0_ffn_ref(x, wqkv, q_scale, k_scale, wo, ln_g, ln_b, w1, b1, w2, b2):
        import jax, jax.numpy as jnp
        import numpy as np
        DIM = 128
        DEPTH = 2
        HEADS = 8
        DIM_HEAD = 64
        WINDOW = 64
        INNER = HEADS * DIM_HEAD
        HID = int(DIM * 4 * 2 / 3)
        B, N = (2, 1024)
        QK_SCALE = 8.0

        def shift_token(t):
            t1, t2 = jnp.split(t, 2, axis=-1)
            t2 = jnp.pad(t2, ((0, 0), (1, 0), (0, 0)))[:, :-1]
            return jnp.concatenate([t1, t2], axis=-1)

        def l2norm(t):
            return t / jnp.clip(jnp.linalg.norm(t, axis=-1, keepdims=True), 1e-12)

        def rotate_half(x):
            x1, x2 = jnp.split(x, 2, axis=-1)
            return jnp.concatenate([-x2, x1], axis=-1)

        def rotary_xpos(q, k):
            n = q.shape[-2]
            half_idx = jnp.arange(0, DIM_HEAD, 2, dtype=jnp.float32)
            inv_freq = 1.0 / 10000.0 ** (half_idx / DIM_HEAD)
            t = jnp.arange(n, dtype=jnp.float32)
            freqs = t[:, None] * inv_freq[None, :]
            freqs = jnp.concatenate([freqs, freqs], axis=-1)
            base = (half_idx + 0.4 * DIM_HEAD) / (1.4 * DIM_HEAD)
            power = (t - n // 2) / float(WINDOW // 2)
            scale = base[None, :] ** power[:, None]
            scale = jnp.concatenate([scale, scale], axis=-1)
            cos, sin = (jnp.cos(freqs), jnp.sin(freqs))
            q = q * cos * scale + rotate_half(q) * sin * scale
            k = k * cos / scale + rotate_half(k) * sin / scale
            return (q, k)

        def local_attention(q, k, v):
            b, h, n, d = q.shape
            w = n // WINDOW
            bq = q.reshape(b, h, w, WINDOW, d) * QK_SCALE
            bk = k.reshape(b, h, w, WINDOW, d)
            bv = v.reshape(b, h, w, WINDOW, d)

            def look_around(t):
                p = jnp.pad(t, ((0, 0), (0, 0), (1, 0), (0, 0), (0, 0)))
                return jnp.concatenate([p[:, :, :w], p[:, :, 1:]], axis=3)
            bk, bv = (look_around(bk), look_around(bv))
            bt = jnp.arange(n).reshape(w, WINDOW)
            btp = jnp.pad(bt, ((1, 0), (0, 0)), constant_values=-1)
            btk = jnp.concatenate([btp[:w], btp[1:]], axis=1)
            sim = jnp.einsum('bhwid,bhwjd->bhwij', bq, bk)
            i = bt[:, :, None]
            j = btk[:, None, :]
            mask = (i < j) | (i > j + WINDOW) | (j == -1)
            sim = jnp.where(mask, -jnp.finfo(sim.dtype).max, sim)
            attn = jax.nn.softmax(sim, axis=-1)
            out = jnp.einsum('bhwij,bhwjd->bhwid', attn, bv)
            return out.reshape(b, h, n, d)

        def _layer(x, wqkv, qs, ksc, wo, lg, lb, w1, b1, w2, b2):
            b, n, _ = x.shape
            h = shift_token(x)
            qkv = h @ wqkv
            q, k, v = jnp.split(qkv, 3, axis=-1)
            to_heads = lambda t: t.reshape(b, n, HEADS, DIM_HEAD).transpose(0, 2, 1, 3)
            q, k, v = (to_heads(q), to_heads(k), to_heads(v))
            q = l2norm(q) * qs
            k = l2norm(k) * ksc
            q, k = rotary_xpos(q, k)
            o = local_attention(q, k, v)
            o = o.transpose(0, 2, 1, 3).reshape(b, n, INNER)
            x = x + o @ wo
            h = shift_token(x)
            mu = h.mean(-1, keepdims=True)
            var = h.var(-1, keepdims=True)
            h = (h - mu) / jnp.sqrt(var + 1e-05) * lg + lb
            h = h @ w1 + b1
            a, g = jnp.split(h, 2, axis=-1)
            h = a * jax.nn.gelu(g, approximate=False)
            x = x + h @ w2 + b2
            return x
        for l in range(DEPTH):
            x = _layer(x, wqkv[l], q_scale[l], k_scale[l], wo[l], ln_g[l], ln_b[l], w1[l], b1[l], w2[l], b2[l])
        return x

    def _L1_xattn_ref(query, key_, value, attention_mask, Wq, bq, Wk, bk, Wv, bv, Wo, bo):
        import jax, jax.numpy as jnp
        import numpy as np
        H = 128
        NH = 16
        HD = H // NH
        B, S = (4, 256)

        def _split_heads(x):
            b, s, _ = x.shape
            return x.reshape(b, s, NH, HD).transpose(0, 2, 1, 3)
        q = _split_heads(query @ Wq.T + bq)
        k = _split_heads(key_ @ Wk.T + bk)
        v = _split_heads(value @ Wv.T + bv)
        scores = jnp.einsum('bhqd,bhkd->bhqk', q, k) / jnp.sqrt(jnp.float32(HD))
        mask = (1.0 - attention_mask) * -10000.0
        scores = scores + mask[:, None, None, :]
        probs = jax.nn.softmax(scores, axis=-1)
        ctx = jnp.einsum('bhqk,bhkd->bhqd', probs, v)
        ctx = ctx.transpose(0, 2, 1, 3).reshape(query.shape[0], query.shape[1], H)
        return ctx @ Wo.T + bo

    def _L1_ffn_ref(x, sg, su, sd, rg, ru, rd, wr, rb):
        import jax, jax.numpy as jnp
        import numpy as np
        H, I, E_ROUTED, TOP_K = (128, 352, 7, 2)
        B, S = (4, 256)

        def _expert(h, g, u, d):
            return jnp.einsum('...i,hi->...h', jax.nn.silu(h @ g.T) * (h @ u.T), d)
        shared_out = _expert(x, sg, su, sd)
        logits = x @ wr.T + rb
        probs = jax.nn.softmax(logits, axis=-1)
        scores, idx = jax.lax.top_k(probs, TOP_K)
        scores = scores / scores.sum(axis=-1, keepdims=True)
        w = jnp.sum(scores[..., None] * jax.nn.one_hot(idx, E_ROUTED, dtype=x.dtype), axis=-2)
        out = shared_out
        for e in range(E_ROUTED):
            out = out + w[..., e:e + 1] * _expert(x, rg[e], ru[e], rd[e])
        return out

    def _L2_xattn_ref(query_seq, value_seq, router_w, q_w, kv_w, out_w):
        import jax, jax.numpy as jnp
        import numpy as np
        NUM_HEADS = 16
        CAPACITY = 64
        ROPE_BASE = 10000.0

        def _rope_factor(positions, dim):
            freqs = jnp.exp(jnp.linspace(0.0, -1.0, dim // 2) * jnp.log(jnp.float32(ROPE_BASE)))
            angles = positions[..., None] * freqs
            return jnp.concatenate([jnp.sin(angles), jnp.cos(angles)], axis=-1)
        B, Sq, D = query_seq.shape
        Skv = value_seq.shape[1]
        H, C = (NUM_HEADS, CAPACITY)
        d = D // H
        rw = jnp.einsum('bsd,od->bs', query_seq, router_w).astype(jnp.float32)
        top_w, top_idx = jax.lax.top_k(rw, C)
        resampled = jnp.take_along_axis(query_seq, top_idx[:, :, None], axis=1)
        q = jnp.einsum('bcd,ed->bce', resampled, q_w)
        kv = jnp.einsum('bsd,ed->bse', value_seq, kv_w)
        k, v = jnp.split(kv, 2, axis=-1)
        q = q.reshape(B, C, H, d).transpose(0, 2, 1, 3)
        k = k.reshape(B, Skv, H, d).transpose(0, 2, 1, 3)
        v = v.reshape(B, Skv, H, d).transpose(0, 2, 1, 3)
        q_pos = top_idx.astype(jnp.float32)[:, None, :]
        q = q * _rope_factor(q_pos, d)
        k_pos = jnp.arange(Skv, dtype=jnp.float32)[None, :]
        k = k * _rope_factor(k_pos, d)[None]
        scores = jnp.einsum('bhcd,bhsd->bhcs', q, k) / jnp.sqrt(jnp.float32(d))
        att = jnp.einsum('bhcs,bhsd->bhcd', jax.nn.softmax(scores, axis=-1), v)
        att = att.transpose(0, 2, 1, 3).reshape(B, C, H * d)
        att = jnp.einsum('bce,de->bcd', att, out_w)
        src = att * top_w[:, :, None]
        out = jnp.zeros_like(query_seq).at[jnp.arange(B)[:, None], top_idx].set(src)
        return out

    def _L2_ffn_ref(x, Wr, Wg, Wu, Wd, Sg, Su, Sd):
        import jax, jax.numpy as jnp
        import numpy as np
        TOP_K = 2
        EPS = 1e-20
        B, S, H = x.shape
        T = B * S
        xt = x.reshape(T, H)
        scores = jax.nn.softmax(xt @ Wr, axis=-1)
        topk_w, topk_idx = jax.lax.top_k(scores, TOP_K)
        topk_w = topk_w / (topk_w.sum(axis=-1, keepdims=True) + EPS)
        g = jax.nn.silu(jnp.einsum('th,ehd->etd', xt, Wg))
        u = jnp.einsum('th,ehd->etd', xt, Wu)
        out_all = jnp.einsum('etd,edh->eth', g * u, Wd)
        tok = jnp.arange(T)[:, None]
        gathered = out_all[topk_idx, tok, :]
        out = jnp.sum(gathered * topk_w[..., None], axis=1).reshape(B, S, H)
        shared = jax.nn.silu(x @ Sg) * (x @ Su) @ Sd
        return out + shared

    def _L3_xattn_ref(q_in, k_in, v_in, key_mask, Wq, bq, Wk, bk, Wv, bv, Wo, bo):
        import jax, jax.numpy as jnp
        import numpy as np
        HEADS, QSIZE, KSIZE = (16, 64, 64)
        B, M, _ = q_in.shape
        N = k_in.shape[1]
        qw = (q_in @ Wq + bq).reshape(B, M, HEADS, QSIZE)
        kw = (k_in @ Wk + bk).reshape(B, N, HEADS, QSIZE)
        vw = (v_in @ Wv + bv).reshape(B, N, HEADS, KSIZE)
        a = jnp.einsum('bmhd,bnhd->bhmn', qw, kw) / jnp.sqrt(jnp.float32(QSIZE))
        a = jnp.where(key_mask[:, None, None, :], a, -jnp.inf)
        a = jax.nn.softmax(a, axis=-1)
        o = jnp.einsum('bhmn,bnhd->bmhd', a, vw).reshape(B, M, HEADS * KSIZE)
        return o @ Wo + bo

    def _L3_ffn_ref(x, ln1_w, ln1_b, ln2_w, ln2_b, conv_w, attn_w, proj_w, router_w, expert_wv, expert_proj):
        import jax, jax.numpy as jnp
        import numpy as np
        EPS = 1e-05

        def _layernorm(x, w, b):
            mu = jnp.mean(x, axis=-1, keepdims=True)
            var = jnp.mean((x - mu) ** 2, axis=-1, keepdims=True)
            return (x - mu) * jax.lax.rsqrt(var + EPS) * w + b

        def _rope_tables(T, D, base=10000.0):
            inv_freq = 1.0 / base ** (jnp.arange(0, D, 2, dtype=jnp.float32) / D)
            t = jnp.arange(T, dtype=jnp.float32)
            freqs = jnp.einsum('i,j->ij', t, inv_freq)
            emb = jnp.concatenate([freqs, freqs], axis=-1)
            return (jnp.cos(emb), jnp.sin(emb))

        def _rotate_half(x):
            x1, x2 = (x[..., :x.shape[-1] // 2], x[..., x.shape[-1] // 2:])
            return jnp.concatenate([-x2, x1], axis=-1)

        def _attn(x, ln_w, ln_b, conv_w, attn_w, proj_w, n_head):
            B, T, C = x.shape
            D = C // n_head
            h = _layernorm(x, ln_w, ln_b)
            hc = jnp.transpose(h, (0, 2, 1))
            hc = jnp.pad(hc, ((0, 0), (0, 0), (2, 0)))
            hc = jax.lax.conv_general_dilated(hc, conv_w, window_strides=(1,), padding='VALID', dimension_numbers=('NCH', 'OIH', 'NCH'), feature_group_count=C)
            h = jnp.transpose(hc, (0, 2, 1))
            qkv = h @ attn_w
            q, k, v = jnp.split(qkv, 3, axis=-1)
            q = q.reshape(B, T, n_head, D)
            k = k.reshape(B, T, n_head, D)
            v = v.reshape(B, T, n_head, D)
            cos, sin = _rope_tables(T, D)
            cos = cos[None, :, None, :]
            sin = sin[None, :, None, :]
            q = q * cos + _rotate_half(q) * sin
            k = k * cos + _rotate_half(k) * sin
            scores = jnp.einsum('bqhd,bkhd->bhqk', q, k) / jnp.sqrt(jnp.float32(D))
            causal = jnp.tril(jnp.ones((T, T), dtype=bool))
            scores = jnp.where(causal, scores, jnp.float32(-1e+30))
            p = jax.nn.softmax(scores, axis=-1)
            y = jnp.einsum('bhqk,bkhd->bqhd', p, v).reshape(B, T, C)
            return y @ proj_w

        def _moe(x, ln_w, ln_b, router_w, expert_wv, expert_proj):
            h = _layernorm(x, ln_w, ln_b)
            logits = h @ router_w
            expert_idx = jnp.argmax(logits, axis=-1)
            E = router_w.shape[-1]
            out = jnp.zeros_like(x)
            for e in range(E):
                gv = h @ expert_wv[e]
                gate_raw, value = jnp.split(gv, 2, axis=-1)
                y = gate_raw * jax.nn.sigmoid(gate_raw) * value @ expert_proj[e]
                out = out + jnp.where((expert_idx == e)[..., None], y, 0.0)
            return out
        n_head = 16
        x = x + _attn(x, ln1_w, ln1_b, conv_w, attn_w, proj_w, n_head)
        x = x + _moe(x, ln2_w, ln2_b, router_w, expert_wv, expert_proj)
        return x
    x = x + _L0_xattn_ref(_layernorm(x, axis=-1), ctx_1024, L0_xattn_Wq, L0_xattn_bq, L0_xattn_Wk, L0_xattn_bk, L0_xattn_Wv, L0_xattn_bv, L0_xattn_Wo, L0_xattn_bo, L0_xattn_g0, L0_xattn_b0, L0_xattn_g1, L0_xattn_b1)
    x = x + _L0_ffn_ref(_layernorm(x, axis=-1), L0_ffn_wqkv, L0_ffn_q_scale, L0_ffn_k_scale, L0_ffn_wo, L0_ffn_ln_g, L0_ffn_ln_b, L0_ffn_w1, L0_ffn_b1, L0_ffn_w2, L0_ffn_b2)
    x = x + _L1_xattn_ref(_layernorm(x, axis=-1), ctx_1024, ctx_1024, mask_BxS2_ff1, L1_xattn_Wq, L1_xattn_bq, L1_xattn_Wk, L1_xattn_bk, L1_xattn_Wv, L1_xattn_bv, L1_xattn_Wo, L1_xattn_bo)
    x = x + _L1_ffn_ref(_layernorm(x, axis=-1), L1_ffn_sg, L1_ffn_su, L1_ffn_sd, L1_ffn_rg, L1_ffn_ru, L1_ffn_rd, L1_ffn_wr, L1_ffn_rb)
    x = x + _L2_xattn_ref(_layernorm(x, axis=-1), ctx_1024, L2_xattn_router_w, L2_xattn_q_w, L2_xattn_kv_w, L2_xattn_out_w)
    x = x + _L2_ffn_ref(_layernorm(x, axis=-1), L2_ffn_Wr, L2_ffn_Wg, L2_ffn_Wu, L2_ffn_Wd, L2_ffn_Sg, L2_ffn_Su, L2_ffn_Sd)
    x = x + _L3_xattn_ref(_layernorm(x, axis=-1), ctx_1024, ctx_1024, mask_BxS2_bf1, L3_xattn_Wq, L3_xattn_bq, L3_xattn_Wk, L3_xattn_bk, L3_xattn_Wv, L3_xattn_bv, L3_xattn_Wo, L3_xattn_bo)
    x = x + _L3_ffn_ref(_layernorm(x, axis=-1), L3_ffn_ln1_w, L3_ffn_ln1_b, L3_ffn_ln2_w, L3_ffn_ln2_b, L3_ffn_conv_w, L3_ffn_attn_w, L3_ffn_proj_w, L3_ffn_router_w, L3_ffn_expert_wv, L3_ffn_expert_proj)
    return x

_drawn_inputs = setup_inputs


def setup_inputs(seed=0):
    import zlib

    import numpy as np

    out = dict(_drawn_inputs(seed))
    spreads = {'L0_xattn_g0': (1.0, 0.2),
     'L0_xattn_b0': (0.0, 0.1),
     'L0_xattn_g1': (1.0, 0.2),
     'L0_xattn_b1': (0.0, 0.1),
     'L0_ffn_q_scale': (1.0, 0.6),
     'L0_ffn_k_scale': (1.0, 0.6),
     'L0_ffn_ln_g': (1.0, 0.6),
     'L0_ffn_ln_b': (0.0, 0.8),
     'L0_ffn_b1': (0.0, 0.8),
     'L0_ffn_b2': (0.0, 0.1),
     'L1_xattn_bq': (0.0, 0.8),
     'L1_xattn_bk': (0.0, 0.8),
     'L1_xattn_bv': (0.0, 0.291),
     'L1_xattn_bo': (0.0, 0.1),
     'L1_ffn_rb': (0.0, 0.8),
     'L3_xattn_bq': (0.0, 0.375),
     'L3_xattn_bk': (0.0, 0.8),
     'L3_xattn_bv': (0.0, 0.1),
     'L3_xattn_bo': (0.0, 0.1),
     'L3_ffn_ln1_w': (1.0, 0.6),
     'L3_ffn_ln1_b': (0.0, 0.8),
     'L3_ffn_ln2_w': (1.0, 0.6),
     'L3_ffn_ln2_b': (0.0, 0.8)}
    factors = {'L0_xattn_Wk': 4.695,
     'L0_xattn_bk': 8.0,
     'L0_xattn_bo': 2.698,
     'L0_ffn_wqkv': 2.728,
     'L0_ffn_wo': 2.779,
     'L0_ffn_w1': 8.0,
     'L0_ffn_w2': 8.0,
     'L1_ffn_sg': 8.0,
     'L1_ffn_su': 8.0,
     'L1_ffn_sd': 8.0,
     'L1_ffn_rg': 8.0,
     'L1_ffn_ru': 8.0,
     'L1_ffn_rd': 8.0,
     'L1_ffn_wr': 8.0,
     'L2_xattn_router_w': 8.0,
     'L2_xattn_q_w': 8.0,
     'L2_xattn_kv_w': 8.0,
     'L2_xattn_out_w': 8.0,
     'L2_ffn_Wr': 8.0,
     'L2_ffn_Wg': 8.0,
     'L2_ffn_Wu': 8.0,
     'L2_ffn_Wd': 8.0,
     'L2_ffn_Sg': 8.0,
     'L2_ffn_Su': 8.0,
     'L2_ffn_Sd': 8.0,
     'L3_ffn_conv_w': 8.0,
     'L3_ffn_attn_w': 8.0,
     'L3_ffn_proj_w': 8.0,
     'L3_ffn_router_w': 8.0,
     'L3_ffn_expert_wv': 8.0,
     'L3_ffn_expert_proj': 8.0}
    for name, (base, spread) in spreads.items():
        noise = np.random.default_rng([zlib.crc32(name.encode()), seed]).standard_normal(out[name].shape)
        drawn = base * np.exp(spread * noise) if base else spread * noise
        out[name] = jnp.asarray(drawn.astype(out[name].dtype))
    for name, factor in factors.items():
        out[name] = (out[name] * factor).astype(out[name].dtype)
    return out
```

```python
from contextlib import ExitStack

import concourse.bass as bass
from concourse import mybir

ds = bass.ds
F32 = mybir.dt.float32
BF16 = mybir.dt.bfloat16
U8 = mybir.dt.uint8
ALU = mybir.AluOpType
ACT = mybir.ActivationFunctionType
AX_X = mybir.AxisListType.X

P = 128
B = 8
S = 256
SK = 512
C = 128
TOK = B * S
TILES = TOK // P
QT = S // P
KT = SK // P
GROUP = 512
GROUPS = TOK // GROUP
GT = GROUP // P

L0_HEADS, L0F_HEADS, L1_HEADS, L2_HEADS, L3_HEADS, L3F_HEADS = 8, 8, 16, 16, 16, 16
WIDE = 64
L0F_HID = 341
L1F_EXPERTS, L1F_HID = 7, 352
L2F_EXPERTS, L2F_HID = 8, 256
L3F_EXPERTS, L3F_HID = 4, 512
L2_CAP = 64
CHUNKS_L3 = L3_HEADS * WIDE // P
CHUNKS_L0F = L0F_HEADS * WIDE // P


def pieces(n):
    return [(a, min(P, n - a)) for a in range(0, n, P)]


XW = {
    "L0x": [("wq", C), ("wk", C), ("wv", C), ("wo", C), ("bq", 1), ("bk", 1), ("bq_row", C), ("bv_row", C),
            ("bo_row", C), ("g0_row", C), ("b0_row", C), ("g1_row", C), ("b1_row", C)],
    "L1x": [("wq", C), ("wk", C), ("wv", C), ("wo", C), ("bq", 1), ("bk", 1), ("bv_row", C), ("bo_row", C)],
    "L2x": [("wq", C), ("wk", C), ("wv", C), ("wo", C), ("router_row", C)],
    "L3x": [("wq", CHUNKS_L3 * C), ("wk", CHUNKS_L3 * C), ("wv", CHUNKS_L3 * C), ("wo", CHUNKS_L3 * C),
            ("bq", CHUNKS_L3), ("bk", CHUNKS_L3), ("bv_row", CHUNKS_L3 * C), ("bo_row", C)],
}
FW = {
    "L0f": [(n + str(d), c) for d in (0, 1) for n, c in (
        ("wqkv", 3 * CHUNKS_L0F * C), ("wo", CHUNKS_L0F * C), ("w1", 2 * L0F_HID), ("w2", 3 * C), ("qs_row", WIDE),
        ("ks_row", WIDE), ("g", 1), ("b", 1), ("b1", 6), ("b2_row", C))],
    "L1f": [("gate", 8 * L1F_HID), ("up", 8 * L1F_HID), ("down", 8 * 3 * C), ("router", L1F_EXPERTS),
            ("rb_row", L1F_EXPERTS)],
    "L2f": [("gate", 9 * L2F_HID), ("up", 9 * L2F_HID), ("down", 9 * 2 * C), ("router", L2F_EXPERTS)],
    "L3f": [("wv2", L3F_EXPERTS * 2 * L3F_HID), ("down", L3F_EXPERTS * 4 * C), ("wq", C), ("wqr", C), ("wk", C),
            ("wkr", C), ("wv", C), ("wo", C), ("conv", 3), ("g1_row", C), ("b1_row", C), ("g2_row", C),
            ("b2_row", C), ("router", L3F_EXPERTS)],
}
CW = [("ident", P), ("scale_L0x", L0_HEADS), ("scale_8", L1_HEADS), ("scale_L3x", L3_HEADS), ("scale_L0f", L0F_HEADS),
      ("before", 64), ("causal", QT * S), ("band", QT * S), ("l2_ropeq", QT * C), ("l2_ropek", SK),
      ("l3f_cos", S), ("l3f_sin", S), ("xq_cos", QT * WIDE), ("xq_sin", QT * WIDE), ("xk_cos", QT * WIDE),
      ("xk_sin", QT * WIDE), ("slot", L2_CAP), ("earlier", QT * S)]


def width(table):
    return sum(n for _, n in table)


def views(tile, table):
    out, at = {}, 0
    for name, n in table:
        out[name] = tile[:, at:at + n]
        at += n
    return out


def row(ap, *counts):
    for at, n in enumerate(counts):
        ap = ap.unsqueeze(1)
    return ap.broadcast_to([P, *counts, ap.shape[-1]])


def each(ap, n):
    return ap.unsqueeze(len(ap.shape)).broadcast_to([*ap.shape, n])


class Steps:

    def __init__(self, eng, sem, base=0):
        self.eng, self.sem, self.base, self.n = eng, sem, base, 0

    def done(self, ins):
        ins.then_inc(self.sem, 1)
        self.n += 1
        self.eng.wait_ge(self.sem, self.base + self.n)


class Memory:

    def __init__(self, nc, ctx):
        def sb(name, shape, dt=F32):
            return ctx.enter_context(nc.sbuf_tensor(name, shape, dt))

        def ps(name, shape):
            return ctx.enter_context(nc.psum_tensor(name, shape, F32))

        self.x = sb("x", [P, TILES, C])
        self.xn = sb("xn", [P, TILES, C])
        self.h = sb("h", [P, TILES, C])
        self.o = sb("o", [P, TILES, C])
        self.hT = sb("hT", [P, TOK])
        self.ctxT = sb("ctxT", [P, B * SK])
        self.const = sb("const", [P, width(CW)])
        self.k = views(self.const, CW)
        self.xw = sb("xw", [P, max(width(t) for t in XW.values())])
        self.fw = sb("fw", [P, max(width(t) for t in FW.values())])
        self.sum = sb("row_sum", [P, TILES])
        self.mean = sb("row_mean", [P, TILES])
        self.var = sb("row_var", [P, TILES])
        self.std = sb("row_std", [P, TILES])
        self.rstd = sb("row_rstd", [P, TILES])
        self.qT = sb("qT", [P, CHUNKS_L3, S])
        self.kT = sb("kT", [P, CHUNKS_L3, SK])
        self.v = sb("v", [P, KT, L3_HEADS * WIDE])
        self.ctx_now = sb("ctx_now", [P, SK])
        self.x_now = sb("x_now", [P, S])
        self.q_head = sb("q_head", [P, 2, S])
        self.prob = sb("prob", [P, 2, 2 * SK])
        self.probT = sb("probT", [P, 2, KT, S])
        self.top = sb("top", [P, 2, 2])
        self.total = sb("total", [P, 16, 2])
        self.inverse = sb("inverse", [P, 16, 2])
        self.sel = sb("sel", [P, TILES, L2_CAP])
        self.ones = sb("ones", [P, P])
        self.o_now = sb("o_now", [P, C])
        self.scores16 = sb("scores16", [P, TILES, 8])
        self.weight = sb("weight", [P, TILES, 8])
        self.rank = sb("rank", [P, TILES, 8])
        self.norm = sb("norm", [P, 4, L0F_HEADS])
        self.inv_norm = sb("inv_norm", [P, 4, L0F_HEADS])
        self.turn_cos = sb("turn_cos", [P, 4, WIDE])
        self.turn_sin = sb("turn_sin", [P, 4, WIDE])
        self.own = sb("own", [P, TILES])
        self.route = sb("route", [P, TILES])
        self.mask_in = sb("mask_in", [P, B * SK // P])
        self.mask_u8 = sb("mask_u8", [P, B * SK // P], U8)
        self.mask_part = sb("mask_part", [P, 3, B * SK // P], BF16)
        self.mask_rest = sb("mask_rest", [P, 3, B * SK // P])
        self.identb = sb("identb", [P, P], BF16)
        self.onesb = sb("onesb", [P, P], BF16)
        self.bandb = sb("bandb", [P, QT, S], BF16)
        self.key_mask = sb("key_mask", [P, B * SK], BF16)
        self.pS = ps("pS", [P, 2, 1024])
        self.pT = ps("pT", [P, 2, 512])
        self.pO = ps("pO", [P, 2, 2, P])
        self.pG = ps("pG", [P, 512])
        self.banks = self.pS[:, :, :].rearrange("p a (b n) -> p (a b) n", b=2)


class Phase:

    def __init__(self, nc, name):
        self.nc, self.name, self.sems = nc, name, []
        self.stack = ExitStack()

    def sem(self, name):
        s = self.nc.alloc_semaphore(f"{self.name}_{name}")
        self.sems.append(s)
        return s

    def __enter__(self):
        self.block = self.stack.enter_context(self.nc.Block(f"{self.name}_block"))
        return self

    def __exit__(self, *e):
        self.stack.close()
        if e[0] is None:
            self.nc.clear_and_free_semaphores(self.sems)
            self.nc.all_engine_barrier()


def wide(ap):
    return ap[:, :, :].rearrange("p t c -> p (t c)")


def normalize_act(act, m, centred, squared, varied, rooted, n, dst):
    act.wait_ge(centred, n)
    act.activation(wide(m.h), wide(dst), ACT.Square).then_inc(squared, 1)
    act.wait_ge(varied, n)
    act.activation(m.std[:, :], m.var[:, :], ACT.Sqrt).then_inc(rooted, 1)


def normalize_dve(dve, m, steps, centred, squared, varied, n, src, dst, eps, scale=None, shift=None):
    nc = dve
    steps.done(nc.tensor_reduce(m.sum[:, :], src, AX_X, ALU.add))
    steps.done(nc.tensor_scalar(m.mean[:, :], m.sum[:, :], 1.0 / C, None, ALU.mult))
    nc.tensor_tensor(dst, src, each(m.mean[:, :], C), ALU.subtract).then_inc(centred, 1)
    dve.wait_ge(squared, n)
    steps.done(nc.tensor_reduce(m.var[:, :], m.h[:, :, :], AX_X, ALU.add))
    nc.tensor_scalar(m.var[:, :], m.var[:, :], 1.0 / C, eps, ALU.mult, ALU.add).then_inc(varied[0], 1)
    dve.wait_ge(varied[1], n)
    steps.done(nc.reciprocal(m.rstd[:, :], m.std[:, :]))
    steps.done(nc.tensor_tensor(dst, dst, each(m.rstd[:, :], C), ALU.mult))
    if scale is not None:
        steps.done(nc.tensor_tensor(dst, dst, row(scale, TILES), ALU.mult))
        steps.done(nc.tensor_tensor(dst, dst, row(shift, TILES), ALU.add))


def turn_pe(pe, m, src, turned, rows=P):
    for g in range(4):
        for t in range(4):
            last = pe.transpose(m.banks[0:rows, g, t * P:(t + 1) * P], src[:, 4 * g + t, :], m.k["ident"])
        last.then_inc(turned, 1)


def turn_out_act(act, m, dst, turned, copied, rows=P):
    for g in (0, 2):
        act.wait_ge(turned, g + 1)
        act.activation(dst[0:rows, g * 512:(g + 1) * 512], m.banks[0:rows, g, :], ACT.Copy).then_inc(copied, 1)


def turn_out_dve(dve, m, dst, turned, copied, rows=P):
    for g in (1, 3):
        dve.wait_ge(turned, g + 1)
        dve.tensor_copy(dst[0:rows, g * 512:(g + 1) * 512], m.banks[0:rows, g, :]).then_inc(copied, 1)


def load_phase(nc, m, x, ctxT, masks, wx, wf, const):
    mask_f, mask_b = masks
    with Phase(nc, "load") as ph:
        loaded = ph.sem("loaded")
        steps_dve = ph.sem("steps")

        @ph.block.sync
        def _(sp):
            sp.dma_start(m.x[:, :, :], x.rearrange("(t p) c -> p t c", p=P)).then_inc(loaded, 16)
            sp.dma_start(m.const[:, :], const).then_inc(loaded, 16)
            sp.dma_start(m.xw[:, 0:width(XW["L0x"])], wx["L0x"]).then_inc(loaded, 16)
            sp.dma_start(m.ctxT[:, :], ctxT).then_inc(loaded, 16)
            sp.wait_ge(loaded, 64)

        @ph.block.vector
        def _(dve):
            steps = Steps(dve, steps_dve)
            dve.memset(m.onesb[:, :], 1.0)
            dve.memset(m.ones[:, :], 1.0)
            dve.memset(m.key_mask[:, :], 0.0)
            dve.wait_ge(loaded, 64)
            steps.done(dve.tensor_copy(m.identb[:, :], m.k["ident"]))


def fetch_sync(ph, fetch):
    if fetch is None:
        return
    fetched = ph.sem("fetched")

    @ph.block.sync
    def _(sp):
        sp.dma_start(*fetch).then_inc(fetched, 16)
        sp.wait_ge(fetched, 16)


def prepare(nc, m, name):
    with Phase(nc, name + "_prepare") as ph:
        steps, centred, squared, varied, rooted, turned, copied = (ph.sem(n) for n in (
            "steps", "centred", "squared", "varied", "rooted", "turned", "copied"))

        @ph.block.vector
        def _(dve):
            st = Steps(dve, steps)
            normalize_dve(dve, m, st, centred, squared, (varied, rooted), 1, m.x[:, :, :], m.xn[:, :, :], 1e-5)
            turn_out_dve(dve, m, m.hT, turned, copied)

        @ph.block.scalar
        def _(act):
            normalize_act(act, m, centred, squared, varied, rooted, 1, m.xn)
            turn_out_act(act, m, m.hT, turned, copied)

        @ph.block.tensor
        def _(pe):
            pe.wait_ge(steps, 5)
            turn_pe(pe, m, m.xn, turned)


class Attention:

    def __init__(self, ph, heads, width_, keys, scale, q_rows=P, tiles=QT, mask=None):
        self.H, self.dh, self.NK, self.KC, self.scale = heads, width_, keys, keys // P, scale
        self.rows, self.T, self.mask = q_rows, tiles, mask
        self.paired = width_ == WIDE
        self.head_ready = ph.sem("head_ready")
        self.scored = ph.sem("scored")
        self.topped = ph.sem("topped")
        self.exped = ph.sem("exped")
        self.turned = ph.sem("turned")
        self.low_copied = ph.sem("low_copied")
        self.high_copied = ph.sem("high_copied")
        self.weighed = ph.sem("weighed")
        self.inverted = ph.sem("inverted")
        self.normed = ph.sem("normed")

    def count(self, b, n):
        return b * self.H + (1 + max(n, 0) if isinstance(n, int) else n + 1)

    def slots(self, eng, slot):
        for i in range(4):
            slot(i, i % 2, i // 2)
        with eng.Fori(2, self.H // 2) as j:
            for s in (0, 1):
                slot(2 * j + s, s, j)
        for i in (self.H, self.H + 1):
            slot(i, i % 2, i // 2)

    def has(self, i, back):
        return not isinstance(i, int) or 0 <= i - back < self.H


def opened(eng, *sems):
    for s in sems:
        eng.sem_inc(s, 1)


def attention_pool(pool, m, a, b):
    nq = a.T * a.rows

    def slot(i, s, j):
        if a.has(i, 0):
            pool.wait_ge(a.scored, a.count(b, i - 1))
            scale = a.scale[:, ds(i, 1)]
            q = m.qT[:, ds(j, 1), 0:nq] if a.paired else m.qT[:, 0:1, 0:nq]
            pool.tensor_tensor(m.q_head[:, s:s + 1, 0:nq], q, each(scale, nq), ALU.mult).then_inc(a.head_ready, 1)

    a.slots(pool, slot)


def attention_pe(pe, m, a, b):
    nq, rows = a.T * a.rows, a.rows

    def scores(i, s, j):
        pe.wait_ge(a.head_ready, a.count(b, i + 1))
        pe.wait_ge(a.exped, a.count(b, i - 1))
        k = m.kT[:, ds(j, 1), 0:a.NK] if a.paired else m.kT[:, 0:1, 0:a.NK]
        for t in range(a.T):
            out = m.pS[0:rows, s:s + 1, t * a.NK:(t + 1) * a.NK]
            if a.mask == "keys":
                pe.matmul(out, m.onesb[:, 0:rows], m.key_mask[:, ds(b * SK, SK)], start=True, stop=False)
            if a.mask == "tiles":
                pe.matmul(out, m.identb[:, :], m.bandb[:, t, :], start=True, stop=False)
            last = pe.matmul(out, m.q_head[:, s, t * P:t * P + rows], k, start=a.mask is None, stop=True)
        last.then_inc(a.scored, 1)

    def weigh(i, s):
        pe.wait_ge(a.low_copied, a.count(b, i - 1))
        pe.wait_ge(a.high_copied, a.count(b, i - 1))
        pe.wait_ge(a.normed, a.count(b, i - 3))
        for t in range(a.T):
            for c in range(a.KC):
                last = pe.matmul(m.pO[0:rows, s, t, 0:a.dh], m.probT[:, s, c, t * P:t * P + rows],
                                 m.v[:, c, ds((i - 2) * a.dh, a.dh)], start=c == 0, stop=c == a.KC - 1)
        last.then_inc(a.weighed, 1)

    def turn(i, s):
        pe.wait_ge(a.exped, a.count(b, i))
        pe.wait_ge(a.low_copied, a.count(b, i - 1))
        pe.wait_ge(a.high_copied, a.count(b, i - 1))
        half = a.KC // 2
        for c in range(a.KC):
            for t in range(a.T):
                at = (c % half) * a.T * P + t * P
                last = pe.transpose(m.pT[:, c // half, at:at + P],
                                    m.prob[:, s, t * a.NK + c * P:t * a.NK + (c + 1) * P], m.k["ident"])
        last.then_inc(a.turned, 1)

    def slot(i, s, j):
        if a.has(i, 0):
            scores(i, s, j)
        if a.has(i, 2):
            weigh(i, s)
        if a.has(i, 1):
            turn(i, 1 - s)

    a.slots(pe, slot)


def turned_half(m, a, s, half):
    nq, n = a.T * a.rows, a.KC // 2
    return (m.probT[:, s, half * n:(half + 1) * n, 0:nq],
            m.pT[:, half, 0:n * a.T * P].rearrange("p (c q) -> p c q", q=a.T * P)[:, :, 0:nq])


def attention_act(act, m, a, b):
    def slot(i, s, j):
        if a.has(i, 0):
            act.wait_ge(a.topped, a.count(b, i + 1))
            act.wait_ge(a.turned, a.count(b, i - 1))
            for t in range(a.T):
                last = act.activation(m.prob[0:a.rows, s, t * a.NK:(t + 1) * a.NK],
                                      m.pS[0:a.rows, s, t * a.NK:(t + 1) * a.NK], ACT.Exp,
                                      bias=m.top[0:a.rows, s, t:t + 1],
                                      accum_out=m.total[0:a.rows, ds(i, 1), t:t + 1])
            last.then_inc(a.exped, 1)
        if a.has(i, 1):
            act.wait_ge(a.turned, a.count(b, i))
            act.wait_ge(a.weighed, a.count(b, i - 2))
            dst, src = turned_half(m, a, 1 - s, 1)
            act.activation(dst, src, ACT.Copy).then_inc(a.high_copied, 1)

    act.wait_ge(a.normed, a.count(b, 0))
    a.slots(act, slot)


def attention_dve(dve, m, a, b, out):

    def slot(i, s, j):
        if a.has(i, 0):
            dve.wait_ge(a.scored, a.count(b, i + 1))
            dve.tensor_reduce(m.top[0:a.rows, s, 0:a.T],
                              m.pS[0:a.rows, s, 0:a.T * a.NK].rearrange("p (t k) -> p t k", k=a.NK),
                              AX_X, ALU.max, negate=True).then_inc(a.topped, 1)
        if a.has(i, 2):
            dve.wait_ge(a.weighed, a.count(b, i - 1))
            dve.wait_ge(a.inverted, a.count(b, i - 1))
            for t in range(a.T):
                last = dve.tensor_scalar(out(t, i - 2), m.pO[0:a.rows, s, t, 0:a.dh],
                                         m.inverse[0:a.rows, ds(i - 2, 1), t:t + 1], None, ALU.mult)
            last.then_inc(a.normed, 1)
        if a.has(i, 1):
            dve.wait_ge(a.turned, a.count(b, i))
            dve.reciprocal(m.inverse[0:a.rows, ds(i - 1, 1), 0:a.T],
                           m.total[0:a.rows, ds(i - 1, 1), 0:a.T]).then_inc(a.inverted, 1)
            dve.wait_ge(a.weighed, a.count(b, i - 2))
            dst, src = turned_half(m, a, 1 - s, 0)
            dve.tensor_copy(dst, src).then_inc(a.low_copied, 1)

    a.slots(dve, slot)


def cross_phase(nc, m, name, w, heads, scale, with_q=False, mask=None, fetch=None):
    with Phase(nc, name) as ph:
        a = Attention(ph, heads, C // heads, SK, scale, mask=mask)
        copied, keys_mm, values_mm = ph.sem("copied"), ph.sem("keys_mm"), ph.sem("values_mm")
        keys_ready, rest_ready, mask_ready = ph.sem("keys_ready"), ph.sem("rest_ready"), ph.sem("mask_ready")
        banks = m.banks
        fetch_sync(ph, fetch)

        @ph.block.gpsimd
        def _(pool):
            opened(pool, a.head_ready)
            with pool.Fori(0, B) as b:
                pool.wait_ge(values_mm, b + 1)
                pool.tensor_copy(m.ctx_now[:, :], m.ctxT[:, ds(b * SK, SK)])
                pool.tensor_copy(m.x_now[:, :], m.hT[:, ds(b * S, S)]).then_inc(copied, 1)
                pool.wait_ge(rest_ready, b + 1)
                attention_pool(pool, m, a, b)

        @ph.block.tensor
        def _(pe):
            opened(pe, a.scored, a.turned, a.weighed, values_mm)
            with pe.Fori(0, B) as b:
                pe.wait_ge(a.normed, a.count(b, 0))
                pe.matmul(banks[:, 0, :], w["wk"], m.ctxT[:, ds(b * SK, SK)], start=True, stop=True)
                pe.matmul(banks[:, 1, 0:S], w["wq"], m.hT[:, ds(b * S, S)], start=True,
                          stop=True).then_inc(keys_mm, 1)
                pe.wait_ge(copied, b + 1)
                for t in range(KT):
                    last = pe.matmul(banks[:, 2, t * P:(t + 1) * P], m.ctx_now[:, t * P:(t + 1) * P], w["wv"],
                                     start=True, stop=True)
                if with_q:
                    for t in range(QT):
                        last = pe.matmul(banks[:, 3, t * P:(t + 1) * P], m.x_now[:, t * P:(t + 1) * P], w["wq"],
                                         start=True, stop=True)
                last.then_inc(values_mm, 1)
                pe.wait_ge(keys_ready, b + 1)
                pe.wait_ge(rest_ready, b + 1)
                attention_pe(pe, m, a, b)

        @ph.block.scalar
        def _(act):
            opened(act, a.exped, a.high_copied)
            with act.Fori(0, B) as b:
                act.wait_ge(keys_mm, b + 1)
                act.activation(m.kT[:, 0, :], banks[:, 0, :], ACT.Identity, bias=w["bk"]).then_inc(keys_ready, 1)
                attention_act(act, m, a, b)

        @ph.block.vector
        def _(dve):
            opened(dve, a.topped, a.normed, a.low_copied, a.inverted)
            with dve.Fori(0, B) as b:
                dve.wait_ge(keys_mm, b + 1)
                dve.tensor_scalar(m.qT[:, 0, :], banks[:, 1, 0:S], w["bq"], None, ALU.add)
                dve.wait_ge(values_mm, b + 2)
                last = dve.tensor_tensor(m.v[:, :, 0:C], banks[:, 2, :].rearrange("p (t c) -> p t c", c=C),
                                         row(w["bv_row"], KT), ALU.add)
                if with_q:
                    last = dve.tensor_tensor(m.h[:, ds(b * QT, QT), :],
                                             banks[:, 3, 0:S].rearrange("p (t c) -> p t c", c=C),
                                             row(w["bq_row"], QT), ALU.add)
                last.then_inc(rest_ready, 1)
                attention_dve(dve, m, a, b,
                              lambda t, h: m.o[:, ds(b * QT + t, 1), ds(h * a.dh, a.dh)])


def project_pe(pe, m, weight, ready, turned, out_ready):
    if ready is not None:
        pe.wait_ge(*ready)
    turn_pe(pe, m, m.o, turned)
    pe.wait_ge(out_ready[0], 4)
    for g in range(4):
        for t in range(4):
            last = pe.matmul(m.banks[:, g, t * P:(t + 1) * P], m.hT[:, (4 * g + t) * P:(4 * g + t + 1) * P],
                             weight, start=True, stop=True)
        last.then_inc(out_ready[1], 1)


def l0_xattn_finish(nc, m, w):
    with Phase(nc, "L0x_finish") as ph:
        steps, centred, squared, varied, rooted, turned, copied, projected = (ph.sem(n) for n in (
            "steps", "centred", "squared", "varied", "rooted", "turned", "copied", "projected"))

        @ph.block.vector
        def _(dve):
            st = Steps(dve, steps)
            st.done(dve.tensor_tensor(wide(m.o), wide(m.o), wide(m.h), ALU.add))
            normalize_dve(dve, m, st, centred, squared, (varied, rooted), 1, m.o[:, :, :], m.o[:, :, :], 1e-5,
                          w["g0_row"], w["b0_row"])
            turn_out_dve(dve, m, m.hT, turned, copied)
            for g in range(4):
                dve.wait_ge(projected, g + 1)
                st.done(dve.tensor_tensor(m.h[:, 4 * g:4 * g + 4, :],
                                          m.banks[:, g, :].rearrange("p (t c) -> p t c", c=C),
                                          row(w["bo_row"], 4), ALU.add))
            st.done(dve.scalar_tensor_tensor(out=wide(m.o), in0=wide(m.h), scalar=0.0, in1=wide(m.o),
                                             op0=ALU.max, op1=ALU.add))
            normalize_dve(dve, m, st, centred, squared, (varied, rooted), 2, m.o[:, :, :], m.o[:, :, :], 1e-5,
                          w["g1_row"], w["b1_row"])
            st.done(dve.tensor_tensor(wide(m.x), wide(m.x), wide(m.o), ALU.add))

        @ph.block.scalar
        def _(act):
            normalize_act(act, m, centred, squared, varied, rooted, 1, m.o)
            turn_out_act(act, m, m.hT, turned, copied)
            normalize_act(act, m, centred, squared, varied, rooted, 2, m.o)

        @ph.block.tensor
        def _(pe):
            project_pe(pe, m, w["wo"], (steps, 8), turned, (copied, projected))


def xattn_finish(nc, m, name, w, x, bias=True):
    with Phase(nc, name + "_finish") as ph:
        steps, turned, copied, projected = (ph.sem(n) for n in ("steps", "turned", "copied", "projected"))

        @ph.block.vector
        def _(dve):
            st = Steps(dve, steps)
            if bias:
                st.done(dve.tensor_tensor(x[:, :, :], x[:, :, :], row(w["bo_row"], TILES), ALU.add))
            turn_out_dve(dve, m, m.hT, turned, copied)
            for g in range(4):
                dve.wait_ge(projected, g + 1)
                st.done(dve.tensor_tensor(wide(x[:, 4 * g:4 * g + 4, :]), wide(x[:, 4 * g:4 * g + 4, :]),
                                          m.banks[:, g, :], ALU.add))

        @ph.block.scalar
        def _(act):
            turn_out_act(act, m, m.hT, turned, copied)

        @ph.block.tensor
        def _(pe):
            project_pe(pe, m, w["wo"], None, turned, (copied, projected))


def key_mask_phase(nc, m, name, mask, boolean):
    n = B * SK // P
    with Phase(nc, name + "_mask") as ph:
        loaded, steps, stored = ph.sem("loaded"), ph.sem("steps"), ph.sem("stored")
        here = m.mask_u8 if boolean else m.mask_in
        parts = 1 if boolean else 3

        @ph.block.sync
        def _(sp):
            sp.dma_start(here[:, :], mask.rearrange("a (p n) -> (a p) n", n=n)).then_inc(loaded, 16)
            sp.wait_ge(steps, 3 if boolean else 7)
            for i in range(parts):
                sp.dma_start(m.key_mask[32 * i:32 * i + 1, :], m.mask_part[:, i, :]).then_inc(stored, 16)
            sp.wait_ge(stored, 16 * parts)

        @ph.block.vector
        def _(dve):
            st = Steps(dve, steps)
            part, rest = m.mask_part, m.mask_rest
            dve.wait_ge(loaded, 16)
            if boolean:
                dve.memset(m.key_mask[32:33, :], 0.0)
                dve.memset(m.key_mask[64:65, :], 0.0)
                st.done(dve.tensor_copy(m.mask_in[:, :], m.mask_u8[:, :]))
                st.done(dve.reciprocal(rest[:, 0, :], m.mask_in[:, :]))
                st.done(dve.tensor_scalar(part[:, 0, :], rest[:, 0, :], -1.0, 1.0, ALU.mult, ALU.add))
            else:
                st.done(dve.tensor_scalar(rest[:, 1, :], m.mask_in[:, :], -1.0, 1.0, ALU.mult, ALU.add))
                st.done(dve.tensor_scalar(rest[:, 0, :], rest[:, 1, :], -10000.0, None, ALU.mult))
                st.done(dve.tensor_copy(part[:, 0, :], rest[:, 0, :]))
                st.done(dve.tensor_tensor(rest[:, 1, :], rest[:, 0, :], part[:, 0, :], ALU.subtract))
                st.done(dve.tensor_copy(part[:, 1, :], rest[:, 1, :]))
                st.done(dve.tensor_tensor(rest[:, 2, :], rest[:, 1, :], part[:, 1, :], ALU.subtract))
                st.done(dve.tensor_copy(part[:, 2, :], rest[:, 2, :]))


def moe_phase(nc, m, name, x, experts, sizes, func, weighted, biases=None, row_bias=None, fetch=None):
    E, PIECES = len(experts), len(sizes)
    units = E * PIECES
    gated, hidden, prod = m.prob, m.probT[:, :, :, :].rearrange("p s c q -> p s (c q)"), m.banks
    with Phase(nc, name) as ph:
        expanded = ph.sem("expanded")
        activated = ph.sem("activated")
        multiplied = ph.sem("multiplied")
        contracted = ph.sem("contracted")
        combined = ph.sem("combined")
        biased = ph.sem("biased")
        fetch_sync(ph, fetch)

        @ph.block.tensor
        def _(pe):
            opened(pe, contracted)
            with pe.Fori(0, GROUPS) as g:
                def expand(n):
                    gate, up, _ = experts[n // PIECES]
                    size, s = sizes[n % PIECES], n % 2
                    pe.wait_ge(multiplied, g * units + 1 + max(n - 1, 0))
                    moving = m.hT[:, ds(g * GROUP, GROUP)]
                    pe.matmul(prod[0:size, s, :], gate(n % PIECES), moving, start=True, stop=True)
                    pe.matmul(prod[0:size, 2 + s, :], up(n % PIECES), moving, start=True,
                              stop=True).then_inc(expanded, 1)

                def contract(n):
                    e, i, s = n // PIECES, n % PIECES, n % 2
                    size, down = sizes[i], experts[e][2]
                    pe.wait_ge(multiplied, g * units + n + 2)
                    if i == 0:
                        pe.wait_ge(combined, g * E + 1 + max(e - 1, 0))
                    for t in range(GT):
                        last = pe.matmul(m.pT[:, e % 2, t * C:(t + 1) * C], hidden[0:size, s, t * P:(t + 1) * P],
                                         down(i), start=i == 0 and t == 0, stop=i == PIECES - 1,
                                         skip_group_check=True)
                    last.then_inc(contracted, 1)

                for n in range(units):
                    expand(n)
                    if n:
                        contract(n - 1)
                contract(units - 1)

        @ph.block.scalar
        def _(act):
            with act.Fori(0, GROUPS) as g:
                for n in range(units):
                    size, s = sizes[n % PIECES], n % 2
                    act.wait_ge(expanded, g * units + n + 1)
                    act.wait_ge(multiplied, g * units + 1 + max(n - 1, 0))
                    bias = 0.0 if biases is None else biases[1][0:size, n:n + 1]
                    act.activation(gated[0:size, s, 0:GROUP], prod[0:size, s, :], func,
                                   bias=bias).then_inc(activated, 1)

        @ph.block.vector
        def _(dve):
            opened(dve, multiplied, combined)
            if row_bias is not None:
                dve.tensor_tensor(x[:, :, :], x[:, :, :], row(row_bias, TILES), ALU.add).then_inc(biased, 1)
                dve.wait_ge(biased, 1)
            with dve.Fori(0, GROUPS) as g:
                def multiply(n):
                    size, s = sizes[n % PIECES], n % 2
                    dve.wait_ge(activated, g * units + n + 1)
                    dve.wait_ge(contracted, g * units + 1 + max(n - 1, 0))
                    if biases is None:
                        ins = dve.tensor_tensor(hidden[0:size, s, 0:GROUP], gated[0:size, s, 0:GROUP],
                                                prod[0:size, 2 + s, :], ALU.mult)
                    else:
                        ins = dve.scalar_tensor_tensor(out=hidden[0:size, s, 0:GROUP], in0=prod[0:size, 2 + s, :],
                                                       scalar=biases[0][0:size, n:n + 1],
                                                       in1=gated[0:size, s, 0:GROUP], op0=ALU.add, op1=ALU.mult)
                    ins.then_inc(multiplied, 1)

                def combine(e):
                    dve.wait_ge(contracted, g * units + (e + 1) * PIECES + 1)
                    dve.wait_ge(combined, g * E + e + 1)
                    here = x[:, ds(g * GT, GT), :]
                    if weighted[e] is None:
                        last = dve.tensor_tensor(here, here, m.pT[:, e % 2, :].rearrange("p (t c) -> p t c", c=C),
                                                 ALU.add)
                    else:
                        for t in range(GT):
                            tile = x[:, ds(g * GT + t, 1), :]
                            last = dve.scalar_tensor_tensor(
                                out=tile, in0=m.pT[:, e % 2, t * C:(t + 1) * C].unsqueeze(1),
                                scalar=m.weight[:, ds(g * GT + t, 1), weighted[e]:weighted[e] + 1], in1=tile,
                                op0=ALU.mult, op1=ALU.add)
                    last.then_inc(combined, 1)

                for n in range(units):
                    multiply(n)
                    if n >= PIECES and n % PIECES == 0:
                        combine(n // PIECES - 1)
                combine(E - 1)


def route_phase(nc, m, name, router, experts, keep, bias=None, softmax=True, eps=None):
    E = experts
    with Phase(nc, name + "_route") as ph:
        steps, scored, shifted, exped = ph.sem("steps"), ph.sem("scored"), ph.sem("shifted"), ph.sem("exped")
        p, wt = m.scores16[:, :, 0:E], m.weight[:, :, 0:E]
        logits = m.pG[:, 0:TILES * E].rearrange("p (t e) -> p t e", e=E)
        more = m.prob[:, :, :].rearrange("p s n -> p (s n)")[:, 0:TILES * E * E].rearrange(
            "p (t e f) -> p t e f", e=E, f=E)
        same = m.probT[:, :, :, :].rearrange("p s c q -> p (s c q)")[:, 0:TILES * E * E].rearrange(
            "p (t e f) -> p t e f", e=E, f=E)

        @ph.block.tensor
        def _(pe):
            for t in range(TILES):
                last = pe.matmul(m.pG[:, t * E:(t + 1) * E], m.hT[:, t * P:(t + 1) * P], router, start=True, stop=True)
            last.then_inc(scored, 1)

        @ph.block.scalar
        def _(act):
            if softmax:
                act.wait_ge(shifted, 1)
                act.activation(p, p, ACT.Exp).then_inc(exped, 1)

        @ph.block.vector
        def _(dve):
            st = Steps(dve, steps)
            dve.wait_ge(scored, 1)
            if bias is None:
                st.done(dve.tensor_copy(p, logits))
            else:
                st.done(dve.tensor_tensor(p, logits, row(bias, TILES), ALU.add))
            if softmax:
                st.done(dve.tensor_reduce(m.sum[:, :], p, AX_X, ALU.max))
                dve.tensor_tensor(p, p, each(m.sum[:, :], E), ALU.subtract).then_inc(shifted, 1)
                dve.wait_ge(exped, 1)
                st.done(dve.tensor_reduce(m.var[:, :], p, AX_X, ALU.add))
                st.done(dve.reciprocal(m.rstd[:, :], m.var[:, :]))
                st.done(dve.tensor_tensor(p, p, each(m.rstd[:, :], E), ALU.mult))
            other = p.unsqueeze(2).broadcast_to([P, TILES, E, E])
            before = m.k["before"].rearrange("p (e f) -> p e f", f=8)[:, 0:E, 0:E].unsqueeze(1).broadcast_to(
                [P, TILES, E, E])
            st.done(dve.tensor_tensor(more, other, each(p, E), ALU.is_gt))
            st.done(dve.tensor_tensor(same, other, each(p, E), ALU.is_equal))
            st.done(dve.tensor_tensor(same, same, before, ALU.mult))
            st.done(dve.tensor_tensor(more, more, same, ALU.add))
            st.done(dve.tensor_reduce(m.rank[:, :, 0:E], more, AX_X, ALU.add))
            if not softmax:
                st.done(dve.tensor_scalar(wt, m.rank[:, :, 0:E], keep - 0.5, None, ALU.is_lt))
                return
            st.done(dve.tensor_scalar(m.rank[:, :, 0:E], m.rank[:, :, 0:E], keep - 0.5, None, ALU.is_lt))
            st.done(dve.tensor_tensor(wt, m.rank[:, :, 0:E], p, ALU.mult))
            st.done(dve.tensor_reduce(m.sum[:, :], wt, AX_X, ALU.add))
            if eps is not None:
                st.done(dve.tensor_scalar(m.sum[:, :], m.sum[:, :], eps, None, ALU.add))
            st.done(dve.reciprocal(m.rstd[:, :], m.sum[:, :]))
            st.done(dve.tensor_tensor(wt, wt, each(m.rstd[:, :], E), ALU.mult))


def stacked(w, hidden, shared=True):
    n = len(pieces(hidden))

    def expert(e):
        def part(name):
            return lambda i: w[name][:, e * hidden + pieces(hidden)[i][0]:e * hidden + sum(pieces(hidden)[i])]

        def down(i):
            return w["down"][0:pieces(hidden)[i][1], (e * n + i) * C:(e * n + i + 1) * C]
        return part("gate"), part("up"), down
    return expert


def affine_phase(nc, m, name, src, dst, scale, shift, back=False, columns=None):
    with Phase(nc, name) as ph:
        steps, centred, squared, varied, rooted, turned, copied = (ph.sem(n) for n in (
            "steps", "centred", "squared", "varied", "rooted", "turned", "copied"))
        first = 4 if back else 0
        flat = wide(dst)

        @ph.block.vector
        def _(dve):
            st = Steps(dve, steps)
            if back:
                turn_out_dve(dve, m, flat, turned, copied)
                dve.wait_ge(copied, 4)
            normalize_dve(dve, m, st, centred, squared, (varied, rooted), 1, src[:, :, :], dst[:, :, :], 1e-5,
                          scale, shift)
            for g in (1, 3):
                dve.wait_ge(turned, first + g + 1)
                if columns is None:
                    dve.tensor_copy(m.hT[:, g * 512:(g + 1) * 512], m.banks[:, g, :])
                else:
                    dve.tensor_scalar(m.hT[:, g * 512:(g + 1) * 512], m.banks[:, g, :], columns[0], columns[1],
                                      ALU.mult, ALU.add)

        @ph.block.scalar
        def _(act):
            if back:
                turn_out_act(act, m, flat, turned, copied)
            normalize_act(act, m, centred, squared, varied, rooted, 1, dst)
            for g in (0, 2):
                act.wait_ge(turned, first + g + 1)
                if columns is None:
                    act.activation(m.hT[:, g * 512:(g + 1) * 512], m.banks[:, g, :], ACT.Copy)
                else:
                    act.activation(m.hT[:, g * 512:(g + 1) * 512], m.banks[:, g, :], ACT.Identity,
                                   scale=columns[0], bias=columns[1])

        @ph.block.tensor
        def _(pe):
            if back:
                turn_pe(pe, m, m.hT[:, :].rearrange("p (t c) -> p t c", c=P), turned)
            pe.wait_ge(steps, 5 if scale is None else 7)
            turn_pe(pe, m, dst, turned)


def shift_phase(nc, m, name, y, w):
    half = C // 2
    with Phase(nc, name) as ph:
        turned, cleared = ph.sem("turned"), ph.sem("cleared")
        shifted = m.hT[half:C, :].rearrange("p (b s) -> p b s", s=S)

        @ph.block.gpsimd
        def _(pool):
            pool.memset(shifted[:, :, 0:1], 0.0).then_inc(cleared, 1)
            pool.wait_ge(cleared, 1)
            if w is not None:
                for n, (scale, cos, sin) in enumerate(((w["qs_row"], "xq_cos", "xq_sin"),
                                                       (w["ks_row"], "xk_cos", "xk_sin"))):
                    c = m.k[cos].rearrange("p (t d) -> p t d", d=WIDE)
                    s = m.k[sin].rearrange("p (t d) -> p t d", d=WIDE)
                    at = slice(2 * n, 2 * n + 2)
                    h = WIDE // 2
                    pool.tensor_tensor(m.turn_cos[:, at, :], c, row(scale, QT), ALU.mult)
                    pool.tensor_tensor(m.turn_sin[:, at, 0:h], s[:, :, 0:h], row(scale[:, h:WIDE], QT), ALU.mult)
                    pool.tensor_tensor(m.turn_sin[:, at, h:WIDE], s[:, :, h:WIDE], row(scale[:, 0:h], QT), ALU.mult)

        @ph.block.tensor
        def _(pe):
            turn_pe(pe, m, y, turned)

        def move(g, copy):
            bank = m.banks[:, g, :].rearrange("p (b s) -> p b s", s=S)
            copy(m.hT[0:half, g * 512:(g + 1) * 512], m.banks[0:half, g, :])
            copy(shifted[:, 2 * g:2 * g + 2, 1:S], bank[half:C, :, 0:S - 1])

        @ph.block.scalar
        def _(act):
            for g in (0, 2):
                act.wait_ge(turned, g + 1)
                move(g, lambda dst, src: act.activation(dst, src, ACT.Copy))

        @ph.block.vector
        def _(dve):
            for g in (1, 3):
                dve.wait_ge(turned, g + 1)
                move(g, lambda dst, src: dve.tensor_copy(dst, src))


def output_pe(pe, m, w, n, o, o_turned, oT_ready, out_mm, b):
    for c in range(n):
        for t in range(QT):
            last = pe.transpose(m.banks[:, c // 2, (c % 2) * S + t * P:(c % 2) * S + (t + 1) * P],
                                o[:, t, c * P:(c + 1) * P], m.k["ident"])
    last.then_inc(o_turned, 1)
    pe.wait_ge(oT_ready, b + 1)
    for t in range(QT):
        for c in range(n):
            last = pe.matmul(m.pG[:, t * P:(t + 1) * P], m.qT[:, c, t * P:(t + 1) * P], w[:, c * C:(c + 1) * C],
                             start=c == 0, stop=c == n - 1)
    last.then_inc(out_mm, 1)


def local_phase(nc, m, name, w, y, fetch=None):
    CH, W = CHUNKS_L0F, CHUNKS_L0F * P
    with Phase(nc, name) as ph:
        a = Attention(ph, L0F_HEADS, WIDE, S, m.k["scale_L0f"], mask="tiles")
        (copied, multiplied, values_ready, squared, summed, rooted, rotated, joined, scaled, turned, queries_ready,
         keys_ready, o_turned, oT_ready, out_mm, done) = (ph.sem(n) for n in (
             "copied", "multiplied", "values_ready", "squared", "summed", "rooted", "rotated", "joined", "scaled",
             "qk_turned", "queries_ready", "keys_ready", "o_turned", "oT_ready", "out_mm", "done"))
        fetch_sync(ph, fetch)
        squares = m.probT[:, :, :, :].rearrange("p s c q -> p (s c q)")
        swapped = m.prob[:, :, :].rearrange("p s (c n) -> p (s c) n", n=512)
        rotating = m.h[:, :, :].rearrange("p (a b) c -> p a (b c)", b=4)
        o = m.o[:, 0:8, :].rearrange("p (t c) d -> p t (c d)", t=QT)

        def by_head(ap):
            return ap.rearrange("p a (h d) -> p a h d", d=WIDE)

        @ph.block.gpsimd
        def _(pool):
            opened(pool, a.head_ready)
            with pool.Fori(0, B) as b:
                pool.wait_ge(multiplied, b + 1)
                pool.tensor_copy(m.x_now[:, :], m.hT[:, ds(b * S, S)]).then_inc(copied, 1)
                pool.wait_ge(rotated, b + 1)
                pool.tensor_tensor(rotating, rotating, swapped, ALU.add).then_inc(joined, 1)
                pool.wait_ge(joined, b + 1)
                pool.tensor_tensor(wide(m.h).rearrange("p (n d) -> p n d", d=WIDE),
                                   wide(m.h).rearrange("p (n d) -> p n d", d=WIDE),
                                   each(m.inv_norm[:, :, :].rearrange("p a h -> p (a h)"), WIDE),
                                   ALU.mult).then_inc(scaled, 1)
                pool.wait_ge(queries_ready, b + 1)
                attention_pool(pool, m, a, b)

        @ph.block.tensor
        def _(pe):
            opened(pe, a.scored, a.turned, a.weighed, multiplied)
            with pe.Fori(0, B) as b:
                pe.wait_ge(copied, b + 1)
                pe.wait_ge(done, b + 1)
                for t in range(QT):
                    x = m.x_now[:, t * P:(t + 1) * P]
                    pe.matmul(m.banks[:, t, :], x, w["wqkv"][:, 0:W], start=True, stop=True)
                    pe.matmul(m.banks[:, 2 + t, :], x, w["wqkv"][:, W:2 * W], start=True, stop=True)
                    last = pe.matmul(m.pT[:, t, :], x, w["wqkv"][:, 2 * W:3 * W], start=True, stop=True)
                last.then_inc(multiplied, 1)
                pe.wait_ge(scaled, b + 1)
                for n in range(2):
                    for c in range(CH):
                        for t in range(QT):
                            at = (c % 2) * S + t * P
                            last = pe.transpose(m.banks[:, 2 * n + c // 2, at:at + P],
                                                rotating[:, 2 * n + t, c * P:(c + 1) * P], m.k["ident"])
                last.then_inc(turned, 1)
                for s in (queries_ready, keys_ready, values_ready):
                    pe.wait_ge(s, b + 1)
                attention_pe(pe, m, a, b)
                pe.wait_ge(a.normed, a.count(b, a.H))
                output_pe(pe, m, w["wo"], CH, o, o_turned, oT_ready, out_mm, b)

        @ph.block.scalar
        def _(act):
            opened(act, a.exped, a.high_copied)
            with act.Fori(0, B) as b:
                act.wait_ge(multiplied, b + 2)
                act.activation(squares.rearrange("p (a n) -> p a n", a=4), m.banks, ACT.Square).then_inc(squared, 1)
                act.activation(m.v[:, 0:QT, 0:W], m.pT[:, :, :], ACT.Copy).then_inc(values_ready, 1)
                act.wait_ge(summed, b + 1)
                act.activation(m.inv_norm[:, :, :], m.norm[:, :, :], ACT.Sqrt).then_inc(rooted, 1)
                act.wait_ge(turned, b + 1)
                act.activation(m.kT[:, 0:CH, 0:S],
                               m.banks[:, 2:4, :].rearrange("p a (c q) -> p (a c) q", q=S),
                               ACT.Copy).then_inc(keys_ready, 1)
                attention_act(act, m, a, b)
                act.wait_ge(o_turned, b + 1)
                act.activation(m.qT[:, 0:CH, :], m.banks[:, 0:2, :].rearrange("p a (c q) -> p (a c) q", q=S),
                               ACT.Copy).then_inc(oT_ready, 1)

        @ph.block.vector
        def _(dve):
            opened(dve, a.topped, a.normed, a.low_copied, a.inverted, done)
            st = ph.sem("dve_steps")
            with dve.Fori(0, B) as b:
                steps = Steps(dve, st, base=b * 2)
                dve.wait_ge(squared, b + 1)
                dve.tensor_reduce(m.norm[:, :, :].rearrange("p a h -> p (a h)"),
                                  squares.rearrange("p (n d) -> p n d", d=WIDE), AX_X, ALU.add).then_inc(summed, 1)
                h = WIDE // 2
                qk, sw = by_head(m.banks), by_head(swapped)
                cos = m.turn_cos[:, :, :].unsqueeze(2).broadcast_to([P, 4, L0F_HEADS, WIDE])
                sin = m.turn_sin[:, :, :].unsqueeze(2).broadcast_to([P, 4, L0F_HEADS, WIDE])
                dve.tensor_tensor(by_head(rotating), qk, cos, ALU.mult)
                dve.tensor_tensor(sw[:, :, :, 0:h], qk[:, :, :, h:WIDE], sin[:, :, :, 0:h], ALU.mult)
                dve.tensor_tensor(sw[:, :, :, h:WIDE], qk[:, :, :, 0:h], sin[:, :, :, h:WIDE], ALU.mult)
                dve.wait_ge(rooted, b + 1)
                steps.done(dve.tensor_scalar(m.norm[:, :, :], m.inv_norm[:, :, :], 1e-12, None, ALU.max))
                dve.reciprocal(m.inv_norm[:, :, :], m.norm[:, :, :]).then_inc(rotated, 1)
                dve.wait_ge(turned, b + 1)
                dve.tensor_copy(m.qT[:, 0:CH, :],
                                m.banks[:, 0:2, :].rearrange("p a (c q) -> p (a c) q", q=S)).then_inc(queries_ready, 1)
                attention_dve(dve, m, a, b, lambda t, h_: o[:, t:t + 1, ds(h_ * WIDE, WIDE)])
                dve.wait_ge(out_mm, b + 1)
                here = y[:, ds(b * QT, QT), :]
                steps.done(dve.tensor_tensor(here, here, m.pG[:, 0:S].rearrange("p (t c) -> p t c", c=C), ALU.add))
                dve.sem_inc(done, 1)


def place_mask_phase(nc, m, name, which):
    with Phase(nc, name) as ph:
        @ph.block.vector
        def _(dve):
            dve.tensor_copy(m.bandb[:, :, :].rearrange("p t k -> p (t k)"), m.k[which])


def add_phase(nc, m, name):
    with Phase(nc, name) as ph:
        @ph.block.vector
        def _(dve):
            dve.tensor_tensor(wide(m.x), wide(m.x), wide(m.xn), ALU.add)


def l0_ffn(nc, m, w, fetch):
    prepare(nc, m, "L0f")
    place_mask_phase(nc, m, "L0f_mask", "band")
    for d in range(2):
        wd = {n[:-1]: v for n, v in w.items() if n.endswith(str(d))}
        shift_phase(nc, m, f"L0f{d}_shift", m.xn, wd)
        local_phase(nc, m, f"L0f{d}_attend", wd, m.xn, fetch if d == 0 else None)
        shift_phase(nc, m, f"L0f{d}_shift2", m.xn, None)
        affine_phase(nc, m, f"L0f{d}_norm", m.o, m.o, None, None, back=True, columns=(wd["g"], wd["b"]))
        cut = pieces(L0F_HID)
        value = lambda i: wd["w1"][:, cut[i][0]:sum(cut[i])]
        gate = lambda i: wd["w1"][:, L0F_HID + cut[i][0]:L0F_HID + sum(cut[i])]
        down = lambda i: wd["w2"][0:cut[i][1], i * C:(i + 1) * C]
        moe_phase(nc, m, f"L0f{d}_glu", m.xn, [(gate, value, down)], [n for _, n in cut], ACT.Gelu, [None],
                  biases=(wd["b1"][:, 0:3], wd["b1"][:, 3:6]), row_bias=wd["b2_row"])
    add_phase(nc, m, "L0f_add")


def select_phase(nc, m, w, sel, selT):
    with Phase(nc, "L2x_select") as ph:
        steps, diagonal, spread, own_read, picked, turned, copied, queries, taken = (ph.sem(n) for n in (
            "steps", "diagonal", "spread", "own_read", "picked", "turned", "copied", "queries", "taken"))
        more = m.kT[:, :, :].rearrange("p c n -> p (c n)").rearrange("p (b t j) -> p b t j", b=B, t=QT)
        same = m.v[:, :, :].rearrange("p c n -> p (c n)").rearrange("p (b t j) -> p b t j", b=B, t=QT)
        every = m.banks.rearrange("p a n -> p (a n)").rearrange("p (b j) -> p b j", j=S)
        ident = m.k["ident"].unsqueeze(1).broadcast_to([P, TILES, P])

        @ph.block.tensor
        def _(pe):
            pe.wait_ge(diagonal, 1)
            for g in range(4):
                last = pe.matmul(m.banks[:, g, :], m.ones[:, :], wide(m.h)[:, g * 512:(g + 1) * 512], start=True,
                                 stop=True)
            last.then_inc(spread, 1)
            pe.wait_ge(picked, 1)
            turn_pe(pe, m, sel, turned, rows=L2_CAP)
            pe.wait_ge(copied, 4)
            for g in range(4):
                for t in range(4):
                    last = pe.matmul(m.banks[:, g, t * P:(t + 1) * P], m.hT[:, (4 * g + t) * P:(4 * g + t + 1) * P],
                                     w["wq"], start=True, stop=True)
            last.then_inc(queries, 1)

        @ph.block.vector
        def _(dve):
            st = Steps(dve, steps)
            st.done(dve.tensor_tensor(m.h[:, :, :], m.xn[:, :, :], row(w["router_row"], TILES), ALU.mult))
            st.done(dve.tensor_reduce(m.route[:, :], m.h[:, :, :], AX_X, ALU.add))
            dve.tensor_tensor(m.h[:, :, :], ident, each(m.route[:, :], P), ALU.mult).then_inc(diagonal, 1)
            dve.wait_ge(spread, 1)
            st.done(dve.tensor_tensor(m.o[:, :, :], m.banks.rearrange("p a (t c) -> p (a t) c", c=P), ident,
                                      ALU.mult))
            st.done(dve.tensor_reduce(m.own[:, :], m.o[:, :, :], AX_X, ALU.add))
            own = each(m.own[:, :].rearrange("p (b t) -> p b t", t=QT), S)
            for b in range(2):
                at = slice(4 * b, 4 * b + 4)
                other = every[:, at, :].unsqueeze(2).broadcast_to([P, 4, QT, S])
                mine = own[:, at]
                for n in range(4):
                    st.done(dve.tensor_tensor(more[:, 4 * b + n], other[:, n], mine[:, n], ALU.is_gt))
                    st.done(dve.tensor_tensor(same[:, 4 * b + n], other[:, n], mine[:, n], ALU.is_equal))
            earlier = m.k["earlier"].rearrange("p (t j) -> p t j", t=QT).unsqueeze(1).broadcast_to([P, B, QT, S])
            st.done(dve.tensor_tensor(same, same, earlier, ALU.mult))
            st.done(dve.tensor_tensor(more, more, same, ALU.add))
            st.done(dve.tensor_reduce(m.own[:, :].rearrange("p (b t) -> p b t", t=QT), more, AX_X, ALU.add))
            dve.tensor_tensor(sel, row(m.k["slot"], TILES), each(m.own[:, :], L2_CAP), ALU.is_equal).then_inc(picked, 1)
            turn_out_dve(dve, m, selT, turned, copied, rows=L2_CAP)
            dve.wait_ge(queries, 1)
            rope = m.k["l2_ropeq"].rearrange("p (n) -> p n").unsqueeze(1).broadcast_to([P, B, QT * C])
            dve.tensor_tensor(wide(m.h).rearrange("p (b n) -> p b n", b=B),
                              m.banks.rearrange("p a (b n) -> p (a b) n", b=2), rope, ALU.mult)

        @ph.block.scalar
        def _(act):
            turn_out_act(act, m, selT, turned, copied, rows=L2_CAP)


def chosen_phase(nc, m, w, sel, selT, fetch):
    with Phase(nc, "L2x_attend") as ph:
        a = Attention(ph, L2_HEADS, C // L2_HEADS, SK, m.k["scale_8"], q_rows=L2_CAP, tiles=1)
        cleared, copied, multiplied, ready, values_ready, scattered, done = (ph.sem(n) for n in (
            "cleared", "copied", "multiplied", "ready", "values_ready", "scattered", "done"))
        banks = m.banks
        fetch_sync(ph, fetch)

        @ph.block.gpsimd
        def _(pool):
            opened(pool, a.head_ready)
            pool.memset(m.prob[L2_CAP:P, :, :], 0.0).then_inc(cleared, 1)
            pool.wait_ge(cleared, 1)
            with pool.Fori(0, B) as b:
                pool.wait_ge(multiplied, b + 1)
                pool.tensor_copy(m.ctx_now[:, :], m.ctxT[:, ds(b * SK, SK)])
                pool.tensor_copy(m.x_now[:, :], wide(m.h)[:, ds(b * S, S)]).then_inc(copied, 1)
                pool.wait_ge(ready, b + 1)
                attention_pool(pool, m, a, b)

        @ph.block.tensor
        def _(pe):
            opened(pe, a.scored, a.turned, a.weighed, multiplied)
            with pe.Fori(0, B) as b:
                pe.wait_ge(done, b + 1)
                pe.wait_ge(copied, b + 1)
                pe.matmul(banks[:, 0, :], w["wk"], m.ctxT[:, ds(b * SK, SK)], start=True, stop=True)
                for t in range(QT):
                    pe.matmul(banks[:, 1, 0:L2_CAP], m.x_now[:, t * P:(t + 1) * P],
                              sel[:, ds(b * QT + t, 1), :], start=t == 0, stop=t == QT - 1)
                for t in range(KT):
                    last = pe.matmul(banks[:, 2, t * P:(t + 1) * P], m.ctx_now[:, t * P:(t + 1) * P], w["wv"],
                                     start=True, stop=True)
                last.then_inc(multiplied, 1)
                pe.wait_ge(ready, b + 1)
                pe.wait_ge(values_ready, b + 1)
                attention_pe(pe, m, a, b)
                pe.wait_ge(a.normed, a.count(b, a.H))
                pe.matmul(m.pG[:, 0:S], m.o_now[0:L2_CAP, :], selT[0:L2_CAP, ds(b * S, S)], start=True,
                          stop=True).then_inc(scattered, 1)

        @ph.block.scalar
        def _(act):
            opened(act, a.exped, a.high_copied, done)
            with act.Fori(0, B) as b:
                act.wait_ge(multiplied, b + 2)
                act.activation(m.v[:, :, 0:C], banks[:, 2, :].rearrange("p (t c) -> p t c", c=C),
                               ACT.Copy).then_inc(values_ready, 1)
                attention_act(act, m, a, b)
                act.wait_ge(scattered, b + 1)
                act.activation(wide(m.o)[:, ds(b * S, S)], m.pG[:, 0:S], ACT.Copy).then_inc(done, 1)

        @ph.block.vector
        def _(dve):
            opened(dve, a.topped, a.normed, a.low_copied, a.inverted)
            with dve.Fori(0, B) as b:
                dve.wait_ge(multiplied, b + 2)
                dve.tensor_tensor(m.kT[:, 0, :], banks[:, 0, :], m.k["l2_ropek"], ALU.mult)
                dve.tensor_copy(m.qT[:, 0, 0:L2_CAP], banks[:, 1, 0:L2_CAP]).then_inc(ready, 1)
                attention_dve(dve, m, a, b, lambda t, h: m.o_now[0:L2_CAP, ds(h * a.dh, a.dh)])


def chosen_finish(nc, m, w):
    with Phase(nc, "L2x_finish") as ph:
        steps, projected = ph.sem("steps"), ph.sem("projected")

        @ph.block.tensor
        def _(pe):
            for g in range(4):
                for t in range(4):
                    at = (4 * g + t) * P
                    last = pe.matmul(m.banks[:, g, t * P:(t + 1) * P], wide(m.o)[:, at:at + P], w["wo"], start=True,
                                     stop=True)
                last.then_inc(projected, 1)

        @ph.block.vector
        def _(dve):
            st = Steps(dve, steps)
            for g in range(4):
                at = slice(4 * g, 4 * g + 4)
                dve.wait_ge(projected, g + 1)
                st.done(dve.tensor_tensor(m.h[:, at, :], m.banks[:, g, :].rearrange("p (t c) -> p t c", c=C),
                                          each(m.route[:, at], C), ALU.mult))
                st.done(dve.tensor_tensor(m.x[:, at, :], m.x[:, at, :], m.h[:, at, :], ALU.add))


def wide_cross_phase(nc, m, w, fetch):
    CH, W = CHUNKS_L3, CHUNKS_L3 * P
    HALVES = W // 512
    with Phase(nc, "L3x_attend") as ph:
        a = Attention(ph, L3_HEADS, WIDE, SK, m.k["scale_L3x"], mask="keys")
        (copied, keys_mm, rest_mm, keys_ready, rest_ready, o_turned, oT_low, oT_ready, out_mm, done, biased) = (
            ph.sem(n) for n in ("copied", "keys_mm", "rest_mm", "keys_ready", "rest_ready", "o_turned", "oT_low",
                                "oT_ready", "out_mm", "done", "biased"))
        banks = m.banks
        rest = CH + KT * HALVES
        o = m.o[:, :, :].rearrange("p (t c) d -> p t (c d)", t=QT)
        fetch_sync(ph, fetch)

        @ph.block.gpsimd
        def _(pool):
            opened(pool, a.head_ready)
            with pool.Fori(0, B) as b:
                pool.wait_ge(done, b + 1)
                pool.tensor_copy(m.ctx_now[:, :], m.ctxT[:, ds(b * SK, SK)]).then_inc(copied, 1)
                pool.wait_ge(rest_ready, b * rest + rest + 1)
                attention_pool(pool, m, a, b)

        @ph.block.tensor
        def _(pe):
            opened(pe, a.scored, a.turned, a.weighed, keys_mm, rest_mm)
            with pe.Fori(0, B) as b:
                pe.wait_ge(done, b + 1)
                for c in range(CH):
                    if c >= 2:
                        pe.wait_ge(keys_ready, b * CH + c)
                    pe.matmul(banks[:, c % 2, :], w["wk"][:, c * P:(c + 1) * P], m.ctxT[:, ds(b * SK, SK)],
                              start=True, stop=True).then_inc(keys_mm, 1)
                    if c >= 2:
                        pe.wait_ge(rest_ready, b * rest + c)
                    pe.matmul(banks[:, 2 + c % 2, 0:S], w["wq"][:, c * P:(c + 1) * P], m.hT[:, ds(b * S, S)],
                              start=True, stop=True).then_inc(rest_mm, 1)
                pe.wait_ge(copied, b + 1)
                for n in range(KT * HALVES):
                    t, half = n // HALVES, n % HALVES
                    pe.wait_ge(rest_ready, b * rest + CH + n)
                    pe.matmul(banks[:, 2 + n % 2, :], m.ctx_now[:, t * P:(t + 1) * P],
                              w["wv"][:, half * 512:(half + 1) * 512], start=True, stop=True).then_inc(rest_mm, 1)
                pe.wait_ge(keys_ready, b * CH + CH + 1)
                pe.wait_ge(rest_ready, b * rest + rest + 1)
                attention_pe(pe, m, a, b)
                pe.wait_ge(a.normed, a.count(b, a.H))
                output_pe(pe, m, w["wo"], CH, o, o_turned, oT_ready, out_mm, b)

        @ph.block.scalar
        def _(act):
            opened(act, a.exped, a.high_copied, keys_ready)
            with act.Fori(0, B) as b:
                for c in range(CH):
                    act.wait_ge(keys_mm, b * CH + c + 2)
                    act.activation(m.kT[:, c, :], banks[:, c % 2, :], ACT.Identity,
                                   bias=w["bk"][:, c:c + 1]).then_inc(keys_ready, 1)
                attention_act(act, m, a, b)
                act.wait_ge(o_turned, b + 1)
                act.activation(m.qT[:, 4:8, :], banks[:, 2:4, :].rearrange("p a (c q) -> p (a c) q", q=S), ACT.Copy)
                act.wait_ge(oT_low, b + 1)
                act.activation(m.qT[:, 2:4, :], banks[:, 1, :].rearrange("p (c q) -> p c q", q=S),
                               ACT.Copy).then_inc(oT_ready, 1)

        @ph.block.vector
        def _(dve):
            opened(dve, a.topped, a.normed, a.low_copied, a.inverted, rest_ready, done)
            dve.tensor_tensor(m.x[:, :, :], m.x[:, :, :], row(w["bo_row"], TILES), ALU.add).then_inc(biased, 1)
            dve.wait_ge(biased, 1)
            with dve.Fori(0, B) as b:
                for c in range(CH):
                    dve.wait_ge(rest_mm, b * rest + c + 2)
                    dve.tensor_scalar(m.qT[:, c, :], banks[:, 2 + c % 2, 0:S], w["bq"][:, c:c + 1], None,
                                      ALU.add).then_inc(rest_ready, 1)
                for n in range(KT * HALVES):
                    t, half = n // HALVES, n % HALVES
                    at = slice(half * 512, (half + 1) * 512)
                    dve.wait_ge(rest_mm, b * rest + CH + n + 2)
                    dve.tensor_tensor(m.v[:, t, at], banks[:, 2 + n % 2, :], w["bv_row"][:, at],
                                      ALU.add).then_inc(rest_ready, 1)
                attention_dve(dve, m, a, b, lambda t, h: o[:, t:t + 1, ds(h * WIDE, WIDE)])
                dve.wait_ge(o_turned, b + 1)
                dve.tensor_copy(m.qT[:, 0:2, :],
                                banks[:, 0, :].rearrange("p (c q) -> p c q", q=S)).then_inc(oT_low, 1)
                dve.wait_ge(out_mm, b + 1)
                here = m.x[:, ds(b * QT, QT), :]
                dve.tensor_tensor(here, here, m.pG[:, 0:S].rearrange("p (t c) -> p t c", c=C),
                                  ALU.add).then_inc(done, 1)


def conv_phase(nc, m, w):
    with Phase(nc, "L3f_conv") as ph:
        steps = ph.sem("steps")
        src = m.hT[:, :].rearrange("p (b s) -> p b s", s=S)
        dst = wide(m.h).rearrange("p (b s) -> p b s", s=S)

        @ph.block.vector
        def _(dve):
            st = Steps(dve, steps)
            st.done(dve.tensor_scalar(dst, src, w["conv"][:, 2:3], None, ALU.mult))
            for back in (1, 2):
                st.done(dve.scalar_tensor_tensor(out=dst[:, :, back:S], in0=src[:, :, 0:S - back],
                                                 scalar=w["conv"][:, 2 - back:3 - back], in1=dst[:, :, back:S],
                                                 op0=ALU.mult, op1=ALU.add))


def causal_phase(nc, m, w, fetch=None):
    with Phase(nc, "L3f_attend") as ph:
        a = Attention(ph, L3F_HEADS, C // L3F_HEADS, S, m.k["scale_8"], mask="tiles")
        copied, multiplied, values_ready, turned, swapped, ready = (ph.sem(n) for n in (
            "copied", "multiplied", "values_ready", "qk_turned", "qk_swapped", "ready"))
        banks = m.banks
        both = lambda ap: ap.rearrange("p (a s) -> p a s", a=2)

        @ph.block.gpsimd
        def _(pool):
            opened(pool, a.head_ready)
            with pool.Fori(0, B) as b:
                pool.wait_ge(multiplied, b + 1)
                pool.tensor_copy(m.x_now[:, :], wide(m.h)[:, ds(b * S, S)]).then_inc(copied, 1)
                pool.wait_ge(ready, b + 1)
                attention_pool(pool, m, a, b)

        @ph.block.tensor
        def _(pe):
            opened(pe, a.scored, a.turned, a.weighed, multiplied)
            with pe.Fori(0, B) as b:
                pe.wait_ge(a.normed, a.count(b, 0))
                pe.wait_ge(copied, b + 1)
                for n, name in enumerate(("wq", "wk", "wqr", "wkr")):
                    pe.matmul(banks[:, n // 2, (n % 2) * S:(n % 2 + 1) * S], w[name], m.x_now[:, :], start=True,
                              stop=True)
                for t in range(QT):
                    last = pe.matmul(banks[:, 2, t * P:(t + 1) * P], m.x_now[:, t * P:(t + 1) * P], w["wv"],
                                     start=True, stop=True)
                last.then_inc(multiplied, 1)
                pe.wait_ge(ready, b + 1)
                pe.wait_ge(values_ready, b + 1)
                attention_pe(pe, m, a, b)

        @ph.block.scalar
        def _(act):
            opened(act, a.exped, a.high_copied)
            with act.Fori(0, B) as b:
                act.wait_ge(multiplied, b + 2)
                act.activation(m.v[:, 0:QT, 0:C], banks[:, 2, 0:QT * C].rearrange("p (t c) -> p t c", c=C),
                               ACT.Copy).then_inc(values_ready, 1)
                attention_act(act, m, a, b)

        @ph.block.vector
        def _(dve):
            opened(dve, a.topped, a.normed, a.low_copied, a.inverted)
            straight, crossed = both(m.prob[:, 0, 0:2 * S]), both(m.prob[:, 1, 0:2 * S])
            with dve.Fori(0, B) as b:
                dve.wait_ge(multiplied, b + 2)
                dve.tensor_tensor(straight, both(banks[:, 0, :]), row(m.k["l3f_cos"], 2), ALU.mult).then_inc(turned, 1)
                dve.tensor_tensor(crossed, both(banks[:, 1, :]), row(m.k["l3f_sin"], 2), ALU.mult).then_inc(swapped, 1)
                dve.wait_ge(turned, b + 1)
                dve.wait_ge(swapped, b + 1)
                dve.tensor_tensor(m.qT[:, 0, :], straight[:, 0], crossed[:, 0], ALU.add)
                dve.tensor_tensor(m.kT[:, 0, 0:S], straight[:, 1], crossed[:, 1], ALU.add).then_inc(ready, 1)
                attention_dve(dve, m, a, b,
                              lambda t, h: m.o[:, ds(b * QT + t, 1), ds(h * a.dh, a.dh)])


def l3_ffn(nc, m, w):
    prepare(nc, m, "L3f")
    place_mask_phase(nc, m, "L3f_mask", "causal")
    affine_phase(nc, m, "L3f_norm1", m.xn, m.o, w["g1_row"], w["b1_row"])
    conv_phase(nc, m, w)
    causal_phase(nc, m, w)
    xattn_finish(nc, m, "L3f", w, m.xn, bias=False)
    affine_phase(nc, m, "L3f_norm2", m.xn, m.o, w["g2_row"], w["b2_row"])
    route_phase(nc, m, "L3f", w["router"], L3F_EXPERTS, 1, softmax=False)
    cut = pieces(L3F_HID)

    def expert(e):
        at = 2 * L3F_HID * e
        gate = lambda i: w["wv2"][:, at + i * P:at + (i + 1) * P]
        value = lambda i: w["wv2"][:, at + L3F_HID + i * P:at + L3F_HID + (i + 1) * P]
        down = lambda i: w["down"][:, (e * len(cut) + i) * C:(e * len(cut) + i + 1) * C]
        return gate, value, down

    moe_phase(nc, m, "L3f_moe", m.xn, [expert(e) for e in range(L3F_EXPERTS)], [n for _, n in cut], ACT.Silu,
              list(range(L3F_EXPERTS)))
    add_phase(nc, m, "L3f_add")


def store_phase(nc, m, out):
    with Phase(nc, "store") as ph:
        stored = ph.sem("stored")

        @ph.block.sync
        def _(sp):
            sp.dma_start(out.rearrange("(t p) c -> p t c", p=P), m.x[:, :, :]).then_inc(stored, 16)
            sp.wait_ge(stored, 16)


def build(nc, x, ctxT, mask_f, mask_b, wx, wf, const, out):
    with ExitStack() as ctx:
        m = Memory(nc, ctx)
        load_phase(nc, m, x, ctxT, (mask_f, mask_b), wx, wf, const)
        k = m.k

        def weights_f(name):
            return m.fw[:, 0:width(FW[name])], wf[name]

        def weights_x(name):
            return m.xw[:, 0:width(XW[name])], wx[name]

        w = views(m.xw, XW["L0x"])
        prepare(nc, m, "L0x")
        cross_phase(nc, m, "L0x", w, L0_HEADS, k["scale_L0x"], with_q=True, fetch=weights_f("L0f"))
        l0_xattn_finish(nc, m, w)
        l0_ffn(nc, m, views(m.fw, FW["L0f"]), weights_x("L1x"))
        w = views(m.xw, XW["L1x"])
        prepare(nc, m, "L1x")
        key_mask_phase(nc, m, "L1x", mask_f, False)
        cross_phase(nc, m, "L1x", w, L1_HEADS, k["scale_8"], mask="keys", fetch=weights_f("L1f"))
        xattn_finish(nc, m, "L1x", w, m.x)
        w = views(m.fw, FW["L1f"])
        prepare(nc, m, "L1f")
        route_phase(nc, m, "L1f", w["router"], L1F_EXPERTS, 2, bias=w["rb_row"])
        moe_phase(nc, m, "L1f", m.x, [stacked(w, L1F_HID)(e) for e in range(1 + L1F_EXPERTS)],
                  [n for _, n in pieces(L1F_HID)], ACT.Silu, [None, *range(L1F_EXPERTS)],
                  fetch=weights_x("L2x"))
        w = views(m.xw, XW["L2x"])
        sel = m.sel[:, :, :]
        selT = m.kT[:, 4:8, :].rearrange("p c n -> p (c n)")
        prepare(nc, m, "L2x")
        select_phase(nc, m, w, sel, selT)
        chosen_phase(nc, m, w, sel, selT, weights_f("L2f"))
        chosen_finish(nc, m, w)
        w = views(m.fw, FW["L2f"])
        prepare(nc, m, "L2f")
        route_phase(nc, m, "L2f", w["router"], L2F_EXPERTS, 2, eps=1e-20)
        moe_phase(nc, m, "L2f", m.x, [stacked(w, L2F_HID)(e) for e in range(1 + L2F_EXPERTS)],
                  [n for _, n in pieces(L2F_HID)], ACT.Silu, [None, *range(L2F_EXPERTS)],
                  fetch=weights_x("L3x"))
        w = views(m.xw, XW["L3x"])
        prepare(nc, m, "L3x")
        key_mask_phase(nc, m, "L3x", mask_b, True)
        wide_cross_phase(nc, m, w, weights_f("L3f"))
        l3_ffn(nc, m, views(m.fw, FW["L3f"]))
        store_phase(nc, m, out)


def kernel(**inputs):
    import numpy as np
    import concourse.bacc as bacc
    from concourse import mybir as mb
    from concourse.bass_utils import run_bass_kernel_spmd

    a = {n: np.asarray(v) for n, v in inputs.items()}

    def rows(v):
        return np.broadcast_to(v.reshape(1, -1), (P, v.size))

    def tall(v):
        n = -(-v.shape[0] // P)
        v = np.concatenate([v, np.zeros((n * P - v.shape[0], v.shape[1]), v.dtype)])
        return v.reshape(n, P, -1).transpose(1, 0, 2).reshape(P, -1)

    def chunks(v):
        n = -(-v.size // P)
        return np.concatenate([v, np.zeros(n * P - v.size, v.dtype)]).reshape(n, P).T

    L0x = {n: a["L0_xattn_" + n] for n in ("Wq", "Wk", "Wv", "Wo", "bq", "bk", "bv", "bo", "g0", "b0", "g1", "b1")}
    L1x = {n: a["L1_xattn_" + n] for n in ("Wq", "Wk", "Wv", "Wo", "bq", "bk", "bv", "bo")}
    L2x = {n: a["L2_xattn_" + n] for n in ("router_w", "q_w", "kv_w", "out_w")}
    L3x = {n: a["L3_xattn_" + n] for n in ("Wq", "Wk", "Wv", "Wo", "bq", "bk", "bv", "bo")}
    L0f = {n: a["L0_ffn_" + n] for n in ("wqkv", "q_scale", "k_scale", "wo", "ln_g", "ln_b", "w1", "b1", "w2", "b2")}
    L1f = {n: a["L1_ffn_" + n] for n in ("sg", "su", "sd", "rg", "ru", "rd", "wr", "rb")}
    L2f = {n: a["L2_ffn_" + n] for n in ("Wr", "Wg", "Wu", "Wd", "Sg", "Su", "Sd")}
    L3f = {n: a["L3_ffn_" + n] for n in ("ln1_w", "ln1_b", "ln2_w", "ln2_b", "conv_w", "attn_w", "proj_w",
                                         "router_w", "expert_wv", "expert_proj")}
    packs = {
        "x_L0x": [L0x["Wq"].T, L0x["Wk"].T, L0x["Wv"].T, L0x["Wo"].T, chunks(L0x["bq"]), chunks(L0x["bk"]),
                  *(rows(L0x[n]) for n in ("bq", "bv", "bo", "g0", "b0", "g1", "b1"))],
        "x_L1x": [L1x["Wq"].T, L1x["Wk"].T, L1x["Wv"].T, L1x["Wo"].T, chunks(L1x["bq"]), chunks(L1x["bk"]),
                  rows(L1x["bv"]), rows(L1x["bo"])],
        "x_L2x": [L2x["q_w"].T, L2x["kv_w"][:C].T, L2x["kv_w"][C:].T, L2x["out_w"].T, rows(L2x["router_w"])],
        "x_L3x": [L3x["Wq"], L3x["Wk"], L3x["Wv"], tall(L3x["Wo"]), chunks(L3x["bq"]), chunks(L3x["bk"]),
                  rows(L3x["bv"]), rows(L3x["bo"])],
        "f_L1f": [*(L1f[s].T for s in ("sg",)), *(w.T for w in L1f["rg"]), L1f["su"].T, *(w.T for w in L1f["ru"]),
                  tall(L1f["sd"].T), *(tall(w.T) for w in L1f["rd"]), L1f["wr"].T, rows(L1f["rb"])],
        "f_L2f": [L2f["Sg"], *L2f["Wg"], L2f["Su"], *L2f["Wu"], tall(L2f["Sd"]), *(tall(w) for w in L2f["Wd"]),
                  L2f["Wr"]],
    }
    depth = []
    for d in (0, 1):
        b1 = L0f["b1"][d]
        depth += [L0f["wqkv"][d], tall(L0f["wo"][d]), L0f["w1"][d], tall(L0f["w2"][d]), rows(L0f["q_scale"][d]),
                  rows(L0f["k_scale"][d]), chunks(L0f["ln_g"][d]), chunks(L0f["ln_b"][d]),
                  chunks(b1[:L0F_HID]), chunks(b1[L0F_HID:]), rows(L0f["b2"][d])]
    packs["f_L0f"] = depth
    hd = C // L3F_HEADS
    swap = np.arange(C).reshape(L3F_HEADS, 2, hd // 2)[:, ::-1].reshape(-1)
    wq, wk, wv = np.split(L3f["attn_w"], 3, axis=1)
    packs["f_L3f"] = [*L3f["expert_wv"], *(tall(w) for w in L3f["expert_proj"]), wq, wq[:, swap], wk, wk[:, swap],
                      wv, L3f["proj_w"], L3f["conv_w"].reshape(C, 3), rows(L3f["ln1_w"]), rows(L3f["ln1_b"]),
                      rows(L3f["ln2_w"]), rows(L3f["ln2_b"]), L3f["router_w"]]

    f = np.float32
    part = np.arange(P)
    head_rows = lambda n, s: (part[:, None] // (P // n) == np.arange(n)[None]) * f(s)
    place = np.arange(S)
    q_at, k_at = place[:, None], place[None, :]
    tile2 = lambda t: t.reshape(QT, P, -1).transpose(1, 0, 2).reshape(P, -1)
    masked = f(-1e30)
    freq4 = np.exp(np.linspace(0.0, -1.0, 4, dtype=f) * np.log(f(10000.0))).astype(f)

    def l2_rope(n):
        angle = np.arange(n, dtype=f)[:, None] * freq4
        return np.tile(np.concatenate([np.sin(angle), np.cos(angle)], axis=-1), (1, L2_HEADS))

    inv = (f(1.0) / f(10000.0) ** (np.arange(0, hd, 2, dtype=f) / f(hd))).astype(f)
    ang = place.astype(f)[:, None] * inv
    l3_cos = np.tile(np.cos(ang), (1, 2 * L3F_HEADS)).T
    l3_sin = np.tile(np.concatenate([-np.sin(ang), np.sin(ang)], axis=-1), (1, L3F_HEADS)).T
    half = np.arange(0, WIDE, 2, dtype=f)
    ang = place.astype(f)[:, None] * (f(1.0) / f(10000.0) ** (half / f(WIDE)))[None]
    base = (half + f(0.4 * WIDE)) / f(1.4 * WIDE)
    grow = base[None] ** ((place - S // 2).astype(f) / f(32.0))[:, None]
    both = lambda t: np.concatenate([t, t], axis=-1)
    signed = lambda t: np.concatenate([-t, t], axis=-1)
    consts = [np.eye(P), head_rows(L0_HEADS, 1 / np.sqrt(f(C))), head_rows(L1_HEADS, 1 / np.sqrt(f(8))),
              np.tile(head_rows(2, 1 / 8.0), (1, CHUNKS_L3)), np.tile(head_rows(2, 8.0), (1, CHUNKS_L0F)),
              rows((np.arange(8)[None] < np.arange(8)[:, None]).astype(f)),
              tile2(np.where(k_at <= q_at, f(0), masked)),
              tile2(np.where((k_at <= q_at) & (k_at >= q_at - 64), f(0), masked)),
              tile2(l2_rope(S)), l2_rope(SK).T, l3_cos, l3_sin,
              tile2(both(np.cos(ang) * grow)), tile2(signed(np.sin(ang) * grow)),
              tile2(both(np.cos(ang) / grow)), tile2(signed(np.sin(ang) / grow)), rows(np.arange(L2_CAP)),
              tile2((k_at < q_at).astype(f))]

    arrays = {n: np.ascontiguousarray(np.concatenate(p, axis=1)) for n, p in packs.items()}
    arrays["const"] = np.ascontiguousarray(np.concatenate(consts, axis=1).astype(f))
    arrays["x"] = np.ascontiguousarray(a["x"].reshape(TOK, C))
    arrays["ctxT"] = np.ascontiguousarray(a["ctx_1024"].reshape(B * SK, C).T)
    arrays["mask_f"] = np.ascontiguousarray(a["mask_BxS2_ff1"].reshape(1, B * SK))
    arrays["mask_b"] = np.ascontiguousarray(a["mask_BxS2_bf1"].reshape(1, B * SK)).view(np.uint8)

    nc = bacc.Bacc("TRN2", target_bir_lowering=False, num_devices=1)
    d = {n: nc.dram_tensor("in_" + n, v.shape, mb.dt.from_np(v.dtype), kind="ExternalInput").ap() for n, v in arrays.items()}
    out = nc.dram_tensor("out_0", (TOK, C), mb.dt.float32, kind="ExternalOutput").ap()
    build(nc, d["x"], d["ctxT"], d["mask_f"], d["mask_b"], {n[2:]: d[n] for n in d if n.startswith("x_")},
          {n[2:]: d[n] for n in d if n.startswith("f_")}, d["const"], out)
    got = run_bass_kernel_spmd(nc, [{"in_" + n: v for n, v in arrays.items()}], core_ids=[0]).results[0]["out_0"]
    return got.reshape(B, S, C)
```

```python
from contextlib import ExitStack

import concourse.bass as bass
from concourse import mybir

ds = bass.ds
F32 = mybir.dt.float32
BF16 = mybir.dt.bfloat16
U8 = mybir.dt.uint8
ALU = mybir.AluOpType
ACT = mybir.ActivationFunctionType
AX_X = mybir.AxisListType.X

P = 128
B = 8
S = 256
SK = 512
C = 128
TOK = B * S
TILES = TOK // P
QT = S // P
KT = SK // P
GROUP = 512
GROUPS = TOK // GROUP
GT = GROUP // P

L0_HEADS, L0F_HEADS, L1_HEADS, L2_HEADS, L3_HEADS, L3F_HEADS = 8, 8, 16, 16, 16, 16
WIDE = 64
L0F_HID = 341
L1F_EXPERTS, L1F_HID = 7, 352
L2F_EXPERTS, L2F_HID = 8, 256
L3F_EXPERTS, L3F_HID = 4, 512
L2_CAP = 64
CHUNKS_L3 = L3_HEADS * WIDE // P
CHUNKS_L0F = L0F_HEADS * WIDE // P


def pieces(n):
    return [(a, min(P, n - a)) for a in range(0, n, P)]


XW = {
    "L0x": [("wq", C), ("wq_plain", C), ("wk", C), ("wv", C), ("wo", C), ("bq", 1), ("bk", 1), ("bq_row", C), ("bv_row", C),
            ("bo_row", C), ("g0_row", C), ("b0_row", C), ("g1_row", C), ("b1_row", C)],
    "L1x": [("wq", C), ("wk", C), ("wv", C), ("wo", C), ("bq", 1), ("bk", 1), ("bv_row", C), ("bo_row", C)],
    "L2x": [("wq", C), ("wk", C), ("wv", C), ("wo", C), ("router_row", C), ("l2_ropeq", QT * C),
            ("l2_ropek", SK), ("slot", L2_CAP), ("earlier", QT * S)],
    "L3x": [("wq", CHUNKS_L3 * C), ("wk", CHUNKS_L3 * C), ("wv", CHUNKS_L3 * C), ("wo", CHUNKS_L3 * C),
            ("bq", CHUNKS_L3), ("bk", CHUNKS_L3), ("bv_row", CHUNKS_L3 * C), ("bo_row", C), ("scale", L3_HEADS)],
}
FW = {
    "L0f": [(n + str(d), c) for d in (0, 1) for n, c in (
        ("wqkv", 3 * CHUNKS_L0F * C), ("wo", CHUNKS_L0F * C), ("w1", 2 * L0F_HID), ("w2", 3 * C), ("qs_row", WIDE),
        ("ks_row", WIDE), ("g", 1), ("b", 1), ("b1", 6), ("b2_row", C))]
           + [("scale", L0F_HEADS), ("band", QT * S), ("xq_cos", QT * WIDE), ("xq_sin", QT * WIDE),
              ("xk_cos", QT * WIDE), ("xk_sin", QT * WIDE)],
    "L1f": [("gate", 8 * L1F_HID), ("up", 8 * L1F_HID), ("down", 8 * 3 * C), ("router", L1F_EXPERTS),
            ("rb_row", L1F_EXPERTS)],
    "L2f": [("gate", 9 * L2F_HID), ("up", 9 * L2F_HID), ("down", 9 * 2 * C), ("router", L2F_EXPERTS)],
    "L3f": [("wv2", L3F_EXPERTS * 2 * L3F_HID), ("down", L3F_EXPERTS * 4 * C), ("wq", C), ("wqr", C), ("wk", C),
            ("wkr", C), ("wv", C), ("wo", C), ("conv", 3), ("g1_row", C), ("b1_row", C), ("g2_row", C),
            ("b2_row", C), ("router", L3F_EXPERTS), ("causal", QT * S), ("l3f_cos", 2 * S), ("l3f_sin", 2 * S)],
}
CW = [("ident", P), ("before", 64)]


def width(table):
    return sum(n for _, n in table)


def views(tile, table):
    out, at = {}, 0
    for name, n in table:
        out[name] = tile[:, at:at + n]
        at += n
    return out


def row(ap, *counts):
    for at, n in enumerate(counts):
        ap = ap.unsqueeze(1)
    return ap.broadcast_to([P, *counts, ap.shape[-1]])


def each(ap, n):
    return ap.unsqueeze(len(ap.shape)).broadcast_to([*ap.shape, n])


class Steps:

    def __init__(self, eng, sem, base=0):
        self.eng, self.sem, self.base, self.n = eng, sem, base, 0

    def done(self, ins):
        ins.then_inc(self.sem, 1)
        self.n += 1
        self.eng.wait_ge(self.sem, self.base + self.n)


class Memory:

    def __init__(self, nc, ctx):
        def sb(name, shape, dt=F32):
            return ctx.enter_context(nc.sbuf_tensor(name, shape, dt))

        def ps(name, shape):
            return ctx.enter_context(nc.psum_tensor(name, shape, F32))

        self.x = sb("x", [P, TILES, C])
        self.xn = sb("xn", [P, TILES, C])
        self.h = sb("h", [P, TILES, C])
        self.o = sb("o", [P, TILES, C])
        self.hT = sb("hT", [P, TOK])
        self.ctxT = sb("ctxT", [P, B * SK])
        self.const = sb("const", [P, width(CW)])
        self.k = views(self.const, CW)
        self.xw = sb("xw", [P, max(width(t) for t in XW.values())])
        self.fw = sb("fw", [P, max(width(t) for t in FW.values())])
        self.sum = sb("row_sum", [P, TILES])
        self.stats = sb("row_stats", [P, TILES, 6])
        self.moments = sb("row_moments", [P, TILES, 2])
        self.offset = sb("row_offset", [P, TILES])
        self.var = sb("row_var", [P, TILES])
        self.std = sb("row_std", [P, TILES])
        self.rstd = sb("row_rstd", [P, TILES])
        self.qT = sb("qT", [P, CHUNKS_L3, S])
        self.kT = sb("kT", [P, CHUNKS_L3, SK])
        self.v = sb("v", [P, KT, L3_HEADS * WIDE])
        self.ctx_now = sb("ctx_now", [P, SK])
        self.x_now = sb("x_now", [P, S])
        self.q_head = sb("q_head", [P, 4, S])
        self.prob = sb("prob", [P, 2, 2 * SK])
        self.probT = sb("probT", [P, 2, KT, S])
        self.top = sb("top", [P, 2, 2])
        self.total = sb("total", [P, 16, 2])
        self.inverse = sb("inverse", [P, 16, 2])
        self.sel = sb("sel", [P, TILES, L2_CAP])
        self.ones = sb("ones", [P, P])
        self.o_now = sb("o_now", [P, C])
        self.scores16 = sb("scores16", [P, TILES, 8])
        self.weight = sb("weight", [P, TILES, 8])
        self.rank = sb("rank", [P, TILES, 8])
        self.norm = sb("norm", [P, 4, L0F_HEADS])
        self.inv_norm = sb("inv_norm", [P, 4, L0F_HEADS])
        self.turn_cos = sb("turn_cos", [P, 4, WIDE])
        self.turn_sin = sb("turn_sin", [P, 4, WIDE])
        self.own = sb("own", [P, TILES])
        self.route = sb("route", [P, TILES])
        self.mask_in = sb("mask_in", [P, B * SK // P])
        self.mask_u8 = sb("mask_u8", [P, B * SK // P], U8)
        self.mask_part = sb("mask_part", [P, 3, B * SK // P], BF16)
        self.mask_rest = sb("mask_rest", [P, 3, B * SK // P])
        q = self.qT[:, :, :].rearrange("p c n -> p (c n)")
        self.qk = q[:, 0:SK + S]
        self.qk_rest = q[:, SK + S:2 * (SK + S)]
        self.qk_part = sb("qk_part", [P, 3, SK + S], BF16)
        self.v_narrow = sb("v_narrow", [P, 2, KT, C])
        self.kS = self.kT[:, :, :].rearrange("p c n -> p (c n)").bitcast(BF16).rearrange(
            "p (two c n) -> p two c n", two=2, n=SK)
        self.qS = self.v[:, :, :].rearrange("p c n -> p (c n)").bitcast(BF16).rearrange(
            "p (two h n) -> p two h n", two=2, n=S)
        self.identb = sb("identb", [P, P], BF16)
        self.onesb = sb("onesb", [P, P], BF16)
        self.bandb = self.ctx_now[:, 0:QT * S // 2].bitcast(BF16).rearrange("p (t k) -> p t k", t=QT)
        self.key_mask = sb("key_mask", [P, B * SK], BF16)
        self.pS = ps("pS", [P, 2, 1024])
        self.pT = ps("pT", [P, 2, 512])
        self.pO = ps("pO", [P, 2, 2, P])
        self.pG = ps("pG", [P, 512])
        self.banks = self.pS[:, :, :].rearrange("p a (b n) -> p (a b) n", b=2)


class Phase:

    def __init__(self, nc, name):
        self.nc, self.name, self.sems = nc, name, []
        self.stack = ExitStack()

    def sem(self, name):
        s = self.nc.alloc_semaphore(f"{self.name}_{name}")
        self.sems.append(s)
        return s

    def __enter__(self):
        self.block = self.stack.enter_context(self.nc.Block(f"{self.name}_block"))
        return self

    def __exit__(self, *e):
        self.stack.close()
        if e[0] is None:
            self.nc.clear_and_free_semaphores(self.sems)
            self.nc.all_engine_barrier()


def wide(ap):
    return ap[:, :, :].rearrange("p t c -> p (t c)")


class Normalization:

    def __init__(self, ph):
        self.measured = ph.sem("measured")
        self.varied = ph.sem("varied")
        self.rooted = ph.sem("rooted")
        self.inverted = ph.sem("inverted")
        self.placed = ph.sem("placed")
        self.low = ph.sem("low_tiles")
        self.high = ph.sem("high_tiles")

    def act(self, act, m, n, src, dst):
        act.wait_ge(self.varied, n)
        act.activation(m.std[:, :], m.var[:, :], ACT.Sqrt).then_inc(self.rooted, 1)
        act.wait_ge(self.placed, n)
        for t in range(8, TILES):
            last = act.activation(dst[:, t, :], src[:, t, :], ACT.Identity, scale=m.rstd[:, t:t + 1],
                                  bias=m.offset[:, t:t + 1])
            if t % 4 == 3:
                last.then_inc(self.high, 1)

    def dve(self, dve, m, n, src, dst, eps):
        for t in range(TILES):
            last = dve.bn_stats(m.stats[:, t, :], src[:, t, :])
        last.then_inc(self.measured, 1)
        dve.wait_ge(self.measured, 2 * n - 1)
        for t in range(TILES):
            last = dve.bn_aggr(m.moments[:, t, :], m.stats[:, t, :])
        last.then_inc(self.measured, 1)
        dve.wait_ge(self.measured, 2 * n)
        dve.tensor_scalar(m.var[:, :], m.moments[:, :, 1], eps, None, ALU.add).then_inc(self.varied, 1)
        dve.wait_ge(self.rooted, n)
        dve.reciprocal(m.rstd[:, :], m.std[:, :]).then_inc(self.inverted, 1)
        dve.wait_ge(self.inverted, n)
        dve.scalar_tensor_tensor(out=m.offset[:, :], in0=m.moments[:, :, 0], scalar=-1.0, in1=m.rstd[:, :],
                                 op0=ALU.mult, op1=ALU.mult).then_inc(self.placed, 1)
        for t in range(8):
            last = dve.tensor_scalar(dst[:, t, :], src[:, t, :], m.moments[:, t, 0:1], m.rstd[:, t:t + 1],
                                     ALU.subtract, ALU.mult)
            if t % 4 == 3:
                last.then_inc(self.low, 1)

    def wait(self, eng, n):
        eng.wait_ge(self.low, 2 * n)
        eng.wait_ge(self.high, 2 * n)

    def scale_dve(self, dve, m, n, steps, dst, scale, shift):
        self.wait(dve, n)
        steps.done(dve.tensor_tensor(dst, dst, row(scale, TILES), ALU.mult))
        steps.done(dve.tensor_tensor(dst, dst, row(shift, TILES), ALU.add))


def turn_pe(pe, m, src, turned, rows=P):
    for g in range(4):
        for t in range(4):
            last = pe.transpose(m.banks[0:rows, g, t * P:(t + 1) * P], src[:, 4 * g + t, :], m.k["ident"])
        last.then_inc(turned, 1)


def turn_out_act(act, m, dst, turned, copied, rows=P):
    for g in (0, 2):
        act.wait_ge(turned, g + 1)
        act.activation(dst[0:rows, g * 512:(g + 1) * 512], m.banks[0:rows, g, :], ACT.Copy).then_inc(copied, 1)


def turn_out_dve(dve, m, dst, turned, copied, rows=P):
    for g in (1, 3):
        dve.wait_ge(turned, g + 1)
        dve.tensor_copy(dst[0:rows, g * 512:(g + 1) * 512], m.banks[0:rows, g, :]).then_inc(copied, 1)


def load_phase(nc, m, x, ctxT, masks, wx, wf, const):
    mask_f, mask_b = masks
    with Phase(nc, "load") as ph:
        loaded = ph.sem("loaded")
        steps_dve = ph.sem("steps")

        @ph.block.sync
        def _(sp):
            sp.dma_start(m.x[:, :, :], x.rearrange("(t p) c -> p t c", p=P)).then_inc(loaded, 16)
            sp.dma_start(m.const[:, :], const).then_inc(loaded, 16)
            sp.dma_start(m.xw[:, 0:width(XW["L0x"])], wx["L0x"]).then_inc(loaded, 16)
            sp.dma_start(m.ctxT[:, :], ctxT).then_inc(loaded, 16)
            sp.wait_ge(loaded, 64)

        @ph.block.vector
        def _(dve):
            steps = Steps(dve, steps_dve)
            dve.memset(m.onesb[:, :], 1.0)
            dve.memset(m.ones[:, :], 1.0)
            dve.memset(m.key_mask[:, :], 0.0)
            dve.wait_ge(loaded, 64)
            steps.done(dve.tensor_copy(m.identb[:, :], m.k["ident"]))


def fetch_sync(ph, fetch):
    if fetch is None:
        return
    fetched = ph.sem("fetched")

    @ph.block.sync
    def _(sp):
        sp.dma_start(*fetch).then_inc(fetched, 16)
        sp.wait_ge(fetched, 16)


def clear_stacks(pool, m):
    pool.memset(m.kS, 0.0)
    pool.memset(m.qS, 0.0)


def prepare(nc, m, name, clear=False):
    with Phase(nc, name + "_prepare") as ph:
        norm = Normalization(ph)
        turned, copied = ph.sem("turned"), ph.sem("copied")

        if clear:
            @ph.block.gpsimd
            def _(pool):
                clear_stacks(pool, m)

        @ph.block.vector
        def _(dve):
            norm.dve(dve, m, 1, m.x, m.xn, 1e-5)
            for n, g in ((3, 1), (4, 3)):
                dve.wait_ge(turned, n)
                dve.tensor_copy(m.hT[:, g * 512:(g + 1) * 512], m.banks[:, g, :]).then_inc(copied, 1)

        @ph.block.scalar
        def _(act):
            norm.act(act, m, 1, m.x, m.xn)
            for n, g in ((1, 0), (2, 2)):
                act.wait_ge(turned, n)
                act.activation(m.hT[:, g * 512:(g + 1) * 512], m.banks[:, g, :], ACT.Copy).then_inc(copied, 1)

        @ph.block.tensor
        def _(pe):
            for g in (0, 2, 1, 3):
                pe.wait_ge(norm.low if g < 2 else norm.high, g % 2 + 1)
                for t in range(4):
                    last = pe.transpose(m.banks[:, g, t * P:(t + 1) * P], m.xn[:, 4 * g + t, :], m.k["ident"])
                last.then_inc(turned, 1)


class Attention:

    def __init__(self, ph, heads, width_, keys, scale=None, q_rows=P, tiles=QT, mask=None):
        self.H, self.dh, self.NK, self.KC, self.scale = heads, width_, keys, keys // P, scale
        self.rows, self.T, self.mask = q_rows, tiles, mask
        self.paired = width_ == WIDE
        self.one_bank = self.paired and keys == S
        self.queries = self.keys = self.values = None
        self.head_ready = ph.sem("head_ready")
        self.scored = ph.sem("scored")
        self.topped = ph.sem("topped")
        self.exped = ph.sem("exped")
        self.turned = ph.sem("turned")
        self.low_copied = ph.sem("low_copied")
        self.high_copied = ph.sem("high_copied")
        self.weighed = ph.sem("weighed")
        self.inverted = ph.sem("inverted")
        self.normed = ph.sem("normed")

    def count(self, b, n, previous=None):
        if isinstance(n, int) and previous is None:
            n = max(n, 0)
        return b * self.H + (n + 1)

    def one_batch(self, eng, slot, b):
        for i in range(4):
            slot(b, i, i % 4, i // 2, None)
        self.others(eng, slot, b)
        for i in range(self.H, self.H + 3):
            slot(b, i, i % 4, i // 2, None)

    def others(self, eng, slot, b):
        with eng.Fori(1, self.H // 4) as r:
            for s in range(4):
                slot(b, 4 * r + s, s, 2 * r + s // 2, None)

    def all_batches(self, eng, slot, ready=None, after=None, end=None):
        def batch(b, previous):
            if ready is not None:
                ready(b)
            for i in range(self.H if self.H == 8 else 4):
                slot(b, i, i % 4, i // 2, previous)
                if after is not None:
                    after(b, i, previous)
            if self.H > 8:
                self.others(eng, slot, b)

        batch(0, None)
        with eng.Fori(0, B - 1) as b:
            batch(b + 1, b)
        for i in range(self.H, self.H + 3):
            slot(B - 1, i, i % 4, i // 2, None)
        if end is not None:
            end()

    def has(self, i, back, previous):
        return not isinstance(i, int) or (i - back < self.H and (i >= back or previous is not None))

    def head(self, b, i, back, previous):
        return (previous, i - back + self.H) if isinstance(i, int) and i < back else (b, i - back)


def opened(eng, *sems, by=1):
    for s in sems:
        eng.sem_inc(s, by)


def queries_slot(pool, m, a):
    nq = a.T * a.rows

    def slot(b, i, s, j, previous):
        if s % 2 == 0 and a.has(i, 0, previous):
            pool.wait_ge(a.scored, a.count(b, i - 2, previous))
            pool.tensor_tensor(m.q_head[:, s:s + 2, 0:nq], a.queries(b, j).broadcast_to([P, 2, nq]),
                               each(a.scale[:, 0:2], nq), ALU.mult).then_inc(a.head_ready, 2)

    return slot


TERMS = ((0, 0), (0, 1), (0, 2), (1, 0), (1, 1), (2, 0))


def stack_sync(sp, m, a, b, two, part_ready, stacked, with_mask):
    per = 2 if a.dh == 8 else 1
    rows, chunks = C // per, a.H // per
    nq = a.T * a.rows
    sp.wait_ge(part_ready, b + 1)
    for s in range(per):
        for n, (qp, kp) in enumerate(TERMS):
            at = s * (P // per) + n * a.dh
            src = m.qk_part[s * rows:(s + 1) * rows, kp, 0:a.NK]
            sp.dma_start(m.kS[at:at + a.dh, two, 0:chunks, 0:a.NK],
                         src).then_inc(stacked, 16)
            src = m.qk_part[s * rows:(s + 1) * rows, qp, a.NK:a.NK + nq]
            sp.dma_start(m.qS[at:at + a.dh, two, s:a.H:per, 0:nq], src).then_inc(stacked, 16)
        if with_mask:
            at = s * (P // per) + len(TERMS) * a.dh
            dst = m.kS[at:at + 3, two, 0:chunks, 0:a.NK]
            src = m.key_mask[0:3, ds(batch_of(b) * SK, SK)].unsqueeze(1).broadcast_to([3, chunks, SK])
            sp.dma_start(dst, src).then_inc(stacked, 16)


def split_pool(pool, m, n, steps, part_ready):
    x, rest, part = m.qk[:, 0:n], m.qk_rest[:, 0:n], m.qk_part[:, :, 0:n]
    one = m.ones[:, 0:1].broadcast_to([P, n])
    steps.done(pool.tensor_tensor(part[:, 0, :], x, one, ALU.mult))
    steps.done(pool.tensor_tensor(rest, x, part[:, 0, :], ALU.subtract))
    steps.done(pool.tensor_tensor(part[:, 1, :], rest, one, ALU.mult))
    pool.tensor_tensor(part[:, 2, :], rest, part[:, 1, :], ALU.subtract).then_inc(part_ready, 1)


def batch_of(b):
    return b % B


def attention_pe(pe, m, a):
    rows = a.rows

    def stacked_scores(b, i, s, j, previous):
        pe.wait_ge(a.exped, a.count(b, i - 1, previous))
        two = b & 1
        chunk = j if a.dh == 8 else i
        k = m.kS[:, ds(two, 1), ds(chunk, 1), 0:a.NK]
        for t in range(a.T):
            out = m.pS[:, s:s + 1, t * a.NK:(t + 1) * a.NK]
            if a.mask == "tiles":
                pe.matmul(out, m.identb[:, :], m.bandb[:, t, :], start=True, stop=False)
            last = pe.matmul(out, m.qS[:, ds(two, 1), ds(i, 1), t * P:(t + 1) * P], k, start=a.mask != "tiles",
                             stop=True)
        last.then_inc(a.scored, 1)

    def scores(b, i, s, j, q, previous):
        pe.wait_ge(a.head_ready, a.count(b, i + 1, previous))
        pe.wait_ge(a.exped, a.count(b, i - 1, previous))
        k = a.keys(b, j)
        for t in range(a.T):
            out = m.pS[:, s:s + 1, t * a.NK:(t + 1) * a.NK]
            if a.mask == "keys":
                pe.matmul(out, m.onesb[:, :], m.key_mask[:, ds(b * SK, SK)], start=True, stop=False)
            if a.mask == "tiles":
                pe.matmul(out, m.identb[:, :], m.bandb[:, t, :], start=True, stop=False)
            last = pe.matmul(out, m.q_head[:, q, t * P:t * P + rows], k, start=a.mask is None, stop=True)
        last.then_inc(a.scored, 1)

    def weigh(b, i, s, batch, head, previous):
        if not a.one_bank:
            pe.wait_ge(a.low_copied, a.count(b, i - 2, previous))
        pe.wait_ge(a.high_copied, a.count(b, i - 2, previous))
        pe.wait_ge(a.normed, a.count(b, i - 3, previous))
        for t in range(a.T):
            for c in range(a.KC):
                v = (a.values(batch, c, head) if a.paired
                     else m.v_narrow[:, ds(batch & 1, 1), c, ds(head * a.dh, a.dh)])
                last = pe.matmul(m.pO[0:rows, s, t, 0:a.dh], m.probT[:, s, c, t * P:t * P + rows], v, start=c == 0,
                                 stop=c == a.KC - 1)
        last.then_inc(a.weighed, 1)

    def turn(b, i, s, previous):
        pe.wait_ge(a.exped, a.count(b, i, previous))
        if not a.one_bank:
            pe.wait_ge(a.low_copied, a.count(b, i - 1, previous))
        pe.wait_ge(a.high_copied, a.count(b, i - 1, previous))
        half = a.KC // 2
        for c in range(a.KC):
            for t in range(a.T):
                bank, c_ = (0, c) if a.one_bank else (c // half, c % half)
                at = (c_ * a.T + t) * P
                last = pe.transpose(m.pT[:, bank, at:at + P],
                                    m.prob[:, s, t * a.NK + c * P:t * a.NK + (c + 1) * P], m.k["ident"])
        last.then_inc(a.turned, 1)

    def slot(b, i, place, j, previous):
        s = place % 2
        if a.has(i, 0, previous):
            scores(b, i, s, j, place, previous) if a.paired else stacked_scores(b, i, s, j, previous)
        if a.has(i, 3, previous):
            weigh(b, i, 1 - s, *a.head(b, i, 3, previous), previous)
        if a.has(i, 1, previous):
            turn(b, i, 1 - s, previous)

    return slot


def turned_half(m, a, s, half):
    nq, n = a.T * a.rows, a.KC // 2
    if a.one_bank:
        return m.probT[:, s, 0:a.KC, 0:nq], m.pT[:, 0, :].rearrange("p (c q) -> p c q", q=nq)
    return (m.probT[:, s, half * n:(half + 1) * n, 0:nq],
            m.pT[:, half, 0:n * a.T * P].rearrange("p (c q) -> p c q", q=a.T * P)[:, :, 0:nq])


def attention_act(act, m, a):

    def slot(b, i, place, j, previous):
        s = place % 2
        if a.has(i, 0, previous):
            act.wait_ge(a.topped, a.count(b, i + 1, previous))
            act.wait_ge(a.turned, a.count(b, i - 1, previous))
            for t in range(a.T):
                last = act.activation(m.prob[0:a.rows, s, t * a.NK:(t + 1) * a.NK],
                                      m.pS[0:a.rows, s, t * a.NK:(t + 1) * a.NK], ACT.Exp,
                                      bias=m.top[0:a.rows, s, t:t + 1],
                                      accum_out=m.total[0:a.rows, ds(i, 1), t:t + 1])
            last.then_inc(a.exped, 1)
        if a.has(i, 1, previous):
            act.wait_ge(a.turned, a.count(b, i, previous))
            act.wait_ge(a.weighed, a.count(b, i - 2, previous))
            dst, src = turned_half(m, a, 1 - s, 1)
            act.activation(dst, src, ACT.Copy).then_inc(a.high_copied, 1)

    return slot


def attention_dve(dve, m, a, out):

    def slot(b, i, place, j, previous):
        s = place % 2
        if a.has(i, 0, previous):
            dve.wait_ge(a.scored, a.count(b, i + 1, previous))
            dve.tensor_reduce(m.top[0:a.rows, s, 0:a.T],
                              m.pS[0:a.rows, s, 0:a.T * a.NK].rearrange("p (t k) -> p t k", k=a.NK),
                              AX_X, ALU.max, negate=True).then_inc(a.topped, 1)
        if a.has(i, 3, previous):
            batch, head = a.head(b, i, 3, previous)
            dve.wait_ge(a.weighed, a.count(b, i - 2, previous))
            dve.wait_ge(a.inverted, a.count(b, i - 2, previous))
            for t in range(a.T):
                last = dve.tensor_scalar(out(batch, t, head), m.pO[0:a.rows, 1 - s, t, 0:a.dh],
                                         m.inverse[0:a.rows, ds(head, 1), t:t + 1], None, ALU.mult)
            last.then_inc(a.normed, 1)
        if a.has(i, 1, previous):
            _, head = a.head(b, i, 1, previous)
            dve.wait_ge(a.turned, a.count(b, i, previous))
            dve.reciprocal(m.inverse[0:a.rows, ds(head, 1), 0:a.T],
                           m.total[0:a.rows, ds(head, 1), 0:a.T]).then_inc(a.inverted, 1)
            if not a.one_bank:
                dve.wait_ge(a.weighed, a.count(b, i - 2, previous))
                dst, src = turned_half(m, a, 1 - s, 0)
                dve.tensor_copy(dst, src).then_inc(a.low_copied, 1)

    return slot


class Preparation:

    PIECES = 3

    def __init__(self, ph, a, columns):
        self.a, self.columns = a, columns
        self.copied = ph.sem("copied")
        self.made = ph.sem("piece_made")
        self.taken = ph.sem("piece_taken")
        self.part_ready = ph.sem("part_ready")
        self.pool_steps = ph.sem("pool_steps")
        self.stacked = ph.sem("stacked")
        self.masked = False

    def per_batch(self):
        per = 2 if self.a.dh == 8 else 1
        return 16 * per * (2 * len(TERMS) + (1 if self.masked else 0))

    def first(self, piece):
        for n in range(self.PIECES):
            piece(n, 0)

    def after(self, piece, finish=None):
        def work(b, i, previous):
            if i < self.PIECES:
                piece(i, b + 1)
            if i == 2 and finish is not None and previous is not None:
                finish(previous)
        return work


def narrow_pool(pool, m, a, p, sources):
    opened(pool, p.copied)

    def prepare_batch(b):
        for dst, src, n in sources:
            last = pool.tensor_copy(dst, src[:, ds(batch_of(b) * n, n)])
        last.then_inc(p.copied, 1)
        pool.wait_ge(p.taken, 3 * b + 3)
        split_pool(pool, m, p.columns, Steps(pool, p.pool_steps, base=3 * b), p.part_ready)

    prepare_batch(0)
    with pool.Fori(0, B) as b:
        pool.wait_ge(p.made, 3 * b + 3)
        prepare_batch(b + 1)


def narrow_sync(sp, m, a, p):
    extra = 0
    if p.masked:
        for two in range(2):
            for s in range(2):
                at = s * 64 + len(TERMS) * a.dh
                for t in range(a.T):
                    sp.dma_start(m.qS[at:at + 3, two, s:a.H:2, t * P:(t + 1) * P],
                                 row(m.onesb[:, :], a.H // 2)[0:3]).then_inc(p.stacked, 16)
                    extra += 16
    stack_sync(sp, m, a, 0, 0, p.part_ready, p.stacked, p.masked)
    with sp.Fori(0, B // 2) as pair:
        stack_sync(sp, m, a, 2 * pair + 1, 1, p.part_ready, p.stacked, p.masked)
        stack_sync(sp, m, a, 2 * pair + 2, 0, p.part_ready, p.stacked, p.masked)
    sp.wait_ge(p.stacked, extra + (B + 1) * p.per_batch())


def narrow_pe(pe, m, a, p, piece, finish=None):
    opened(pe, a.scored, a.turned, a.weighed)
    extra = 16 * 4 * a.T if p.masked else 0

    def ready(b):
        pe.wait_ge(p.stacked, (b + 1) * p.per_batch() + extra)
        pe.wait_ge(p.taken, 3 * b + 4)

    p.first(piece)
    a.all_batches(pe, attention_pe(pe, m, a), ready, p.after(piece, finish),
                  None if finish is None else lambda: finish(B - 1))


def cross_phase(nc, m, name, w, heads, with_q=False, mask=False, fetch=None):
    scale = 1.0 / float(C if with_q else C // heads) ** 0.5
    with Phase(nc, name) as ph:
        a = Attention(ph, heads, C // heads, SK)
        p = Preparation(ph, a, SK + S)
        p.masked = mask
        G, fetched = m.pG, None if fetch is None else ph.sem("fetched")

        @ph.block.sync
        def _(sp):
            narrow_sync(sp, m, a, p)

        @ph.block.gpsimd
        def _(pool):
            if fetch is not None:
                pool.dma_start(*fetch).then_inc(fetched, 16)
            narrow_pool(pool, m, a, p, ((m.ctx_now[:, :], m.ctxT, SK), (m.x_now[:, :], m.hT, S)))
            if fetch is not None:
                pool.wait_ge(fetched, 16)

        @ph.block.tensor
        def _(pe):
            def piece(n, b):
                pe.wait_ge(p.taken, 3 * b + n + 1)
                if n == 0:
                    last = pe.matmul(G[:, :], w["wk"], m.ctxT[:, ds(batch_of(b) * SK, SK)], start=True, stop=True)
                if n == 1:
                    last = pe.matmul(G[:, 0:S], w["wq"], m.hT[:, ds(batch_of(b) * S, S)], start=True, stop=True)
                    pe.wait_ge(p.copied, b + 2)
                    if with_q:
                        for t in range(QT):
                            last = pe.matmul(G[:, S + t * P:S + (t + 1) * P], m.x_now[:, t * P:(t + 1) * P],
                                             w["wq_plain"], start=True, stop=True)
                if n == 2:
                    for t in range(KT):
                        last = pe.matmul(G[:, t * P:(t + 1) * P], m.ctx_now[:, t * P:(t + 1) * P], w["wv"],
                                         start=True, stop=True)
                last.then_inc(p.made, 1)

            narrow_pe(pe, m, a, p, piece)

        @ph.block.scalar
        def _(act):
            opened(act, a.exped, a.high_copied)

            def piece(n, b):
                if n == 0:
                    act.wait_ge(p.made, 3 * b + 1)
                    act.activation(m.qk[:, 0:SK], G[:, :], ACT.Identity, bias=w["bk"]).then_inc(p.taken, 1)

            p.first(piece)
            a.all_batches(act, attention_act(act, m, a), None, p.after(piece))

        @ph.block.vector
        def _(dve):
            opened(dve, a.topped, a.normed, a.low_copied, a.inverted, p.taken)

            def piece(n, b):
                if n == 1:
                    dve.wait_ge(p.made, 3 * b + 2)
                    last = dve.tensor_scalar(m.qk[:, SK:SK + S], G[:, 0:S], w["bq"], scale, ALU.add, ALU.mult)
                    if with_q:
                        last = dve.tensor_tensor(m.h[:, ds(batch_of(b) * QT, QT), :],
                                                 G[:, S:2 * S].rearrange("p (t c) -> p t c", c=C),
                                                 row(w["bq_row"], QT), ALU.add)
                    last.then_inc(p.taken, 1)
                if n == 2:
                    dve.wait_ge(p.made, 3 * b + 3)
                    two = b & 1
                    dve.tensor_tensor(m.v_narrow[:, ds(two, 1), :, :].rearrange("p a t c -> p (a t) c"),
                                      G[:, :].rearrange("p (t c) -> p t c", c=C), row(w["bv_row"], KT),
                                      ALU.add).then_inc(p.taken, 1)

            p.first(piece)
            slot = attention_dve(dve, m, a, lambda b, t, h: m.o[:, ds(b * QT + t, 1), ds(h * a.dh, a.dh)])
            a.all_batches(dve, slot, None, p.after(piece))


def project_pe(pe, m, weight, ready, turned, out_ready):
    if ready is not None:
        pe.wait_ge(*ready)
    turn_pe(pe, m, m.o, turned)
    pe.wait_ge(out_ready[0], 4)
    for g in range(4):
        for t in range(4):
            last = pe.matmul(m.banks[:, g, t * P:(t + 1) * P], m.hT[:, (4 * g + t) * P:(4 * g + t + 1) * P],
                             weight, start=True, stop=True)
        last.then_inc(out_ready[1], 1)


def l0_xattn_finish(nc, m, w):
    with Phase(nc, "L0x_finish") as ph:
        steps, turned, copied, projected = (ph.sem(n) for n in ("steps", "turned", "copied", "projected"))
        norm = Normalization(ph)

        @ph.block.vector
        def _(dve):
            st = Steps(dve, steps)
            st.done(dve.tensor_tensor(wide(m.o), wide(m.o), wide(m.h), ALU.add))
            norm.dve(dve, m, 1, m.o, m.o, 1e-5)
            norm.scale_dve(dve, m, 1, st, m.o[:, :, :], w["g0_row"], w["b0_row"])
            turn_out_dve(dve, m, m.hT, turned, copied)
            for g in range(4):
                dve.wait_ge(projected, g + 1)
                st.done(dve.tensor_tensor(m.h[:, 4 * g:4 * g + 4, :],
                                          m.banks[:, g, :].rearrange("p (t c) -> p t c", c=C),
                                          row(w["bo_row"], 4), ALU.add))
            st.done(dve.scalar_tensor_tensor(out=wide(m.o), in0=wide(m.h), scalar=0.0, in1=wide(m.o),
                                             op0=ALU.max, op1=ALU.add))
            norm.dve(dve, m, 2, m.o, m.o, 1e-5)
            norm.scale_dve(dve, m, 2, st, m.o[:, :, :], w["g1_row"], w["b1_row"])
            st.done(dve.tensor_tensor(wide(m.x), wide(m.x), wide(m.o), ALU.add))

        @ph.block.scalar
        def _(act):
            norm.act(act, m, 1, m.o, m.o)
            turn_out_act(act, m, m.hT, turned, copied)
            norm.act(act, m, 2, m.o, m.o)

        @ph.block.tensor
        def _(pe):
            project_pe(pe, m, w["wo"], (steps, 3), turned, (copied, projected))


def xattn_finish(nc, m, name, w, x, bias=True):
    with Phase(nc, name + "_finish") as ph:
        steps, turned, copied, projected = (ph.sem(n) for n in ("steps", "turned", "copied", "projected"))

        @ph.block.vector
        def _(dve):
            st = Steps(dve, steps)
            if bias:
                st.done(dve.tensor_tensor(x[:, :, :], x[:, :, :], row(w["bo_row"], TILES), ALU.add))
            turn_out_dve(dve, m, m.hT, turned, copied)
            for g in range(4):
                dve.wait_ge(projected, g + 1)
                st.done(dve.tensor_tensor(wide(x[:, 4 * g:4 * g + 4, :]), wide(x[:, 4 * g:4 * g + 4, :]),
                                          m.banks[:, g, :], ALU.add))

        @ph.block.scalar
        def _(act):
            turn_out_act(act, m, m.hT, turned, copied)

        @ph.block.tensor
        def _(pe):
            project_pe(pe, m, w["wo"], None, turned, (copied, projected))


def key_mask_phase(nc, m, name, mask, boolean):
    n = B * SK // P
    with Phase(nc, name + "_mask") as ph:
        loaded, steps, stored = ph.sem("loaded"), ph.sem("steps"), ph.sem("stored")
        here = m.mask_u8 if boolean else m.mask_in
        parts = 1 if boolean else 3

        @ph.block.sync
        def _(sp):
            sp.dma_start(here[:, :], mask.rearrange("a (p n) -> (a p) n", n=n)).then_inc(loaded, 16)
            sp.wait_ge(steps, 3 if boolean else 7)
            for i in range(parts):
                sp.dma_start(m.key_mask[i:i + 1, :], m.mask_part[:, i, :]).then_inc(stored, 16)
            sp.wait_ge(stored, 16 * parts)

        @ph.block.vector
        def _(dve):
            st = Steps(dve, steps)
            part, rest = m.mask_part, m.mask_rest
            dve.wait_ge(loaded, 16)
            if boolean:
                dve.memset(m.key_mask[:, :], 0.0)
                st.done(dve.tensor_copy(m.mask_in[:, :], m.mask_u8[:, :]))
                st.done(dve.reciprocal(rest[:, 0, :], m.mask_in[:, :]))
                st.done(dve.tensor_scalar(part[:, 0, :], rest[:, 0, :], -1.0, 1.0, ALU.mult, ALU.add))
            else:
                st.done(dve.tensor_scalar(rest[:, 1, :], m.mask_in[:, :], -1.0, 1.0, ALU.mult, ALU.add))
                st.done(dve.tensor_scalar(rest[:, 0, :], rest[:, 1, :], -10000.0, None, ALU.mult))
                st.done(dve.tensor_copy(part[:, 0, :], rest[:, 0, :]))
                st.done(dve.tensor_tensor(rest[:, 1, :], rest[:, 0, :], part[:, 0, :], ALU.subtract))
                st.done(dve.tensor_copy(part[:, 1, :], rest[:, 1, :]))
                st.done(dve.tensor_tensor(rest[:, 2, :], rest[:, 1, :], part[:, 1, :], ALU.subtract))
                st.done(dve.tensor_copy(part[:, 2, :], rest[:, 2, :]))


def moe_phase(nc, m, name, x, experts, sizes, func, weighted, biases=None, row_bias=None, fetch=None):
    E, PIECES = len(experts), len(sizes)
    units = E * PIECES
    gated, hidden, prod = m.prob, m.probT[:, :, :, :].rearrange("p s c q -> p s (c q)"), m.banks
    with Phase(nc, name) as ph:
        expanded = ph.sem("expanded")
        activated = ph.sem("activated")
        multiplied = ph.sem("multiplied")
        contracted = ph.sem("contracted")
        combined = ph.sem("combined")
        biased = ph.sem("biased")
        fetch_sync(ph, fetch)

        @ph.block.tensor
        def _(pe):
            opened(pe, contracted)
            with pe.Fori(0, GROUPS) as g:
                def expand(n):
                    gate, up, _ = experts[n // PIECES]
                    size, s = sizes[n % PIECES], n % 2
                    pe.wait_ge(multiplied, g * units + 1 + max(n - 1, 0))
                    moving = m.hT[:, ds(g * GROUP, GROUP)]
                    pe.matmul(prod[0:size, s, :], gate(n % PIECES), moving, start=True, stop=True)
                    pe.matmul(prod[0:size, 2 + s, :], up(n % PIECES), moving, start=True,
                              stop=True).then_inc(expanded, 1)

                def contract(n):
                    e, i, s = n // PIECES, n % PIECES, n % 2
                    size, down = sizes[i], experts[e][2]
                    pe.wait_ge(multiplied, g * units + n + 2)
                    if i == 0:
                        pe.wait_ge(combined, g * E + 1 + max(e - 1, 0))
                    for t in range(GT):
                        last = pe.matmul(m.pT[:, e % 2, t * C:(t + 1) * C], hidden[0:size, s, t * P:(t + 1) * P],
                                         down(i), start=i == 0 and t == 0, stop=i == PIECES - 1,
                                         skip_group_check=True)
                    last.then_inc(contracted, 1)

                for n in range(units):
                    expand(n)
                    if n:
                        contract(n - 1)
                contract(units - 1)

        @ph.block.scalar
        def _(act):
            with act.Fori(0, GROUPS) as g:
                for n in range(units):
                    size, s = sizes[n % PIECES], n % 2
                    act.wait_ge(expanded, g * units + n + 1)
                    act.wait_ge(multiplied, g * units + 1 + max(n - 1, 0))
                    bias = 0.0 if biases is None else biases[1][0:size, n:n + 1]
                    act.activation(gated[0:size, s, 0:GROUP], prod[0:size, s, :], func,
                                   bias=bias).then_inc(activated, 1)

        @ph.block.vector
        def _(dve):
            opened(dve, multiplied, combined)
            if row_bias is not None:
                dve.tensor_tensor(x[:, :, :], x[:, :, :], row(row_bias, TILES), ALU.add).then_inc(biased, 1)
                dve.wait_ge(biased, 1)
            with dve.Fori(0, GROUPS) as g:
                def multiply(n):
                    size, s = sizes[n % PIECES], n % 2
                    dve.wait_ge(activated, g * units + n + 1)
                    dve.wait_ge(contracted, g * units + 1 + max(n - 1, 0))
                    if biases is None:
                        ins = dve.tensor_tensor(hidden[0:size, s, 0:GROUP], gated[0:size, s, 0:GROUP],
                                                prod[0:size, 2 + s, :], ALU.mult)
                    else:
                        ins = dve.scalar_tensor_tensor(out=hidden[0:size, s, 0:GROUP], in0=prod[0:size, 2 + s, :],
                                                       scalar=biases[0][0:size, n:n + 1],
                                                       in1=gated[0:size, s, 0:GROUP], op0=ALU.add, op1=ALU.mult)
                    ins.then_inc(multiplied, 1)

                def combine(e):
                    dve.wait_ge(contracted, g * units + (e + 1) * PIECES + 1)
                    dve.wait_ge(combined, g * E + e + 1)
                    here = x[:, ds(g * GT, GT), :]
                    if weighted[e] is None:
                        last = dve.tensor_tensor(here, here, m.pT[:, e % 2, :].rearrange("p (t c) -> p t c", c=C),
                                                 ALU.add)
                    else:
                        for t in range(GT):
                            tile = x[:, ds(g * GT + t, 1), :]
                            last = dve.scalar_tensor_tensor(
                                out=tile, in0=m.pT[:, e % 2, t * C:(t + 1) * C].unsqueeze(1),
                                scalar=m.weight[:, ds(g * GT + t, 1), weighted[e]:weighted[e] + 1], in1=tile,
                                op0=ALU.mult, op1=ALU.add)
                    last.then_inc(combined, 1)

                for n in range(units):
                    multiply(n)
                    if n >= PIECES and n % PIECES == 0:
                        combine(n // PIECES - 1)
                combine(E - 1)


def route_phase(nc, m, name, router, experts, keep, bias=None, softmax=True, eps=None):
    E = experts
    with Phase(nc, name + "_route") as ph:
        steps, scored, shifted, exped = ph.sem("steps"), ph.sem("scored"), ph.sem("shifted"), ph.sem("exped")
        p, wt = m.scores16[:, :, 0:E], m.weight[:, :, 0:E]
        logits = m.pG[:, 0:TILES * E].rearrange("p (t e) -> p t e", e=E)
        more = m.prob[:, :, :].rearrange("p s n -> p (s n)")[:, 0:TILES * E * E].rearrange(
            "p (t e f) -> p t e f", e=E, f=E)
        same = m.probT[:, :, :, :].rearrange("p s c q -> p (s c q)")[:, 0:TILES * E * E].rearrange(
            "p (t e f) -> p t e f", e=E, f=E)

        @ph.block.tensor
        def _(pe):
            for t in range(TILES):
                last = pe.matmul(m.pG[:, t * E:(t + 1) * E], m.hT[:, t * P:(t + 1) * P], router, start=True, stop=True)
            last.then_inc(scored, 1)

        @ph.block.scalar
        def _(act):
            if softmax:
                act.wait_ge(shifted, 1)
                act.activation(p, p, ACT.Exp).then_inc(exped, 1)

        @ph.block.vector
        def _(dve):
            st = Steps(dve, steps)
            dve.wait_ge(scored, 1)
            if bias is None:
                st.done(dve.tensor_copy(p, logits))
            else:
                st.done(dve.tensor_tensor(p, logits, row(bias, TILES), ALU.add))
            if softmax:
                st.done(dve.tensor_reduce(m.sum[:, :], p, AX_X, ALU.max))
                dve.tensor_tensor(p, p, each(m.sum[:, :], E), ALU.subtract).then_inc(shifted, 1)
                dve.wait_ge(exped, 1)
                st.done(dve.tensor_reduce(m.var[:, :], p, AX_X, ALU.add))
                st.done(dve.reciprocal(m.rstd[:, :], m.var[:, :]))
                st.done(dve.tensor_tensor(p, p, each(m.rstd[:, :], E), ALU.mult))
            other = p.unsqueeze(2).broadcast_to([P, TILES, E, E])
            before = m.k["before"].rearrange("p (e f) -> p e f", f=8)[:, 0:E, 0:E].unsqueeze(1).broadcast_to(
                [P, TILES, E, E])
            st.done(dve.tensor_tensor(more, other, each(p, E), ALU.is_gt))
            st.done(dve.tensor_tensor(same, other, each(p, E), ALU.is_equal))
            st.done(dve.tensor_tensor(same, same, before, ALU.mult))
            st.done(dve.tensor_tensor(more, more, same, ALU.add))
            st.done(dve.tensor_reduce(m.rank[:, :, 0:E], more, AX_X, ALU.add))
            if not softmax:
                st.done(dve.tensor_scalar(wt, m.rank[:, :, 0:E], keep - 0.5, None, ALU.is_lt))
                return
            st.done(dve.tensor_scalar(m.rank[:, :, 0:E], m.rank[:, :, 0:E], keep - 0.5, None, ALU.is_lt))
            st.done(dve.tensor_tensor(wt, m.rank[:, :, 0:E], p, ALU.mult))
            st.done(dve.tensor_reduce(m.sum[:, :], wt, AX_X, ALU.add))
            if eps is not None:
                st.done(dve.tensor_scalar(m.sum[:, :], m.sum[:, :], eps, None, ALU.add))
            st.done(dve.reciprocal(m.rstd[:, :], m.sum[:, :]))
            st.done(dve.tensor_tensor(wt, wt, each(m.rstd[:, :], E), ALU.mult))


def stacked(w, hidden, shared=True):
    n = len(pieces(hidden))

    def expert(e):
        def part(name):
            return lambda i: w[name][:, e * hidden + pieces(hidden)[i][0]:e * hidden + sum(pieces(hidden)[i])]

        def down(i):
            return w["down"][0:pieces(hidden)[i][1], (e * n + i) * C:(e * n + i + 1) * C]
        return part("gate"), part("up"), down
    return expert


def affine_phase(nc, m, name, src, dst, scale, shift, back=False, columns=None):
    with Phase(nc, name) as ph:
        steps, turned, copied = ph.sem("steps"), ph.sem("turned"), ph.sem("copied")
        norm = Normalization(ph)
        first = 4 if back else 0
        flat = wide(dst)

        @ph.block.vector
        def _(dve):
            st = Steps(dve, steps)
            if back:
                turn_out_dve(dve, m, flat, turned, copied)
                dve.wait_ge(copied, 4)
            norm.dve(dve, m, 1, src, dst, 1e-5)
            if scale is not None:
                norm.scale_dve(dve, m, 1, st, dst[:, :, :], scale, shift)
            for g in (1, 3):
                dve.wait_ge(turned, first + g + 1)
                if columns is None:
                    dve.tensor_copy(m.hT[:, g * 512:(g + 1) * 512], m.banks[:, g, :])
                else:
                    dve.tensor_scalar(m.hT[:, g * 512:(g + 1) * 512], m.banks[:, g, :], columns[0], columns[1],
                                      ALU.mult, ALU.add)

        @ph.block.scalar
        def _(act):
            if back:
                turn_out_act(act, m, flat, turned, copied)
            norm.act(act, m, 1, src, dst)
            for g in (0, 2):
                act.wait_ge(turned, first + g + 1)
                if columns is None:
                    act.activation(m.hT[:, g * 512:(g + 1) * 512], m.banks[:, g, :], ACT.Copy)
                else:
                    act.activation(m.hT[:, g * 512:(g + 1) * 512], m.banks[:, g, :], ACT.Identity,
                                   scale=columns[0], bias=columns[1])

        @ph.block.tensor
        def _(pe):
            if back:
                turn_pe(pe, m, m.hT[:, :].rearrange("p (t c) -> p t c", c=P), turned)
            if scale is None:
                norm.wait(pe, 1)
            else:
                pe.wait_ge(steps, 2)
            turn_pe(pe, m, dst, turned)


def shift_phase(nc, m, name, y, w):
    half = C // 2
    with Phase(nc, name) as ph:
        turned, cleared = ph.sem("turned"), ph.sem("cleared")
        shifted = m.hT[half:C, :].rearrange("p (b s) -> p b s", s=S)

        @ph.block.gpsimd
        def _(pool):
            pool.memset(shifted[:, :, 0:1], 0.0).then_inc(cleared, 1)
            pool.wait_ge(cleared, 1)
            if w is not None:
                for n, (scale, cos, sin) in enumerate(((w["qs_row"], "xq_cos", "xq_sin"),
                                                       (w["ks_row"], "xk_cos", "xk_sin"))):
                    c = w[cos].rearrange("p (t d) -> p t d", d=WIDE)
                    s = w[sin].rearrange("p (t d) -> p t d", d=WIDE)
                    at = slice(2 * n, 2 * n + 2)
                    h = WIDE // 2
                    pool.tensor_tensor(m.turn_cos[:, at, :], c, row(scale, QT), ALU.mult)
                    pool.tensor_tensor(m.turn_sin[:, at, 0:h], s[:, :, 0:h], row(scale[:, h:WIDE], QT), ALU.mult)
                    pool.tensor_tensor(m.turn_sin[:, at, h:WIDE], s[:, :, h:WIDE], row(scale[:, 0:h], QT), ALU.mult)

        @ph.block.tensor
        def _(pe):
            turn_pe(pe, m, y, turned)

        def move(g, copy):
            bank = m.banks[:, g, :].rearrange("p (b s) -> p b s", s=S)
            copy(m.hT[0:half, g * 512:(g + 1) * 512], m.banks[0:half, g, :])
            copy(shifted[:, 2 * g:2 * g + 2, 1:S], bank[half:C, :, 0:S - 1])

        @ph.block.scalar
        def _(act):
            for g in (0, 2):
                act.wait_ge(turned, g + 1)
                move(g, lambda dst, src: act.activation(dst, src, ACT.Copy))

        @ph.block.vector
        def _(dve):
            for g in (1, 3):
                dve.wait_ge(turned, g + 1)
                move(g, lambda dst, src: dve.tensor_copy(dst, src))


def output_pe(pe, m, w, n, o, o_turned, oT_ready, out_mm, b):
    for c in range(n):
        for t in range(QT):
            last = pe.transpose(m.banks[:, c // 2, (c % 2) * S + t * P:(c % 2) * S + (t + 1) * P],
                                o[:, t, c * P:(c + 1) * P], m.k["ident"])
    last.then_inc(o_turned, 1)
    pe.wait_ge(oT_ready, b + 1)
    for t in range(QT):
        for c in range(n):
            last = pe.matmul(m.pG[:, t * P:(t + 1) * P], m.qT[:, c, t * P:(t + 1) * P], w[:, c * C:(c + 1) * C],
                             start=c == 0, stop=c == n - 1)
    last.then_inc(out_mm, 1)


def local_phase(nc, m, name, w, y, fetch=None):
    CH, W = CHUNKS_L0F, CHUNKS_L0F * P
    h = WIDE // 2
    with Phase(nc, name) as ph:
        a = Attention(ph, L0F_HEADS, WIDE, S, w["scale"], mask="tiles")
        copied = ph.sem("copied")
        rooted = ph.sem("rooted")
        bounded = ph.sem("bounded")
        inv_ready = ph.sem("inv_ready")
        o_copied = ph.sem("o_copied")
        o_turned = ph.sem("o_turned")
        oT_ready = ph.sem("oT_ready")
        out_mm = ph.sem("out_mm")
        added = ph.sem("added")
        qk_mm = ph.sem("qk_mm")
        values_mm = ph.sem("values_mm")
        split_off = ph.sem("split_off")
        values_ready = ph.sem("values_ready")
        summed = ph.sem("summed")
        rotated = ph.sem("rotated")
        joined = ph.sem("joined")
        scaled = ph.sem("scaled")
        qk_turned = ph.sem("qk_turned")
        queries_ready = ph.sem("queries_ready")
        keys_ready = ph.sem("keys_ready")
        flat_q, flat_k, flat_v = (t[:, :, :].rearrange("p c n -> p (c n)") for t in (m.qT, m.kT, m.v))
        qT = flat_q.rearrange("p (two c n) -> p two c n", two=2, n=S)
        kT = flat_k[:, 0:2048].rearrange("p (two c n) -> p two c n", two=2, n=S)
        v = flat_v[:, 0:2048].rearrange("p (two t n) -> p two t n", two=2, n=W)
        raw = flat_v[:, 2048:4096].rearrange("p (t a n) -> p t a n", t=QT, n=W)
        squares = flat_k[:, 2048:3072]
        oT = flat_k[:, 3072:4096].rearrange("p (t n) -> p t n", n=W)
        swapped = m.key_mask[:, :].bitcast(F32).rearrange("p (t a n) -> p t a n", t=QT, n=W)
        rotating = wide(m.h).rearrange("p (t a n) -> p t a n", t=QT, n=W)
        o = wide(m.o).rearrange("p (two t n) -> p two t n", two=2, n=W)
        o_all = wide(m.o).rearrange("p (two n) -> p two n", two=2)
        free = max(width(XW["L0x"]), width(XW["L1x"]))
        o_flat = m.xw[:, free:free + QT * W]
        o_now = o_flat.rearrange("p (t n) -> p t n", n=W)
        bankq, bankk, bankv, G = m.banks[:, 1, :], m.banks[:, 3, :], m.pT[:, 1, :], m.pG
        a.queries = lambda b, j: qT[:, ds(b & 1, 1), ds(j, 1), :].rearrange("p two c n -> p (two c) n")
        a.keys = lambda b, j: kT[:, ds(b & 1, 1), ds(j, 1), :]
        a.values = lambda b, c, head: v[:, ds(b & 1, 1), c, ds(head * WIDE, WIDE)]
        fetch_sync(ph, fetch)

        def done(b, t, back=0):
            return 2 * b + (t + 3 - back)

        def batch_done(b, back=0):
            return b + (2 - back)

        def by_head(ap):
            return ap.rearrange("p a (h d) -> p a h d", d=WIDE)

        @ph.block.gpsimd
        def _(pool):
            opened(pool, a.head_ready, copied, o_copied)
            opened(pool, joined, scaled, by=2)
            one = m.ones[:, 0:1]

            def copy_in(b):
                pool.wait_ge(values_mm, done(b, 0, 1))
                pool.tensor_tensor(m.x_now[:, :], m.hT[:, ds(batch_of(b) * S, S)], one.broadcast_to([P, S]),
                                   ALU.mult).then_inc(copied, 1)

            def join(b, t):
                pool.wait_ge(rotated, done(b, t))
                pool.tensor_tensor(rotating[:, t], rotating[:, t], swapped[:, t], ALU.add).then_inc(joined, 1)

            def divide(b, t):
                pool.wait_ge(inv_ready, batch_done(b))
                pool.wait_ge(joined, done(b, t))
                heads = rotating[:, t].rearrange("p a (h d) -> p (a h) d", d=WIDE)
                inverse = m.inv_norm[:, 2 * t:2 * t + 2, :].rearrange("p a h -> p (a h)")
                pool.tensor_tensor(heads, heads, each(inverse, WIDE), ALU.mult).then_inc(scaled, 1)

            def copy_o(b):
                pool.wait_ge(a.normed, a.count(b, a.H))
                pool.wait_ge(o_turned, batch_done(b, 1))
                pool.tensor_tensor(o_flat.unsqueeze(1), o_all[:, ds(b & 1, 1), :],
                                   one.unsqueeze(1).broadcast_to([P, 1, QT * W]), ALU.mult).then_inc(o_copied, 1)

            def after(b, i, previous):
                if i == 4:
                    for step in (join, divide):
                        for t in range(QT):
                            step(b + 1, t)
                if i == 6:
                    if previous is not None:
                        copy_o(previous)
                    copy_in(b + 2)

            copy_in(0)
            for t in range(QT):
                join(0, t)
                divide(0, t)
            copy_in(1)
            a.all_batches(pool, queries_slot(pool, m, a), lambda b: pool.wait_ge(queries_ready, done(b, 1)), after,
                          lambda: copy_o(B - 1))

        @ph.block.tensor
        def _(pe):
            opened(pe, a.scored, a.turned, a.weighed)
            opened(pe, o_turned, out_mm)
            opened(pe, qk_mm, values_mm, qk_turned, by=2)

            def multiply_qk(b, t):
                pe.wait_ge(copied, batch_done(b))
                pe.wait_ge(split_off, done(b, t, 1))
                if t == 0:
                    pe.wait_ge(queries_ready, done(b, t, 1))
                    pe.wait_ge(keys_ready, done(b, t, 1))
                for n, bank in enumerate((bankq, bankk)):
                    last = pe.matmul(bank, m.x_now[:, t * P:(t + 1) * P], w["wqkv"][:, n * W:(n + 1) * W],
                                     start=True, stop=True)
                last.then_inc(qk_mm, 1)

            def multiply_v(b, t):
                pe.wait_ge(values_ready, done(b, t, 1))
                pe.matmul(bankv, m.x_now[:, t * P:(t + 1) * P], w["wqkv"][:, 2 * W:3 * W], start=True,
                          stop=True).then_inc(values_mm, 1)

            def turn_qk(b, t):
                pe.wait_ge(scaled, done(b, t))
                if t == 0:
                    pe.wait_ge(split_off, done(b, 1))
                else:
                    pe.wait_ge(queries_ready, done(b, 0))
                    pe.wait_ge(keys_ready, done(b, 0))
                for n, bank in enumerate((bankq, bankk)):
                    for c in range(CH):
                        last = pe.transpose(bank[:, c * P:(c + 1) * P], rotating[:, t, n, c * P:(c + 1) * P],
                                            m.k["ident"])
                last.then_inc(qk_turned, 1)

            def turn_o(b, values):
                pe.wait_ge(o_copied, batch_done(b))
                pe.wait_ge(added, batch_done(b, 1))
                pe.wait_ge(values_ready, done(values, 1))
                for t, bank in enumerate((G, bankv)):
                    for c in range(CH):
                        last = pe.transpose(bank[:, c * P:(c + 1) * P], o_now[:, t, c * P:(c + 1) * P],
                                            m.k["ident"])
                last.then_inc(o_turned, 1)

            def put_out(b):
                pe.wait_ge(oT_ready, batch_done(b))
                for t in range(QT):
                    for c in range(CH):
                        last = pe.matmul(G[:, t * P:(t + 1) * P], oT[:, t, c * P:(c + 1) * P],
                                         w["wo"][:, c * C:(c + 1) * C], start=c == 0, stop=c == CH - 1)
                last.then_inc(out_mm, 1)

            def after(b, i, previous):
                if i in (0, 1):
                    multiply_qk(b + 1, i)
                if i in (2, 3):
                    multiply_v(b + 1, i - 2)
                if i in (5, 6):
                    turn_qk(b + 1, i - 5)
                if i == 6 and previous is not None:
                    turn_o(previous, b + 1)
                if i == 7 and previous is not None:
                    put_out(previous)

            def ready(b):
                pe.wait_ge(keys_ready, done(b, 1))
                pe.wait_ge(values_ready, done(b, 1))

            def end():
                turn_o(B - 1, B)
                put_out(B - 1)

            for step in (multiply_qk, multiply_v, turn_qk):
                for t in range(QT):
                    step(0, t)
            a.all_batches(pe, attention_pe(pe, m, a), ready, after, end)

        @ph.block.scalar
        def _(act):
            opened(act, a.exped, a.high_copied)
            opened(act, oT_ready, rooted)
            opened(act, split_off, values_ready, keys_ready, by=2)

            def split(b, t):
                act.wait_ge(qk_mm, done(b, t))
                act.wait_ge(rotated, done(b, t, 2))
                act.wait_ge(summed, done(b, t, 1))
                for n, bank in enumerate((bankq, bankk)):
                    act.activation(raw[:, t, n, :], bank, ACT.Copy)
                    last = act.activation(squares[:, n * W:(n + 1) * W], bank, ACT.Square)
                last.then_inc(split_off, 1)

            def root(b):
                act.wait_ge(summed, done(b, 1))
                act.wait_ge(scaled, done(b, 0, 1))
                act.activation(m.inv_norm[:, :, :], m.norm[:, :, :], ACT.Sqrt).then_inc(rooted, 1)

            def copy_values(b, t):
                act.wait_ge(values_mm, done(b, t))
                act.activation(v[:, ds(b & 1, 1), t, :], bankv.unsqueeze(1), ACT.Copy).then_inc(values_ready, 1)

            def copy_keys(b, t):
                act.wait_ge(qk_turned, done(b, t))
                act.activation(kT[:, ds(b & 1, 1), :, t * P:(t + 1) * P].rearrange("p two c n -> p (two c) n"),
                               bankk.rearrange("p (c n) -> p c n", n=P), ACT.Copy).then_inc(keys_ready, 1)

            def copy_oT(b):
                act.wait_ge(o_turned, batch_done(b))
                act.activation(oT[:, 0, :], G[:, :], ACT.Copy)
                act.activation(oT[:, 1, :], bankv, ACT.Copy).then_inc(oT_ready, 1)

            def after(b, i, previous):
                if i in (0, 1):
                    split(b + 1, i)
                if i in (2, 3):
                    copy_values(b + 1, i - 2)
                if i == 3:
                    root(b + 1)
                if i in (5, 6):
                    copy_keys(b + 1, i - 5)
                if i == 6 and previous is not None:
                    copy_oT(previous)

            for t in range(QT):
                split(0, t)
            root(0)
            for step in (copy_values, copy_keys):
                for t in range(QT):
                    step(0, t)
            a.all_batches(act, attention_act(act, m, a), None, after, lambda: copy_oT(B - 1))

        @ph.block.vector
        def _(dve):
            opened(dve, a.topped, a.normed, a.low_copied, a.inverted, bounded, inv_ready, added)
            opened(dve, summed, rotated, queries_ready, by=2)

            def rotate(b, t):
                dve.wait_ge(split_off, done(b, t))
                dve.wait_ge(joined, done(b, t, 2))
                dve.wait_ge(qk_turned, done(b, t, 2))
                qk, sw = by_head(raw[:, t]), by_head(swapped[:, t])
                at = slice(t, 4, 2)
                cos = m.turn_cos[:, at, :].unsqueeze(2).broadcast_to([P, 2, L0F_HEADS, WIDE])
                sin = m.turn_sin[:, at, :].unsqueeze(2).broadcast_to([P, 2, L0F_HEADS, WIDE])
                dve.tensor_tensor(by_head(rotating[:, t]), qk, cos, ALU.mult)
                dve.tensor_tensor(sw[:, :, :, 0:h], qk[:, :, :, h:WIDE], sin[:, :, :, 0:h], ALU.mult)
                dve.tensor_tensor(sw[:, :, :, h:WIDE], qk[:, :, :, 0:h], sin[:, :, :, h:WIDE],
                                  ALU.mult).then_inc(rotated, 1)

            def measure(b, t):
                dve.wait_ge(inv_ready, batch_done(b, 1))
                dve.wait_ge(split_off, done(b, t))
                dve.tensor_reduce(m.norm[:, 2 * t:2 * t + 2, :].rearrange("p a h -> p (a h)"),
                                  squares.rearrange("p (n d) -> p n d", d=WIDE), AX_X, ALU.add).then_inc(summed, 1)

            def invert(b):
                dve.wait_ge(rooted, batch_done(b))
                dve.tensor_scalar(m.norm[:, :, :], m.inv_norm[:, :, :], 1e-12, None, ALU.max).then_inc(bounded, 1)
                dve.wait_ge(bounded, batch_done(b))
                dve.reciprocal(m.inv_norm[:, :, :], m.norm[:, :, :]).then_inc(inv_ready, 1)

            def copy_queries(b, t):
                dve.wait_ge(qk_turned, done(b, t))
                dve.tensor_copy(qT[:, ds(b & 1, 1), :, t * P:(t + 1) * P].rearrange("p two c n -> p (two c) n"),
                                bankq.rearrange("p (c n) -> p c n", n=P)).then_inc(queries_ready, 1)

            def add_out(b):
                dve.wait_ge(out_mm, batch_done(b))
                here = y[:, ds(b * QT, QT), :]
                dve.tensor_tensor(here, here, G[:, 0:S].rearrange("p (t c) -> p t c", c=C), ALU.add).then_inc(added, 1)

            def after(b, i, previous):
                if i in (1, 2):
                    measure(b + 1, i - 1)
                    rotate(b + 1, i - 1)
                if i == 3:
                    invert(b + 1)
                if i in (5, 6):
                    copy_queries(b + 1, i - 5)
                if i == 7 and previous is not None:
                    add_out(previous)

            for t in range(QT):
                measure(0, t)
                rotate(0, t)
            invert(0)
            for t in range(QT):
                copy_queries(0, t)
            slot = attention_dve(dve, m, a, lambda b, t, head: o[:, ds(b & 1, 1), t, ds(head * WIDE, WIDE)])
            a.all_batches(dve, slot, None, after, lambda: add_out(B - 1))


def place_mask_phase(nc, m, name, allowed):
    with Phase(nc, name) as ph:
        @ph.block.vector
        def _(dve):
            dve.tensor_copy(m.bandb[:, :, :].rearrange("p t k -> p (t k)"), allowed)


def add_phase(nc, m, name):
    with Phase(nc, name) as ph:
        @ph.block.vector
        def _(dve):
            dve.tensor_tensor(wide(m.x), wide(m.x), wide(m.xn), ALU.add)


def l0_ffn(nc, m, w, fetch):
    prepare(nc, m, "L0f")
    place_mask_phase(nc, m, "L0f_mask", w["band"])
    for d in range(2):
        wd = {n[:-1]: v for n, v in w.items() if n.endswith(str(d))}
        wd.update({n: w[n] for n in ("scale", "xq_cos", "xq_sin", "xk_cos", "xk_sin")})
        shift_phase(nc, m, f"L0f{d}_shift", m.xn, wd)
        local_phase(nc, m, f"L0f{d}_attend", wd, m.xn, fetch if d == 0 else None)
        shift_phase(nc, m, f"L0f{d}_shift2", m.xn, None)
        affine_phase(nc, m, f"L0f{d}_norm", m.o, m.o, None, None, back=True, columns=(wd["g"], wd["b"]))
        cut = pieces(L0F_HID)
        value = lambda i: wd["w1"][:, cut[i][0]:sum(cut[i])]
        gate = lambda i: wd["w1"][:, L0F_HID + cut[i][0]:L0F_HID + sum(cut[i])]
        down = lambda i: wd["w2"][0:cut[i][1], i * C:(i + 1) * C]
        moe_phase(nc, m, f"L0f{d}_glu", m.xn, [(gate, value, down)], [n for _, n in cut], ACT.Gelu, [None],
                  biases=(wd["b1"][:, 0:3], wd["b1"][:, 3:6]), row_bias=wd["b2_row"])
    add_phase(nc, m, "L0f_add")


def select_phase(nc, m, w, sel, selT):
    with Phase(nc, "L2x_select") as ph:
        steps, diagonal, spread, own_read, picked, turned, copied, queries, taken = (ph.sem(n) for n in (
            "steps", "diagonal", "spread", "own_read", "picked", "turned", "copied", "queries", "taken"))
        more = m.kT[:, :, :].rearrange("p c n -> p (c n)").rearrange("p (b t j) -> p b t j", b=B, t=QT)
        same = m.v[:, :, :].rearrange("p c n -> p (c n)").rearrange("p (b t j) -> p b t j", b=B, t=QT)
        every = m.banks.rearrange("p a n -> p (a n)").rearrange("p (b j) -> p b j", j=S)
        ident = m.k["ident"].unsqueeze(1).broadcast_to([P, TILES, P])

        @ph.block.gpsimd
        def _(pool):
            pool.wait_ge(picked, 1)
            clear_stacks(pool, m)

        @ph.block.tensor
        def _(pe):
            pe.wait_ge(diagonal, 1)
            for g in range(4):
                last = pe.matmul(m.banks[:, g, :], m.ones[:, :], wide(m.h)[:, g * 512:(g + 1) * 512], start=True,
                                 stop=True)
            last.then_inc(spread, 1)
            pe.wait_ge(picked, 1)
            turn_pe(pe, m, sel, turned, rows=L2_CAP)
            pe.wait_ge(copied, 4)
            for g in range(4):
                for t in range(4):
                    last = pe.matmul(m.banks[:, g, t * P:(t + 1) * P], m.hT[:, (4 * g + t) * P:(4 * g + t + 1) * P],
                                     w["wq"], start=True, stop=True)
            last.then_inc(queries, 1)

        @ph.block.vector
        def _(dve):
            st = Steps(dve, steps)
            st.done(dve.tensor_tensor(m.h[:, :, :], m.xn[:, :, :], row(w["router_row"], TILES), ALU.mult))
            st.done(dve.tensor_reduce(m.route[:, :], m.h[:, :, :], AX_X, ALU.add))
            dve.tensor_tensor(m.h[:, :, :], ident, each(m.route[:, :], P), ALU.mult).then_inc(diagonal, 1)
            dve.wait_ge(spread, 1)
            st.done(dve.tensor_tensor(m.o[:, :, :], m.banks.rearrange("p a (t c) -> p (a t) c", c=P), ident,
                                      ALU.mult))
            st.done(dve.tensor_reduce(m.own[:, :], m.o[:, :, :], AX_X, ALU.add))
            own = each(m.own[:, :].rearrange("p (b t) -> p b t", t=QT), S)
            for b in range(2):
                at = slice(4 * b, 4 * b + 4)
                other = every[:, at, :].unsqueeze(2).broadcast_to([P, 4, QT, S])
                mine = own[:, at]
                for n in range(4):
                    st.done(dve.tensor_tensor(more[:, 4 * b + n], other[:, n], mine[:, n], ALU.is_gt))
                    st.done(dve.tensor_tensor(same[:, 4 * b + n], other[:, n], mine[:, n], ALU.is_equal))
            earlier = w["earlier"].rearrange("p (t j) -> p t j", t=QT).unsqueeze(1).broadcast_to([P, B, QT, S])
            st.done(dve.tensor_tensor(same, same, earlier, ALU.mult))
            st.done(dve.tensor_tensor(more, more, same, ALU.add))
            st.done(dve.tensor_reduce(m.own[:, :].rearrange("p (b t) -> p b t", t=QT), more, AX_X, ALU.add))
            dve.tensor_tensor(sel, row(w["slot"], TILES), each(m.own[:, :], L2_CAP), ALU.is_equal).then_inc(picked, 1)
            turn_out_dve(dve, m, selT, turned, copied, rows=L2_CAP)
            dve.wait_ge(queries, 1)
            rope = w["l2_ropeq"].rearrange("p (n) -> p n").unsqueeze(1).broadcast_to([P, B, QT * C])
            dve.tensor_tensor(wide(m.h).rearrange("p (b n) -> p b n", b=B),
                              m.banks.rearrange("p a (b n) -> p (a b) n", b=2), rope, ALU.mult)

        @ph.block.scalar
        def _(act):
            turn_out_act(act, m, selT, turned, copied, rows=L2_CAP)


def chosen_phase(nc, m, w, sel, selT, fetch):
    with Phase(nc, "L2x_attend") as ph:
        a = Attention(ph, L2_HEADS, C // L2_HEADS, SK, q_rows=L2_CAP, tiles=1)
        p = Preparation(ph, a, SK + L2_CAP)
        scattered, placed, blanked, fetched = (ph.sem(n) for n in ("scattered", "placed", "blanked", "fetched"))
        G, free = m.pG, m.banks[:, 1, :]

        @ph.block.sync
        def _(sp):
            narrow_sync(sp, m, a, p)

        @ph.block.gpsimd
        def _(pool):
            pool.dma_start(*fetch).then_inc(fetched, 16)
            pool.memset(m.prob[L2_CAP:P, :, :], 0.0).then_inc(blanked, 1)
            pool.wait_ge(blanked, 1)
            narrow_pool(pool, m, a, p, ((m.ctx_now[:, :], m.ctxT, SK), (m.x_now[:, :], wide(m.h), S)))
            pool.wait_ge(fetched, 16)

        @ph.block.tensor
        def _(pe):
            def piece(n, b):
                pe.wait_ge(p.taken, 3 * b + n + 1)
                if n == 0:
                    last = pe.matmul(G[:, :], w["wk"], m.ctxT[:, ds(batch_of(b) * SK, SK)], start=True, stop=True)
                if n == 1:
                    pe.wait_ge(p.copied, b + 2)
                    for t in range(QT):
                        last = pe.matmul(G[:, 0:L2_CAP], m.x_now[:, t * P:(t + 1) * P],
                                         sel[:, ds(batch_of(b) * QT + t, 1), :], start=t == 0, stop=t == QT - 1)
                if n == 2:
                    for t in range(KT):
                        last = pe.matmul(G[:, t * P:(t + 1) * P], m.ctx_now[:, t * P:(t + 1) * P], w["wv"],
                                         start=True, stop=True)
                last.then_inc(p.made, 1)

            def scatter(b):
                pe.wait_ge(a.normed, a.count(b, a.H))
                pe.wait_ge(placed, b + 1)
                pe.matmul(free[:, 0:S], m.o_now[0:L2_CAP, :], selT[0:L2_CAP, ds(b * S, S)], start=True,
                          stop=True).then_inc(scattered, 1)

            pe.wait_ge(blanked, 1)
            opened(pe, scattered)
            narrow_pe(pe, m, a, p, piece, scatter)

        @ph.block.scalar
        def _(act):
            opened(act, a.exped, a.high_copied, placed)

            def piece(n, b):
                if n == 2:
                    act.wait_ge(p.made, 3 * b + 3)
                    two = b & 1
                    act.activation(m.v_narrow[:, ds(two, 1), :, :].rearrange("p a t c -> p (a t) c"),
                                   G[:, :].rearrange("p (t c) -> p t c", c=C), ACT.Copy).then_inc(p.taken, 1)

            p.first(piece)

            def place(b):
                act.wait_ge(scattered, b + 2)
                act.activation(wide(m.o)[:, ds(b * S, S)], free[:, 0:S], ACT.Copy).then_inc(placed, 1)

            a.all_batches(act, attention_act(act, m, a), None, p.after(piece, place), lambda: place(B - 1))

        @ph.block.vector
        def _(dve):
            opened(dve, a.topped, a.normed, a.low_copied, a.inverted, p.taken)

            def piece(n, b):
                if n == 0:
                    dve.wait_ge(p.made, 3 * b + 1)
                    dve.tensor_tensor(m.qk[:, 0:SK], G[:, :], w["l2_ropek"], ALU.mult).then_inc(p.taken, 1)
                if n == 1:
                    dve.wait_ge(p.made, 3 * b + 2)
                    dve.tensor_copy(m.qk[:, SK:SK + L2_CAP], G[:, 0:L2_CAP]).then_inc(p.taken, 1)

            p.first(piece)
            slot = attention_dve(dve, m, a, lambda b, t, h: m.o_now[0:L2_CAP, ds(h * a.dh, a.dh)])
            a.all_batches(dve, slot, None, p.after(piece, lambda b: dve.wait_ge(scattered, b + 2)))


def chosen_finish(nc, m, w):
    with Phase(nc, "L2x_finish") as ph:
        steps, projected = ph.sem("steps"), ph.sem("projected")

        @ph.block.tensor
        def _(pe):
            for g in range(4):
                for t in range(4):
                    at = (4 * g + t) * P
                    last = pe.matmul(m.banks[:, g, t * P:(t + 1) * P], wide(m.o)[:, at:at + P], w["wo"], start=True,
                                     stop=True)
                last.then_inc(projected, 1)

        @ph.block.vector
        def _(dve):
            st = Steps(dve, steps)
            for g in range(4):
                at = slice(4 * g, 4 * g + 4)
                dve.wait_ge(projected, g + 1)
                st.done(dve.tensor_tensor(m.h[:, at, :], m.banks[:, g, :].rearrange("p (t c) -> p t c", c=C),
                                          each(m.route[:, at], C), ALU.mult))
                st.done(dve.tensor_tensor(m.x[:, at, :], m.x[:, at, :], m.h[:, at, :], ALU.add))


def wide_cross_phase(nc, m, w, fetch):
    CH, W = CHUNKS_L3, CHUNKS_L3 * P
    HALVES = W // 512
    with Phase(nc, "L3x_attend") as ph:
        a = Attention(ph, L3_HEADS, WIDE, SK, w["scale"], mask="keys")
        (copied, keys_mm, rest_mm, keys_ready, rest_ready, o_turned, oT_low, oT_ready, out_mm, done, biased) = (
            ph.sem(n) for n in ("copied", "keys_mm", "rest_mm", "keys_ready", "rest_ready", "o_turned", "oT_low",
                                "oT_ready", "out_mm", "done", "biased"))
        banks = m.banks
        rest = CH + KT * HALVES
        o = m.o[:, :, :].rearrange("p (t c) d -> p t (c d)", t=QT)
        a.queries = lambda b, j: m.qT[:, ds(j, 1), :]
        a.keys = lambda b, j: m.kT[:, ds(j, 1), :]
        a.values = lambda b, c, head: m.v[:, c, ds(head * WIDE, WIDE)]
        fetch_sync(ph, fetch)

        @ph.block.gpsimd
        def _(pool):
            opened(pool, a.head_ready)
            with pool.Fori(0, B) as b:
                pool.wait_ge(done, b + 1)
                pool.tensor_copy(m.ctx_now[:, :], m.ctxT[:, ds(b * SK, SK)]).then_inc(copied, 1)
                pool.wait_ge(rest_ready, b * rest + rest + 1)
                a.one_batch(pool, queries_slot(pool, m, a), b)

        @ph.block.tensor
        def _(pe):
            opened(pe, a.scored, a.turned, a.weighed, keys_mm, rest_mm)
            with pe.Fori(0, B) as b:
                pe.wait_ge(done, b + 1)
                for c in range(CH):
                    if c >= 2:
                        pe.wait_ge(keys_ready, b * CH + c)
                    pe.matmul(banks[:, c % 2, :], w["wk"][:, c * P:(c + 1) * P], m.ctxT[:, ds(b * SK, SK)],
                              start=True, stop=True).then_inc(keys_mm, 1)
                    if c >= 2:
                        pe.wait_ge(rest_ready, b * rest + c)
                    pe.matmul(banks[:, 2 + c % 2, 0:S], w["wq"][:, c * P:(c + 1) * P], m.hT[:, ds(b * S, S)],
                              start=True, stop=True).then_inc(rest_mm, 1)
                pe.wait_ge(copied, b + 1)
                for n in range(KT * HALVES):
                    t, half = n // HALVES, n % HALVES
                    pe.wait_ge(rest_ready, b * rest + CH + n)
                    pe.matmul(banks[:, 2 + n % 2, :], m.ctx_now[:, t * P:(t + 1) * P],
                              w["wv"][:, half * 512:(half + 1) * 512], start=True, stop=True).then_inc(rest_mm, 1)
                pe.wait_ge(keys_ready, b * CH + CH + 1)
                pe.wait_ge(rest_ready, b * rest + rest + 1)
                a.one_batch(pe, attention_pe(pe, m, a), b)
                pe.wait_ge(a.normed, a.count(b, a.H))
                output_pe(pe, m, w["wo"], CH, o, o_turned, oT_ready, out_mm, b)

        @ph.block.scalar
        def _(act):
            opened(act, a.exped, a.high_copied, keys_ready)
            with act.Fori(0, B) as b:
                for c in range(CH):
                    act.wait_ge(keys_mm, b * CH + c + 2)
                    act.activation(m.kT[:, c, :], banks[:, c % 2, :], ACT.Identity,
                                   bias=w["bk"][:, c:c + 1]).then_inc(keys_ready, 1)
                a.one_batch(act, attention_act(act, m, a), b)
                act.wait_ge(o_turned, b + 1)
                act.activation(m.qT[:, 4:8, :], banks[:, 2:4, :].rearrange("p a (c q) -> p (a c) q", q=S), ACT.Copy)
                act.wait_ge(oT_low, b + 1)
                act.activation(m.qT[:, 2:4, :], banks[:, 1, :].rearrange("p (c q) -> p c q", q=S),
                               ACT.Copy).then_inc(oT_ready, 1)

        @ph.block.vector
        def _(dve):
            opened(dve, a.topped, a.normed, a.low_copied, a.inverted, rest_ready, done)
            dve.tensor_tensor(m.x[:, :, :], m.x[:, :, :], row(w["bo_row"], TILES), ALU.add).then_inc(biased, 1)
            dve.wait_ge(biased, 1)
            with dve.Fori(0, B) as b:
                for c in range(CH):
                    dve.wait_ge(rest_mm, b * rest + c + 2)
                    dve.tensor_scalar(m.qT[:, c, :], banks[:, 2 + c % 2, 0:S], w["bq"][:, c:c + 1], None,
                                      ALU.add).then_inc(rest_ready, 1)
                for n in range(KT * HALVES):
                    t, half = n // HALVES, n % HALVES
                    at = slice(half * 512, (half + 1) * 512)
                    dve.wait_ge(rest_mm, b * rest + CH + n + 2)
                    dve.tensor_tensor(m.v[:, t, at], banks[:, 2 + n % 2, :], w["bv_row"][:, at],
                                      ALU.add).then_inc(rest_ready, 1)
                a.one_batch(dve, attention_dve(dve, m, a, lambda _, t, h: o[:, t:t + 1, ds(h * WIDE, WIDE)]), b)
                dve.wait_ge(o_turned, b + 1)
                dve.tensor_copy(m.qT[:, 0:2, :],
                                banks[:, 0, :].rearrange("p (c q) -> p c q", q=S)).then_inc(oT_low, 1)
                dve.wait_ge(out_mm, b + 1)
                here = m.x[:, ds(b * QT, QT), :]
                dve.tensor_tensor(here, here, m.pG[:, 0:S].rearrange("p (t c) -> p t c", c=C),
                                  ALU.add).then_inc(done, 1)


def conv_phase(nc, m, w):
    with Phase(nc, "L3f_conv") as ph:
        steps = ph.sem("steps")
        src = m.hT[:, :].rearrange("p (b s) -> p b s", s=S)
        dst = wide(m.h).rearrange("p (b s) -> p b s", s=S)

        @ph.block.vector
        def _(dve):
            st = Steps(dve, steps)
            st.done(dve.tensor_scalar(dst, src, w["conv"][:, 2:3], None, ALU.mult))
            for back in (1, 2):
                st.done(dve.scalar_tensor_tensor(out=dst[:, :, back:S], in0=src[:, :, 0:S - back],
                                                 scalar=w["conv"][:, 2 - back:3 - back], in1=dst[:, :, back:S],
                                                 op0=ALU.mult, op1=ALU.add))


def causal_phase(nc, m, w):
    with Phase(nc, "L3f_attend") as ph:
        a = Attention(ph, L3F_HEADS, C // L3F_HEADS, S, mask="tiles")
        p = Preparation(ph, a, 2 * S)
        crossed = ph.sem("crossed")
        G, x = m.pG, wide(m.h)

        @ph.block.sync
        def _(sp):
            narrow_sync(sp, m, a, p)

        @ph.block.gpsimd
        def _(pool):
            narrow_pool(pool, m, a, p, ((m.x_now[:, :], x, S),))

        @ph.block.tensor
        def _(pe):
            def piece(n, b):
                pe.wait_ge(p.taken, 3 * b + n + 1)
                if n < 2:
                    for i, name in enumerate((("wk", "wq"), ("wkr", "wqr"))[n]):
                        last = pe.matmul(G[:, i * S:(i + 1) * S], w[name], x[:, ds(batch_of(b) * S, S)], start=True,
                                         stop=True)
                if n == 2:
                    pe.wait_ge(p.copied, b + 2)
                    for t in range(QT):
                        last = pe.matmul(G[:, t * P:(t + 1) * P], m.x_now[:, t * P:(t + 1) * P], w["wv"],
                                         start=True, stop=True)
                last.then_inc(p.made, 1)

            narrow_pe(pe, m, a, p, piece)

        @ph.block.scalar
        def _(act):
            opened(act, a.exped, a.high_copied)

            def piece(n, b):
                if n == 2:
                    act.wait_ge(p.made, 3 * b + 3)
                    two = b & 1
                    act.activation(m.v_narrow[:, ds(two, 1), 0:QT, :].rearrange("p a t c -> p (a t) c"),
                                   G[:, 0:S].rearrange("p (t c) -> p t c", c=C), ACT.Copy).then_inc(p.taken, 1)

            p.first(piece)
            a.all_batches(act, attention_act(act, m, a), None, p.after(piece))

        @ph.block.vector
        def _(dve):
            opened(dve, a.topped, a.normed, a.low_copied, a.inverted, p.taken)

            def piece(n, b):
                if n == 0:
                    dve.wait_ge(p.made, 3 * b + 1)
                    dve.tensor_tensor(m.qk[:, 0:2 * S], G[:, :], w["l3f_cos"], ALU.mult).then_inc(p.taken, 1)
                if n == 1:
                    dve.wait_ge(p.made, 3 * b + 2)
                    dve.tensor_tensor(m.qk_rest[:, 0:2 * S], G[:, :], w["l3f_sin"], ALU.mult).then_inc(crossed, 1)
                    dve.wait_ge(crossed, b + 1)
                    dve.tensor_tensor(m.qk[:, 0:2 * S], m.qk[:, 0:2 * S], m.qk_rest[:, 0:2 * S],
                                      ALU.add).then_inc(p.taken, 1)

            p.first(piece)
            slot = attention_dve(dve, m, a, lambda b, t, h: m.o[:, ds(b * QT + t, 1), ds(h * a.dh, a.dh)])
            a.all_batches(dve, slot, None, p.after(piece))


def l3_ffn(nc, m, w):
    prepare(nc, m, "L3f", clear=True)
    place_mask_phase(nc, m, "L3f_mask", w["causal"])
    affine_phase(nc, m, "L3f_norm1", m.xn, m.o, w["g1_row"], w["b1_row"])
    conv_phase(nc, m, w)
    causal_phase(nc, m, w)
    xattn_finish(nc, m, "L3f", w, m.xn, bias=False)
    affine_phase(nc, m, "L3f_norm2", m.xn, m.o, w["g2_row"], w["b2_row"])
    route_phase(nc, m, "L3f", w["router"], L3F_EXPERTS, 1, softmax=False)
    cut = pieces(L3F_HID)

    def expert(e):
        at = 2 * L3F_HID * e
        gate = lambda i: w["wv2"][:, at + i * P:at + (i + 1) * P]
        value = lambda i: w["wv2"][:, at + L3F_HID + i * P:at + L3F_HID + (i + 1) * P]
        down = lambda i: w["down"][:, (e * len(cut) + i) * C:(e * len(cut) + i + 1) * C]
        return gate, value, down

    moe_phase(nc, m, "L3f_moe", m.xn, [expert(e) for e in range(L3F_EXPERTS)], [n for _, n in cut], ACT.Silu,
              list(range(L3F_EXPERTS)))
    add_phase(nc, m, "L3f_add")


def store_phase(nc, m, out):
    with Phase(nc, "store") as ph:
        stored = ph.sem("stored")

        @ph.block.sync
        def _(sp):
            sp.dma_start(out.rearrange("(t p) c -> p t c", p=P), m.x[:, :, :]).then_inc(stored, 16)
            sp.wait_ge(stored, 16)


def build(nc, x, ctxT, mask_f, mask_b, wx, wf, const, out):
    with ExitStack() as ctx:
        m = Memory(nc, ctx)
        load_phase(nc, m, x, ctxT, (mask_f, mask_b), wx, wf, const)
        k = m.k

        def weights_f(name):
            return m.fw[:, 0:width(FW[name])], wf[name]

        def weights_x(name):
            return m.xw[:, 0:width(XW[name])], wx[name]

        w = views(m.xw, XW["L0x"])
        prepare(nc, m, "L0x", clear=True)
        cross_phase(nc, m, "L0x", w, L0_HEADS, with_q=True, fetch=weights_f("L0f"))
        l0_xattn_finish(nc, m, w)
        l0_ffn(nc, m, views(m.fw, FW["L0f"]), weights_x("L1x"))
        w = views(m.xw, XW["L1x"])
        prepare(nc, m, "L1x", clear=True)
        key_mask_phase(nc, m, "L1x", mask_f, False)
        cross_phase(nc, m, "L1x", w, L1_HEADS, mask=True, fetch=weights_f("L1f"))
        xattn_finish(nc, m, "L1x", w, m.x)
        w = views(m.fw, FW["L1f"])
        prepare(nc, m, "L1f")
        route_phase(nc, m, "L1f", w["router"], L1F_EXPERTS, 2, bias=w["rb_row"])
        moe_phase(nc, m, "L1f", m.x, [stacked(w, L1F_HID)(e) for e in range(1 + L1F_EXPERTS)],
                  [n for _, n in pieces(L1F_HID)], ACT.Silu, [None, *range(L1F_EXPERTS)],
                  fetch=weights_x("L2x"))
        w = views(m.xw, XW["L2x"])
        sel = m.sel[:, :, :]
        selT = wide(m.xn)
        prepare(nc, m, "L2x")
        select_phase(nc, m, w, sel, selT)
        chosen_phase(nc, m, w, sel, selT, weights_f("L2f"))
        chosen_finish(nc, m, w)
        w = views(m.fw, FW["L2f"])
        prepare(nc, m, "L2f")
        route_phase(nc, m, "L2f", w["router"], L2F_EXPERTS, 2, eps=1e-20)
        moe_phase(nc, m, "L2f", m.x, [stacked(w, L2F_HID)(e) for e in range(1 + L2F_EXPERTS)],
                  [n for _, n in pieces(L2F_HID)], ACT.Silu, [None, *range(L2F_EXPERTS)],
                  fetch=weights_x("L3x"))
        w = views(m.xw, XW["L3x"])
        prepare(nc, m, "L3x")
        key_mask_phase(nc, m, "L3x", mask_b, True)
        wide_cross_phase(nc, m, w, weights_f("L3f"))
        l3_ffn(nc, m, views(m.fw, FW["L3f"]))
        store_phase(nc, m, out)


def kernel(**inputs):
    import numpy as np
    import concourse.bacc as bacc
    from concourse import mybir as mb
    from concourse.bass_utils import run_bass_kernel_spmd

    a = {n: np.asarray(v) for n, v in inputs.items()}

    def rows(v):
        return np.broadcast_to(v.reshape(1, -1), (P, v.size))

    def tall(v):
        n = -(-v.shape[0] // P)
        v = np.concatenate([v, np.zeros((n * P - v.shape[0], v.shape[1]), v.dtype)])
        return v.reshape(n, P, -1).transpose(1, 0, 2).reshape(P, -1)

    def chunks(v):
        n = -(-v.size // P)
        return np.concatenate([v, np.zeros(n * P - v.size, v.dtype)]).reshape(n, P).T

    L0x = {n: a["L0_xattn_" + n] for n in ("Wq", "Wk", "Wv", "Wo", "bq", "bk", "bv", "bo", "g0", "b0", "g1", "b1")}
    L1x = {n: a["L1_xattn_" + n] for n in ("Wq", "Wk", "Wv", "Wo", "bq", "bk", "bv", "bo")}
    L2x = {n: a["L2_xattn_" + n] for n in ("router_w", "q_w", "kv_w", "out_w")}
    L3x = {n: a["L3_xattn_" + n] for n in ("Wq", "Wk", "Wv", "Wo", "bq", "bk", "bv", "bo")}
    L0f = {n: a["L0_ffn_" + n] for n in ("wqkv", "q_scale", "k_scale", "wo", "ln_g", "ln_b", "w1", "b1", "w2", "b2")}
    L1f = {n: a["L1_ffn_" + n] for n in ("sg", "su", "sd", "rg", "ru", "rd", "wr", "rb")}
    L2f = {n: a["L2_ffn_" + n] for n in ("Wr", "Wg", "Wu", "Wd", "Sg", "Su", "Sd")}
    L3f = {n: a["L3_ffn_" + n] for n in ("ln1_w", "ln1_b", "ln2_w", "ln2_b", "conv_w", "attn_w", "proj_w",
                                         "router_w", "expert_wv", "expert_proj")}
    by16 = np.arange(C).reshape(8, 1, 16).transpose(1, 2, 0).reshape(-1)
    by8 = np.arange(C).reshape(8, 2, 8).transpose(1, 2, 0).reshape(-1)
    hd = C // L3F_HEADS
    f = np.float32
    part = np.arange(P)
    head_rows = lambda n, s: (part[:, None] // (P // n) == np.arange(n)[None]) * f(s)
    place = np.arange(S)
    q_at, k_at = place[:, None], place[None, :]
    tile2 = lambda t: t.reshape(QT, P, -1).transpose(1, 0, 2).reshape(P, -1)
    masked = f(-1e30)
    freq4 = np.exp(np.linspace(0.0, -1.0, 4, dtype=f) * np.log(f(10000.0))).astype(f)

    def l2_rope(n):
        angle = np.arange(n, dtype=f)[:, None] * freq4
        return np.tile(np.concatenate([np.sin(angle), np.cos(angle)], axis=-1), (1, L2_HEADS))

    inv = (f(1.0) / f(10000.0) ** (np.arange(0, hd, 2, dtype=f) / f(hd))).astype(f)
    ang = place.astype(f)[:, None] * inv
    l3_cos = np.tile(np.cos(ang), (1, 2 * L3F_HEADS)).T
    l3_sin = np.tile(np.concatenate([-np.sin(ang), np.sin(ang)], axis=-1), (1, L3F_HEADS)).T
    half = np.arange(0, WIDE, 2, dtype=f)
    ang = place.astype(f)[:, None] * (f(1.0) / f(10000.0) ** (half / f(WIDE)))[None]
    base = (half + f(0.4 * WIDE)) / f(1.4 * WIDE)
    grow = base[None] ** ((place - S // 2).astype(f) / f(32.0))[:, None]
    both = lambda t: np.concatenate([t, t], axis=-1)
    signed = lambda t: np.concatenate([-t, t], axis=-1)
    thin = lambda t: np.asarray(t, dtype=f)
    consts = [np.eye(P), rows(np.arange(8)[None] < np.arange(8)[:, None])]
    band = tile2(np.where((k_at <= q_at) & (k_at >= q_at - 64), f(0), masked))
    causal = tile2(np.where(k_at <= q_at, f(0), masked))
    local_tables = [np.tile(head_rows(2, 8.0), (1, CHUNKS_L0F)), band, tile2(both(np.cos(ang) * grow)),
                    tile2(signed(np.sin(ang) * grow)), tile2(both(np.cos(ang) / grow)),
                    tile2(signed(np.sin(ang) / grow))]
    causal_tables = [causal, l3_cos[by8], l3_cos[by8] / np.sqrt(f(8)), l3_sin[by8], l3_sin[by8] / np.sqrt(f(8))]
    chosen_tables = [tile2((l2_rope(S) / np.sqrt(f(8)))[:, by8]), l2_rope(SK).T[by8], rows(np.arange(L2_CAP)),
                     tile2(k_at < q_at)]

    packs = {
        "x_L0x": [L0x["Wq"].T[:, by16], L0x["Wq"].T, L0x["Wk"].T[:, by16], L0x["Wv"].T, L0x["Wo"].T,
                  chunks(L0x["bq"][by16]), chunks(L0x["bk"][by16]),
                  *(rows(L0x[n]) for n in ("bq", "bv", "bo", "g0", "b0", "g1", "b1"))],
        "x_L1x": [L1x["Wq"].T[:, by8], L1x["Wk"].T[:, by8], L1x["Wv"].T, L1x["Wo"].T, chunks(L1x["bq"][by8]),
                  chunks(L1x["bk"][by8]),
                  rows(L1x["bv"]), rows(L1x["bo"])],
        "x_L2x": [L2x["q_w"].T[:, by8], L2x["kv_w"][:C].T[:, by8], L2x["kv_w"][C:].T, L2x["out_w"].T, rows(L2x["router_w"]),
                  *chosen_tables],
        "x_L3x": [L3x["Wq"], L3x["Wk"], L3x["Wv"], tall(L3x["Wo"]), chunks(L3x["bq"]), chunks(L3x["bk"]),
                  rows(L3x["bv"]), rows(L3x["bo"]), np.tile(head_rows(2, 1 / 8.0), (1, CHUNKS_L3))],
        "f_L1f": [*(L1f[s].T for s in ("sg",)), *(w.T for w in L1f["rg"]), L1f["su"].T, *(w.T for w in L1f["ru"]),
                  tall(L1f["sd"].T), *(tall(w.T) for w in L1f["rd"]), L1f["wr"].T, rows(L1f["rb"])],
        "f_L2f": [L2f["Sg"], *L2f["Wg"], L2f["Su"], *L2f["Wu"], tall(L2f["Sd"]), *(tall(w) for w in L2f["Wd"]),
                  L2f["Wr"]],
    }
    depth = []
    for d in (0, 1):
        b1 = L0f["b1"][d]
        depth += [L0f["wqkv"][d], tall(L0f["wo"][d]), L0f["w1"][d], tall(L0f["w2"][d]), rows(L0f["q_scale"][d]),
                  rows(L0f["k_scale"][d]), chunks(L0f["ln_g"][d]), chunks(L0f["ln_b"][d]),
                  chunks(b1[:L0F_HID]), chunks(b1[L0F_HID:]), rows(L0f["b2"][d])]
    packs["f_L0f"] = depth + local_tables
    swap = np.arange(C).reshape(L3F_HEADS, 2, hd // 2)[:, ::-1].reshape(-1)
    wq, wk, wv = np.split(L3f["attn_w"], 3, axis=1)
    packs["f_L3f"] = [*L3f["expert_wv"], *(tall(w) for w in L3f["expert_proj"]), wq[:, by8], wq[:, swap][:, by8],
                      wk[:, by8], wk[:, swap][:, by8],
                      wv, L3f["proj_w"], L3f["conv_w"].reshape(C, 3), rows(L3f["ln1_w"]), rows(L3f["ln1_b"]),
                      rows(L3f["ln2_w"]), rows(L3f["ln2_b"]), L3f["router_w"], *causal_tables]

    arrays = {n: np.ascontiguousarray(np.concatenate([thin(v) for v in p], axis=1)) for n, p in packs.items()}
    arrays["const"] = np.ascontiguousarray(np.concatenate([thin(v) for v in consts], axis=1))
    arrays["x"] = np.ascontiguousarray(a["x"].reshape(TOK, C))
    arrays["ctxT"] = np.ascontiguousarray(a["ctx_1024"].reshape(B * SK, C).T)
    arrays["mask_f"] = np.ascontiguousarray(a["mask_BxS2_ff1"].reshape(1, B * SK))
    arrays["mask_b"] = np.ascontiguousarray(a["mask_BxS2_bf1"].reshape(1, B * SK)).view(np.uint8)

    nc = bacc.Bacc("TRN2", target_bir_lowering=False, num_devices=1)
    d = {n: nc.dram_tensor("in_" + n, v.shape, mb.dt.from_np(v.dtype), kind="ExternalInput").ap() for n, v in arrays.items()}
    out = nc.dram_tensor("out_0", (TOK, C), mb.dt.float32, kind="ExternalOutput").ap()
    build(nc, d["x"], d["ctxT"], d["mask_f"], d["mask_b"], {n[2:]: d[n] for n in d if n.startswith("x_")},
          {n[2:]: d[n] for n in d if n.startswith("f_")}, d["const"], out)
    got = run_bass_kernel_spmd(nc, [{"in_" + n: v for n, v in arrays.items()}], core_ids=[0]).results[0]["out_0"]
    return got.reshape(B, S, C)
```

```python
from contextlib import ExitStack

import concourse.bass as bass
from concourse import mybir

ds = bass.ds
F32 = mybir.dt.float32
BF16 = mybir.dt.bfloat16
U8 = mybir.dt.uint8
ALU = mybir.AluOpType
ACT = mybir.ActivationFunctionType
AX_X = mybir.AxisListType.X

P = 128
B = 8
S = 256
SK = 512
C = 128
TOK = B * S
TILES = TOK // P
QT = S // P
KT = SK // P
GROUP = 512
GROUPS = TOK // GROUP
GT = GROUP // P

L0_HEADS, L0F_HEADS, L1_HEADS, L2_HEADS, L3_HEADS, L3F_HEADS = 8, 8, 16, 16, 16, 16
WIDE = 64
L0F_HID = 341
L1F_EXPERTS, L1F_HID = 7, 352
L2F_EXPERTS, L2F_HID = 8, 256
L3F_EXPERTS, L3F_HID = 4, 512
WARM = 4
L2_CAP = 64
CHUNKS_L3 = L3_HEADS * WIDE // P
CHUNKS_L0F = L0F_HEADS * WIDE // P


def pieces(n):
    return [(a, min(P, n - a)) for a in range(0, n, P)]


XW = {
    "L0x": [("wq", C), ("wq_plain", C), ("wk", C), ("wv", C), ("wo", C), ("bq", 1), ("bk", 1), ("bq_row", C), ("bv_row", C),
            ("bo_row", C), ("g0_row", C), ("b0_row", C), ("g1_row", C), ("b1_row", C)],
    "L1x": [("wq", C), ("wk", C), ("wv", C), ("wo", C), ("bq", 1), ("bk", 1), ("bv_row", C), ("bo_row", C)],
    "L2x": [("wq", C), ("wk", C), ("wv", C), ("wo", C), ("router_row", C), ("l2_ropeq", QT * C),
            ("l2_ropek", SK), ("slot", L2_CAP), ("earlier", QT * S)],
    "L3x": [("wq", CHUNKS_L3 * C), ("wk", CHUNKS_L3 * C), ("wv", CHUNKS_L3 * C), ("wo", CHUNKS_L3 * C),
            ("bq", CHUNKS_L3), ("bk", CHUNKS_L3), ("bv_row", CHUNKS_L3 * C), ("bo_row", C), ("scale", L3_HEADS)],
}
FW = {
    "L0f": [(n + str(d), c) for d in (0, 1) for n, c in (
        ("wqkv", 3 * CHUNKS_L0F * C), ("wo", CHUNKS_L0F * C), ("w1", 2 * L0F_HID), ("w2", 3 * C), ("qs_row", WIDE),
        ("ks_row", WIDE), ("g", 1), ("b", 1), ("b1", 6), ("b2_row", C))]
           + [("scale", L0F_HEADS), ("band", QT * S), ("xq_cos", QT * WIDE), ("xq_sin", QT * WIDE),
              ("xk_cos", QT * WIDE), ("xk_sin", QT * WIDE)],
    "L1f": [("gate", 8 * L1F_HID), ("up", 8 * L1F_HID), ("down", 8 * 3 * C), ("router", L1F_EXPERTS),
            ("rb_row", L1F_EXPERTS)],
    "L2f": [("gate", 9 * L2F_HID), ("up", 9 * L2F_HID), ("down", 9 * 2 * C), ("router", L2F_EXPERTS)],
    "L3f": [("wv2", L3F_EXPERTS * 2 * L3F_HID), ("down", L3F_EXPERTS * 4 * C), ("wq", C), ("wqr", C), ("wk", C),
            ("wkr", C), ("wv", C), ("wo", C), ("conv", 3), ("g1_row", C), ("b1_row", C), ("g2_row", C),
            ("b2_row", C), ("router", L3F_EXPERTS), ("causal", QT * S), ("l3f_cos", 2 * S), ("l3f_sin", 2 * S)],
}
CW = [("ident", P), ("before", 64)]


def width(table):
    return sum(n for _, n in table)


def views(tile, table):
    out, at = {}, 0
    for name, n in table:
        out[name] = tile[:, at:at + n]
        at += n
    return out


def row(ap, *counts):
    for _ in counts:
        ap = ap.unsqueeze(1)
    return ap.broadcast_to([P, *counts, ap.shape[-1]])


def each(ap, n):
    return ap.unsqueeze(len(ap.shape)).broadcast_to([*ap.shape, n])


class Steps:

    def __init__(self, eng, sem, base=0):
        self.eng, self.sem, self.base, self.n = eng, sem, base, 0

    def done(self, ins):
        ins.then_inc(self.sem, 1)
        self.n += 1
        self.eng.wait_ge(self.sem, self.base + self.n)


class Memory:

    def __init__(self, nc, ctx):
        def sb(name, shape, dt=F32):
            return ctx.enter_context(nc.sbuf_tensor(name, shape, dt))

        def ps(name, shape):
            return ctx.enter_context(nc.psum_tensor(name, shape, F32))

        self.x = sb("x", [P, TILES, C])
        self.xn = sb("xn", [P, TILES, C])
        self.h = sb("h", [P, TILES, C])
        self.o = sb("o", [P, TILES, C])
        self.hT = sb("hT", [P, TOK])
        self.ctxT = sb("ctxT", [P, B * SK])
        self.const = sb("const", [P, width(CW)])
        self.k = views(self.const, CW)
        self.xw = sb("xw", [P, max(width(t) for t in XW.values())])
        self.fw = sb("fw", [P, max(width(t) for t in FW.values())])
        self.sum = sb("row_sum", [P, TILES])
        self.carrier = sb("carrier", [P, 2])
        self.stats = sb("row_stats", [P, TILES, 6])
        self.moments = sb("row_moments", [P, TILES, 2])
        self.offset = sb("row_offset", [P, TILES])
        self.var = sb("row_var", [P, TILES])
        self.std = sb("row_std", [P, TILES])
        self.rstd = sb("row_rstd", [P, TILES])
        self.qT = sb("qT", [P, CHUNKS_L3, S])
        self.kT = sb("kT", [P, CHUNKS_L3, SK])
        self.v = sb("v", [P, KT, L3_HEADS * WIDE])
        self.ctx_now = sb("ctx_now", [P, SK])
        self.x_now = sb("x_now", [P, S])
        self.q_head = sb("q_head", [P, 4, S])
        self.prob = sb("prob", [P, 2, 2 * SK])
        self.probT = sb("probT", [P, 2, KT, S])
        self.top = sb("top", [P, 2, 2])
        self.total = sb("total", [P, 16, 2])
        self.inverse = sb("inverse", [P, 16, 2])
        self.sel = sb("sel", [P, TILES, L2_CAP])
        self.ones = sb("ones", [P, P])
        self.o_now = sb("o_now", [P, C])
        self.scores16 = sb("scores16", [P, TILES, 8])
        self.weight = sb("weight", [P, TILES, 8])
        self.rank = sb("rank", [P, TILES, 8])
        self.norm = sb("norm", [P, 4, L0F_HEADS])
        self.inv_norm = sb("inv_norm", [P, 4, L0F_HEADS])
        self.turn_cos = sb("turn_cos", [P, 4, WIDE])
        self.turn_sin = sb("turn_sin", [P, 4, WIDE])
        self.own = sb("own", [P, TILES])
        self.route = sb("route", [P, TILES])
        self.mask_in = sb("mask_in", [P, B * SK // P])
        self.mask_u8 = sb("mask_u8", [P, B * SK // P], U8)
        self.mask_part = sb("mask_part", [P, 3, B * SK // P], BF16)
        self.mask_rest = sb("mask_rest", [P, 3, B * SK // P])
        q = self.qT[:, :, :].rearrange("p c n -> p (c n)")
        self.qk = q[:, 0:SK + S]
        self.qk_rest = q[:, SK + S:2 * (SK + S)]
        self.qk_part = sb("qk_part", [P, 3, SK + S], BF16)
        self.v_narrow = sb("v_narrow", [P, 2, KT, C])
        self.kS = self.kT[:, :, :].rearrange("p c n -> p (c n)").bitcast(BF16).rearrange(
            "p (two c n) -> p two c n", two=2, n=SK)
        self.qS = self.v[:, :, :].rearrange("p c n -> p (c n)").bitcast(BF16).rearrange(
            "p (two h n) -> p two h n", two=2, n=S)
        self.identb = sb("identb", [P, P], BF16)
        self.allowed = self.ctx_now[:, 0:QT * S // 2].bitcast(BF16).rearrange("p (t k) -> p t k", t=QT)
        self.onesb = sb("onesb", [P, P], BF16)
        self.key_mask = sb("key_mask", [P, B * SK], BF16)
        self.pS = ps("pS", [P, 2, 1024])
        self.pT = ps("pT", [P, 2, 512])
        self.pO = ps("pO", [P, 2, 2, P])
        self.pG = ps("pG", [P, 512])
        self.banks = self.pS[:, :, :].rearrange("p a (b n) -> p (a b) n", b=2)


class Phase:

    def __init__(self, nc, name):
        self.nc, self.name, self.sems = nc, name, []
        self.stack = ExitStack()

    def sem(self, name):
        s = self.nc.alloc_semaphore(f"{self.name}_{name}")
        self.sems.append(s)
        return s

    def __enter__(self):
        self.block = self.stack.enter_context(self.nc.Block(f"{self.name}_block"))
        return self

    def __exit__(self, *e):
        self.stack.close()
        if e[0] is None:
            self.nc.clear_and_free_semaphores(self.sems)
            self.nc.all_engine_barrier()


def wide(ap):
    return ap[:, :, :].rearrange("p t c -> p (t c)")


class Normalization:

    def __init__(self, ph):
        self.measured = ph.sem("measured")
        self.varied = ph.sem("varied")
        self.rooted = ph.sem("rooted")
        self.inverted = ph.sem("inverted")
        self.placed = ph.sem("placed")
        self.low = ph.sem("low_tiles")
        self.high = ph.sem("high_tiles")

    def act(self, act, m, n, src, dst):
        act.wait_ge(self.varied, n)
        act.activation(m.std[:, :], m.var[:, :], ACT.Sqrt).then_inc(self.rooted, 1)
        act.wait_ge(self.placed, n)
        for t in range(8, TILES):
            last = act.activation(dst[:, t, :], src[:, t, :], ACT.Identity, scale=m.rstd[:, t:t + 1],
                                  bias=m.offset[:, t:t + 1])
            if t % 4 == 3:
                last.then_inc(self.high, 1)

    def dve(self, dve, m, n, src, dst, eps):
        for t in range(TILES):
            last = dve.bn_stats(m.stats[:, t, :], src[:, t, :])
        last.then_inc(self.measured, 1)
        dve.wait_ge(self.measured, 2 * n - 1)
        for t in range(TILES):
            last = dve.bn_aggr(m.moments[:, t, :], m.stats[:, t, :])
        last.then_inc(self.measured, 1)
        dve.wait_ge(self.measured, 2 * n)
        dve.tensor_scalar(m.var[:, :], m.moments[:, :, 1], eps, None, ALU.add).then_inc(self.varied, 1)
        dve.wait_ge(self.rooted, n)
        dve.reciprocal(m.rstd[:, :], m.std[:, :]).then_inc(self.inverted, 1)
        dve.wait_ge(self.inverted, n)
        dve.scalar_tensor_tensor(out=m.offset[:, :], in0=m.moments[:, :, 0], scalar=-1.0, in1=m.rstd[:, :],
                                 op0=ALU.mult, op1=ALU.mult).then_inc(self.placed, 1)
        for t in range(8):
            last = dve.tensor_scalar(dst[:, t, :], src[:, t, :], m.moments[:, t, 0:1], m.rstd[:, t:t + 1],
                                     ALU.subtract, ALU.mult)
            if t % 4 == 3:
                last.then_inc(self.low, 1)

    def wait(self, eng, n):
        eng.wait_ge(self.low, 2 * n)
        eng.wait_ge(self.high, 2 * n)

    def scale_dve(self, dve, m, n, steps, dst, scale, shift):
        self.wait(dve, n)
        steps.done(dve.tensor_tensor(dst, dst, row(scale, TILES), ALU.mult))
        steps.done(dve.tensor_tensor(dst, dst, row(shift, TILES), ALU.add))


def turn_pe(pe, m, src, turned, rows=P):
    for g in range(4):
        for t in range(4):
            last = pe.transpose(m.banks[0:rows, g, t * P:(t + 1) * P], src[:, 4 * g + t, :], m.k["ident"])
        last.then_inc(turned, 1)


def turn_out_act(act, m, dst, turned, copied, rows=P):
    for g in (0, 2):
        act.wait_ge(turned, g + 1)
        act.activation(dst[0:rows, g * 512:(g + 1) * 512], m.banks[0:rows, g, :], ACT.Copy).then_inc(copied, 1)


def turn_out_dve(dve, m, dst, turned, copied, rows=P):
    for g in (1, 3):
        dve.wait_ge(turned, g + 1)
        dve.tensor_copy(dst[0:rows, g * 512:(g + 1) * 512], m.banks[0:rows, g, :]).then_inc(copied, 1)


def load_phase(nc, m, x, ctxT, wx, const):
    with Phase(nc, "load") as ph:
        loaded = ph.sem("loaded")

        @ph.block.sync
        def _(sp):
            sp.dma_start(m.x[:, :, :], x.rearrange("(t p) c -> p t c", p=P)).then_inc(loaded, 16)
            sp.dma_start(m.const[:, :], const).then_inc(loaded, 16)
            sp.dma_start(m.xw[:, 0:width(XW["L0x"])], wx["L0x"]).then_inc(loaded, 16)
            sp.dma_start(m.ctxT[:, :], ctxT).then_inc(loaded, 16)
            sp.wait_ge(loaded, 64)

        @ph.block.vector
        def _(dve):
            dve.memset(m.onesb[:, :], 1.0)
            dve.memset(m.ones[:, :], 1.0)
            dve.memset(m.key_mask[:, :], 0.0)
            dve.wait_ge(loaded, 64)


def fetch_sync(ph, fetch):
    if fetch is None:
        return
    fetched = ph.sem("fetched")

    @ph.block.sync
    def _(sp):
        sp.dma_start(*fetch).then_inc(fetched, 16)
        sp.wait_ge(fetched, 16)


def clear_stacks(pool, m):
    pool.memset(m.kS, 0.0)
    pool.memset(m.qS, 0.0)


def prepare(nc, m, name, clear=False):
    with Phase(nc, name + "_prepare") as ph:
        norm = Normalization(ph)
        turned, copied = ph.sem("turned"), ph.sem("copied")

        if clear:
            @ph.block.gpsimd
            def _(pool):
                clear_stacks(pool, m)

        @ph.block.vector
        def _(dve):
            norm.dve(dve, m, 1, m.x, m.xn, 1e-5)
            for n, g in ((3, 1), (4, 3)):
                dve.wait_ge(turned, n)
                dve.tensor_copy(m.hT[:, g * 512:(g + 1) * 512], m.banks[:, g, :]).then_inc(copied, 1)

        @ph.block.scalar
        def _(act):
            norm.act(act, m, 1, m.x, m.xn)
            for n, g in ((1, 0), (2, 2)):
                act.wait_ge(turned, n)
                act.activation(m.hT[:, g * 512:(g + 1) * 512], m.banks[:, g, :], ACT.Copy).then_inc(copied, 1)

        @ph.block.tensor
        def _(pe):
            for g in (0, 2, 1, 3):
                pe.wait_ge(norm.low if g < 2 else norm.high, g % 2 + 1)
                for t in range(4):
                    last = pe.transpose(m.banks[:, g, t * P:(t + 1) * P], m.xn[:, 4 * g + t, :], m.k["ident"])
                last.then_inc(turned, 1)


class Attention:

    def __init__(self, ph, heads, width_, keys, scale=None, q_rows=P, tiles=QT, mask=None):
        self.H, self.dh, self.NK, self.KC, self.scale = heads, width_, keys, keys // P, scale
        self.rows, self.T, self.mask = q_rows, tiles, mask
        self.paired = width_ == WIDE
        self.one_bank = self.paired and keys == S
        self.queries = self.keys = self.values = None
        self.causal = False
        self.mask_by_batch = False
        self.warm = 0
        self.mask_ready = ph.sem("mask_ready")
        self.head_ready = ph.sem("head_ready")
        self.scored = ph.sem("scored")
        self.topped = ph.sem("topped")
        self.exped = ph.sem("exped")
        self.turned = ph.sem("turned")
        self.low_copied = ph.sem("low_copied")
        self.high_copied = ph.sem("high_copied")
        self.weighed = ph.sem("weighed")
        self.inverted = ph.sem("inverted")
        self.normed = ph.sem("normed")

    def count(self, b, n, previous=None):
        if isinstance(n, int) and previous is None:
            n = max(n, 0)
        return b * self.H + (n + 1)

    def others(self, eng, slot, b):
        with eng.Fori(1, self.H // 4) as r:
            for s in range(4):
                slot(b, 4 * r + s, s, 2 * r + s // 2, None)

    def all_batches(self, eng, slot, ready=None, after=None, end=None):
        def batch(b, previous):
            if ready is not None:
                ready(b)
            for i in range(self.H if self.H == 8 else 4):
                slot(b, i, i % 4, i // 2, previous)
                if after is not None:
                    after(b, i, previous)
            if self.H > 8:
                self.others(eng, slot, b)

        batch(0, None)
        with eng.Fori(0, B - 1) as b:
            batch(b + 1, b)
        for i in range(self.H, self.H + 3):
            slot(B - 1, i, i % 4, i // 2, None)
        if end is not None:
            end()

    def has(self, i, back, previous):
        return not isinstance(i, int) or (i - back < self.H and (i >= back or previous is not None))

    def head(self, b, i, back, previous):
        return (previous, i - back + self.H) if isinstance(i, int) and i < back else (b, i - back)


def opened(eng, *sems, by=1):
    for s in sems:
        eng.sem_inc(s, by)


def nothing(*args):
    pass


def queries_slot(pool, m, a, before=nothing, more=nothing):
    nq = a.T * a.rows

    def slot(b, i, place, j, previous):
        if place % 2 == 0 and a.has(i, 0, previous):
            before(b, j)
            pool.wait_ge(a.scored, a.count(b, i - 2, previous))
            pool.tensor_tensor(m.q_head[:, place:place + 2, 0:nq], a.queries(b, j).broadcast_to([P, 2, nq]),
                               each(a.scale[:, 0:2], nq), ALU.mult).then_inc(a.head_ready, 2)
            more(b, place, j)

    return slot


TERMS = ((0, 0), (0, 1), (0, 2), (1, 0), (1, 1), (2, 0))


def stack_sync(sp, m, a, b, two, part_ready, stacked, with_mask):
    per = 2 if a.dh == 8 else 1
    rows, chunks = C // per, a.H // per
    nq = a.T * a.rows
    sp.wait_ge(part_ready, b + 1)
    for s in range(per):
        for n, (qp, kp) in enumerate(TERMS):
            at = s * (P // per) + n * a.dh
            src = m.qk_part[s * rows:(s + 1) * rows, kp, 0:a.NK]
            sp.dma_start(m.kS[at:at + a.dh, two, 0:chunks, 0:a.NK],
                         src).then_inc(stacked, 16)
            src = m.qk_part[s * rows:(s + 1) * rows, qp, a.NK:a.NK + nq]
            sp.dma_start(m.qS[at:at + a.dh, two, s:a.H:per, 0:nq], src).then_inc(stacked, 16)
        if with_mask:
            at = s * (P // per) + len(TERMS) * a.dh
            dst = m.kS[at:at + 3, two, 0:chunks, 0:a.NK]
            src = m.key_mask[0:3, ds(batch_of(b) * SK, SK)].unsqueeze(1).broadcast_to([3, chunks, SK])
            sp.dma_start(dst, src).then_inc(stacked, 16)


def split_pool(pool, m, n, steps, part_ready):
    x, rest, part = m.qk[:, 0:n], m.qk_rest[:, 0:n], m.qk_part[:, :, 0:n]
    one = m.ones[:, 0:1].broadcast_to([P, n])
    steps.done(pool.tensor_tensor(part[:, 0, :], x, one, ALU.mult))
    steps.done(pool.tensor_tensor(rest, x, part[:, 0, :], ALU.subtract))
    steps.done(pool.tensor_tensor(part[:, 1, :], rest, one, ALU.mult))
    pool.tensor_tensor(part[:, 2, :], rest, part[:, 1, :], ALU.subtract).then_inc(part_ready, 1)


def batch_of(b):
    return b % B


def attention_pe(pe, m, a, more=nothing):
    rows = a.rows

    def stacked_scores(b, i, s, j, previous):
        pe.wait_ge(a.exped if a.mask is None else a.topped, a.count(b, i - 1, previous))
        two = b & 1
        chunk = j if a.dh == 8 else i
        k = m.kS[:, ds(two, 1), ds(chunk, 1), 0:a.NK]
        for t in range(a.T):
            out = m.pS[:, s:s + 1, t * a.NK:(t + 1) * a.NK]
            if a.causal:
                pe.matmul(out, m.identb[:, :], m.allowed[:, t, :], start=True, stop=False)
            last = pe.matmul(out, m.qS[:, ds(two, 1), ds(i, 1), t * P:(t + 1) * P], k, start=not a.causal, stop=True)
        last.then_inc(a.scored, 1)

    def scores(b, i, s, j, q, previous):
        pe.wait_ge(a.head_ready, a.count(b, i + 1, previous))
        pe.wait_ge(a.exped if a.mask is None else a.topped, a.count(b, i - 1, previous))
        k = a.keys(b, j)
        for t in range(a.T):
            out = m.pS[:, s:s + 1, t * a.NK:(t + 1) * a.NK]
            last = pe.matmul(out, m.q_head[:, q, t * P:t * P + rows], k, start=True, stop=True)
        last.then_inc(a.scored, 1)

    def weigh(b, i, s, batch, head, previous):
        if not a.one_bank:
            pe.wait_ge(a.low_copied, a.count(b, i - 2, previous))
        pe.wait_ge(a.high_copied, a.count(b, i - 2, previous))
        pe.wait_ge(a.normed, a.count(b, i - 3, previous))
        for t in range(a.T):
            for c in range(a.KC):
                v = (a.values(batch, c, head) if a.paired
                     else m.v_narrow[:, ds(batch & 1, 1), c, ds(head * a.dh, a.dh)])
                last = pe.matmul(m.pO[0:rows, s, t, 0:a.dh], m.probT[:, s, c, t * P:t * P + rows], v, start=c == 0,
                                 stop=c == a.KC - 1)
        last.then_inc(a.weighed, 1)

    def turn(b, i, s, previous):
        pe.wait_ge(a.exped, a.count(b, i, previous))
        if not a.one_bank:
            pe.wait_ge(a.low_copied, a.count(b, i - 1, previous))
        pe.wait_ge(a.high_copied, a.count(b, i - 1, previous))
        half = a.KC // 2
        for c in range(a.KC):
            for t in range(a.T):
                bank, c_ = (0, c) if a.one_bank else (c // half, c % half)
                at = (c_ * a.T + t) * P
                last = pe.transpose(m.pT[:, bank, at:at + P],
                                    m.prob[:, s, t * a.NK + c * P:t * a.NK + (c + 1) * P], m.k["ident"])
        last.then_inc(a.turned, 1)

    def slot(b, i, place, j, previous):
        s = place % 2
        if a.has(i, 0, previous):
            scores(b, i, s, j, place, previous) if a.paired else stacked_scores(b, i, s, j, previous)
        more(0, b, i, place, j, previous)
        if a.has(i, 3, previous):
            weigh(b, i, 1 - s, *a.head(b, i, 3, previous), previous)
        more(1, b, i, place, j, previous)
        if a.has(i, 1, previous):
            turn(b, i, 1 - s, previous)
        more(2, b, i, place, j, previous)
        for _ in range(a.warm):
            pe.matmul(m.banks[:, 3, 0:P], m.onesb[:, :], m.onesb[:, :], start=True, stop=True)

    return slot


def turned_half(m, a, s, half):
    nq, n = a.T * a.rows, a.KC // 2
    if a.one_bank:
        return m.probT[:, s, 0:a.KC, 0:nq], m.pT[:, 0, :].rearrange("p (c q) -> p c q", q=nq)
    return (m.probT[:, s, half * n:(half + 1) * n, 0:nq],
            m.pT[:, half, 0:n * a.T * P].rearrange("p (c q) -> p c q", q=a.T * P)[:, :, 0:nq])


def attention_act(act, m, a, more=nothing):

    def slot(b, i, place, j, previous):
        s = place % 2
        if a.has(i, 0, previous):
            act.wait_ge(a.topped, a.count(b, i + 1, previous))
            act.wait_ge(a.turned, a.count(b, i - 1, previous))
            scores = m.pS if a.mask is None else m.prob
            for t in range(a.T):
                last = act.activation(m.prob[0:a.rows, s, t * a.NK:(t + 1) * a.NK],
                                      scores[0:a.rows, s, t * a.NK:(t + 1) * a.NK], ACT.Exp,
                                      scale=1.0 if a.mask is None else -1.0, bias=m.top[0:a.rows, s, t:t + 1],
                                      accum_out=m.total[0:a.rows, ds(i, 1), t:t + 1])
            last.then_inc(a.exped, 1)
        more(1, b, i, place, j, previous)
        if a.has(i, 1, previous):
            act.wait_ge(a.turned, a.count(b, i, previous))
            act.wait_ge(a.weighed, a.count(b, i - 2, previous))
            dst, src = turned_half(m, a, 1 - s, 1)
            act.activation(dst, src, ACT.Copy).then_inc(a.high_copied, 1)
        more(2, b, i, place, j, previous)

    return slot


def attention_dve(dve, m, a, out, more=nothing):

    def maximum(s):
        dve.tensor_reduce(m.top[0:a.rows, s, 0:a.T],
                          m.pS[0:a.rows, s, 0:a.T * a.NK].rearrange("p (t k) -> p t k", k=a.NK),
                          AX_X, ALU.max, negate=True).then_inc(a.topped, 1)

    def masked_maximum(b, i, s, previous):
        dve.wait_ge(a.turned, a.count(b, i - 1, previous))
        if a.mask_by_batch and isinstance(i, int) and i == 0:
            dve.wait_ge(a.mask_ready, b + 1)
        dve.memset(m.carrier[:, s:s + 1], 0.0)
        for t in range(a.T):
            last = dve.tensor_tensor_reduce(m.prob[:, s, t * a.NK:(t + 1) * a.NK], m.pS[:, s, t * a.NK:(t + 1) * a.NK],
                                            a.mask(t), -1.0, 3.0e38, ALU.add, ALU.min,
                                            accum_out=m.top[:, s, t:t + 1])
        last.then_inc(a.topped, 1)

    def slot(b, i, place, j, previous):
        s = place % 2
        if a.has(i, 0, previous):
            dve.wait_ge(a.scored, a.count(b, i + 1, previous))
            if a.mask is not None:
                masked_maximum(b, i, s, previous)
            else:
                maximum(s)
        more(0, b, i, place, j, previous)
        if a.has(i, 3, previous):
            batch, head = a.head(b, i, 3, previous)
            dve.wait_ge(a.weighed, a.count(b, i - 2, previous))
            dve.wait_ge(a.inverted, a.count(b, i - 2, previous))
            for t in range(a.T):
                last = dve.tensor_scalar(out(batch, t, head, (place + 1) % 4), m.pO[0:a.rows, 1 - s, t, 0:a.dh],
                                         m.inverse[0:a.rows, ds(head, 1), t:t + 1], None, ALU.mult)
            last.then_inc(a.normed, 1)
        more(1, b, i, place, j, previous)
        if a.has(i, 1, previous):
            _, head = a.head(b, i, 1, previous)
            dve.wait_ge(a.turned, a.count(b, i, previous))
            dve.reciprocal(m.inverse[0:a.rows, ds(head, 1), 0:a.T],
                           m.total[0:a.rows, ds(head, 1), 0:a.T]).then_inc(a.inverted, 1)
            if not a.one_bank:
                dve.wait_ge(a.weighed, a.count(b, i - 2, previous))
                dst, src = turned_half(m, a, 1 - s, 0)
                dve.tensor_copy(dst, src).then_inc(a.low_copied, 1)
        more(2, b, i, place, j, previous)

    return slot


class Preparation:

    PIECES = 3

    def __init__(self, ph, a, columns):
        self.a, self.columns = a, columns
        self.copied = ph.sem("copied")
        self.made = ph.sem("piece_made")
        self.taken = ph.sem("piece_taken")
        self.part_ready = ph.sem("part_ready")
        self.pool_steps = ph.sem("pool_steps")
        self.stacked = ph.sem("stacked")
        self.masked = False

    def per_batch(self):
        per = 2 if self.a.dh == 8 else 1
        return 16 * per * (2 * len(TERMS) + (1 if self.masked else 0))

    def first(self, piece):
        for n in range(self.PIECES):
            piece(n, 0)

    def after(self, piece, finish=None):
        def work(b, i, previous):
            if i < self.PIECES:
                piece(i, b + 1)
            if i == 2 and finish is not None and previous is not None:
                finish(previous)
        return work


def narrow_pool(pool, m, a, p, sources):
    opened(pool, p.copied)

    def prepare_batch(b):
        for dst, src, n in sources:
            last = pool.tensor_copy(dst, src[:, ds(batch_of(b) * n, n)])
        last.then_inc(p.copied, 1)
        pool.wait_ge(p.taken, 3 * b + 3)
        split_pool(pool, m, p.columns, Steps(pool, p.pool_steps, base=3 * b), p.part_ready)

    prepare_batch(0)
    with pool.Fori(0, B) as b:
        pool.wait_ge(p.made, 3 * b + 3)
        prepare_batch(b + 1)


def narrow_sync(sp, m, a, p):
    extra = 0
    if p.masked:
        for two in range(2):
            for s in range(2):
                at = s * 64 + len(TERMS) * a.dh
                for t in range(a.T):
                    sp.dma_start(m.qS[at:at + 3, two, s:a.H:2, t * P:(t + 1) * P],
                                 row(m.onesb[:, :], a.H // 2)[0:3]).then_inc(p.stacked, 16)
                    extra += 16
    stack_sync(sp, m, a, 0, 0, p.part_ready, p.stacked, p.masked)
    with sp.Fori(0, B // 2) as pair:
        stack_sync(sp, m, a, 2 * pair + 1, 1, p.part_ready, p.stacked, p.masked)
        stack_sync(sp, m, a, 2 * pair + 2, 0, p.part_ready, p.stacked, p.masked)
    sp.wait_ge(p.stacked, extra + (B + 1) * p.per_batch())


def narrow_pe(pe, m, a, p, piece, finish=None):
    opened(pe, a.scored, a.turned, a.weighed)
    extra = 16 * 4 * a.T if p.masked else 0

    def ready(b):
        pe.wait_ge(p.stacked, (b + 1) * p.per_batch() + extra)
        pe.wait_ge(p.taken, 3 * b + 4)

    p.first(piece)
    a.all_batches(pe, attention_pe(pe, m, a), ready, p.after(piece, finish),
                  None if finish is None else lambda: finish(B - 1))


def cross_phase(nc, m, name, w, heads, with_q=False, mask=False, fetch=None):
    scale = 1.0 / float(C if with_q else C // heads) ** 0.5
    with Phase(nc, name) as ph:
        a = Attention(ph, heads, C // heads, SK)
        p = Preparation(ph, a, SK + S)
        p.masked = mask
        G, fetched = m.pG, None if fetch is None else ph.sem("fetched")

        @ph.block.sync
        def _(sp):
            narrow_sync(sp, m, a, p)

        @ph.block.gpsimd
        def _(pool):
            if fetch is not None:
                pool.dma_start(*fetch).then_inc(fetched, 16)
            narrow_pool(pool, m, a, p, ((m.ctx_now[:, :], m.ctxT, SK), (m.x_now[:, :], m.hT, S)))
            if fetch is not None:
                pool.wait_ge(fetched, 16)

        @ph.block.tensor
        def _(pe):
            def piece(n, b):
                pe.wait_ge(p.taken, 3 * b + n + 1)
                if n == 0:
                    last = pe.matmul(G[:, :], w["wk"], m.ctxT[:, ds(batch_of(b) * SK, SK)], start=True, stop=True)
                if n == 1:
                    last = pe.matmul(G[:, 0:S], w["wq"], m.hT[:, ds(batch_of(b) * S, S)], start=True, stop=True)
                    pe.wait_ge(p.copied, b + 2)
                    if with_q:
                        for t in range(QT):
                            last = pe.matmul(G[:, S + t * P:S + (t + 1) * P], m.x_now[:, t * P:(t + 1) * P],
                                             w["wq_plain"], start=True, stop=True)
                if n == 2:
                    for t in range(KT):
                        last = pe.matmul(G[:, t * P:(t + 1) * P], m.ctx_now[:, t * P:(t + 1) * P], w["wv"],
                                         start=True, stop=True)
                last.then_inc(p.made, 1)

            narrow_pe(pe, m, a, p, piece)

        @ph.block.scalar
        def _(act):
            opened(act, a.exped, a.high_copied)

            def piece(n, b):
                if n == 0:
                    act.wait_ge(p.made, 3 * b + 1)
                    act.activation(m.qk[:, 0:SK], G[:, :], ACT.Identity, bias=w["bk"]).then_inc(p.taken, 1)

            p.first(piece)
            a.all_batches(act, attention_act(act, m, a), None, p.after(piece))

        @ph.block.vector
        def _(dve):
            opened(dve, a.topped, a.normed, a.low_copied, a.inverted, p.taken)

            def piece(n, b):
                if n == 1:
                    dve.wait_ge(p.made, 3 * b + 2)
                    last = dve.tensor_scalar(m.qk[:, SK:SK + S], G[:, 0:S], w["bq"], scale, ALU.add, ALU.mult)
                    if with_q:
                        last = dve.tensor_tensor(m.h[:, ds(batch_of(b) * QT, QT), :],
                                                 G[:, S:2 * S].rearrange("p (t c) -> p t c", c=C),
                                                 row(w["bq_row"], QT), ALU.add)
                    last.then_inc(p.taken, 1)
                if n == 2:
                    dve.wait_ge(p.made, 3 * b + 3)
                    two = b & 1
                    dve.tensor_tensor(m.v_narrow[:, ds(two, 1), :, :].rearrange("p a t c -> p (a t) c"),
                                      G[:, :].rearrange("p (t c) -> p t c", c=C), row(w["bv_row"], KT),
                                      ALU.add).then_inc(p.taken, 1)

            p.first(piece)
            slot = attention_dve(dve, m, a, lambda b, t, h, _: m.o[:, ds(b * QT + t, 1), ds(h * a.dh, a.dh)])
            a.all_batches(dve, slot, None, p.after(piece))


def project_pe(pe, m, weight, ready, turned, out_ready):
    if ready is not None:
        pe.wait_ge(*ready)
    turn_pe(pe, m, m.o, turned)
    pe.wait_ge(out_ready[0], 4)
    for g in range(4):
        for t in range(4):
            last = pe.matmul(m.banks[:, g, t * P:(t + 1) * P], m.hT[:, (4 * g + t) * P:(4 * g + t + 1) * P],
                             weight, start=True, stop=True)
        last.then_inc(out_ready[1], 1)


def l0_xattn_finish(nc, m, w):
    with Phase(nc, "L0x_finish") as ph:
        steps, turned, copied, projected = (ph.sem(n) for n in ("steps", "turned", "copied", "projected"))
        norm = Normalization(ph)

        @ph.block.vector
        def _(dve):
            st = Steps(dve, steps)
            st.done(dve.tensor_tensor(wide(m.o), wide(m.o), wide(m.h), ALU.add))
            norm.dve(dve, m, 1, m.o, m.o, 1e-5)
            norm.scale_dve(dve, m, 1, st, m.o[:, :, :], w["g0_row"], w["b0_row"])
            turn_out_dve(dve, m, m.hT, turned, copied)
            for g in range(4):
                dve.wait_ge(projected, g + 1)
                st.done(dve.tensor_tensor(m.h[:, 4 * g:4 * g + 4, :],
                                          m.banks[:, g, :].rearrange("p (t c) -> p t c", c=C),
                                          row(w["bo_row"], 4), ALU.add))
            st.done(dve.scalar_tensor_tensor(out=wide(m.o), in0=wide(m.h), scalar=0.0, in1=wide(m.o),
                                             op0=ALU.max, op1=ALU.add))
            norm.dve(dve, m, 2, m.o, m.o, 1e-5)
            norm.scale_dve(dve, m, 2, st, m.o[:, :, :], w["g1_row"], w["b1_row"])
            st.done(dve.tensor_tensor(wide(m.x), wide(m.x), wide(m.o), ALU.add))

        @ph.block.scalar
        def _(act):
            norm.act(act, m, 1, m.o, m.o)
            turn_out_act(act, m, m.hT, turned, copied)
            norm.act(act, m, 2, m.o, m.o)

        @ph.block.tensor
        def _(pe):
            project_pe(pe, m, w["wo"], (steps, 3), turned, (copied, projected))


def xattn_finish(nc, m, name, w, x, bias=True):
    with Phase(nc, name + "_finish") as ph:
        steps, turned, copied, projected = (ph.sem(n) for n in ("steps", "turned", "copied", "projected"))

        @ph.block.vector
        def _(dve):
            st = Steps(dve, steps)
            if bias:
                st.done(dve.tensor_tensor(x[:, :, :], x[:, :, :], row(w["bo_row"], TILES), ALU.add))
            turn_out_dve(dve, m, m.hT, turned, copied)
            for g in range(4):
                dve.wait_ge(projected, g + 1)
                st.done(dve.tensor_tensor(wide(x[:, 4 * g:4 * g + 4, :]), wide(x[:, 4 * g:4 * g + 4, :]),
                                          m.banks[:, g, :], ALU.add))

        @ph.block.scalar
        def _(act):
            turn_out_act(act, m, m.hT, turned, copied)

        @ph.block.tensor
        def _(pe):
            project_pe(pe, m, w["wo"], None, turned, (copied, projected))


def key_mask_phase(nc, m, name, mask, boolean):
    n = B * SK // P
    with Phase(nc, name + "_mask") as ph:
        loaded, steps, stored = ph.sem("loaded"), ph.sem("steps"), ph.sem("stored")
        here = m.mask_u8 if boolean else m.mask_in
        parts = 1 if boolean else 3

        @ph.block.sync
        def _(sp):
            sp.dma_start(here[:, :], mask.rearrange("a (p n) -> (a p) n", n=n)).then_inc(loaded, 16)
            sp.wait_ge(steps, 3 if boolean else 7)
            for i in range(parts):
                sp.dma_start(m.key_mask[i:i + 1, :], m.mask_part[:, i, :]).then_inc(stored, 16)
            sp.wait_ge(stored, 16 * parts)

        if boolean:
            spread, even_copied, odd_copied = ph.sem("spread"), ph.sem("even_copied"), ph.sem("odd_copied")
            groups = [m.key_mask[:, n * SK:(n + 1) * SK] for n in range(B)]

            @ph.block.tensor
            def _(pe):
                pe.wait_ge(stored, 16)
                for n, group in enumerate(groups):
                    if n >= 4:
                        pe.wait_ge(odd_copied if n % 2 else even_copied, n // 2 - 1)
                    pe.matmul(m.banks[:, n % 4, :], m.onesb[:, :], group, start=True, stop=True).then_inc(spread, 1)

            @ph.block.scalar
            def _(act):
                for n in range(0, B, 2):
                    act.wait_ge(spread, n + 1)
                    act.activation(groups[n], m.banks[:, n % 4, :], ACT.Copy).then_inc(even_copied, 1)

        @ph.block.vector
        def _(dve):
            st = Steps(dve, steps)
            part, rest = m.mask_part, m.mask_rest
            dve.wait_ge(loaded, 16)
            if boolean:
                dve.memset(m.key_mask[:, :], 0.0)
                st.done(dve.tensor_copy(m.mask_in[:, :], m.mask_u8[:, :]))
                st.done(dve.reciprocal(rest[:, 0, :], m.mask_in[:, :]))
                st.done(dve.tensor_scalar(part[:, 0, :], rest[:, 0, :], -1.0, 1.0, ALU.mult, ALU.add))
                for n in range(1, B, 2):
                    dve.wait_ge(spread, n + 1)
                    dve.tensor_copy(groups[n], m.banks[:, n % 4, :]).then_inc(odd_copied, 1)
            else:
                st.done(dve.tensor_scalar(rest[:, 1, :], m.mask_in[:, :], -1.0, 1.0, ALU.mult, ALU.add))
                st.done(dve.tensor_scalar(rest[:, 0, :], rest[:, 1, :], -10000.0, None, ALU.mult))
                st.done(dve.tensor_copy(part[:, 0, :], rest[:, 0, :]))
                st.done(dve.tensor_tensor(rest[:, 1, :], rest[:, 0, :], part[:, 0, :], ALU.subtract))
                st.done(dve.tensor_copy(part[:, 1, :], rest[:, 1, :]))
                st.done(dve.tensor_tensor(rest[:, 2, :], rest[:, 1, :], part[:, 1, :], ALU.subtract))
                st.done(dve.tensor_copy(part[:, 2, :], rest[:, 2, :]))


def moe_phase(nc, m, name, x, experts, sizes, func, weighted, biases=None, row_bias=None, fetch=None):
    E, PIECES = len(experts), len(sizes)
    units = E * PIECES
    gated, hidden, prod = m.prob, m.probT[:, :, :, :].rearrange("p s c q -> p s (c q)"), m.banks
    with Phase(nc, name) as ph:
        expanded = ph.sem("expanded")
        activated = ph.sem("activated")
        multiplied = ph.sem("multiplied")
        contracted = ph.sem("contracted")
        combined = ph.sem("combined")
        biased = ph.sem("biased")
        fetch_sync(ph, fetch)

        @ph.block.tensor
        def _(pe):
            opened(pe, contracted)
            with pe.Fori(0, GROUPS) as g:
                def expand(n):
                    gate, up, _ = experts[n // PIECES]
                    size, s = sizes[n % PIECES], n % 2
                    pe.wait_ge(multiplied, g * units + 1 + max(n - 1, 0))
                    moving = m.hT[:, ds(g * GROUP, GROUP)]
                    pe.matmul(prod[0:size, s, :], gate(n % PIECES), moving, start=True, stop=True)
                    pe.matmul(prod[0:size, 2 + s, :], up(n % PIECES), moving, start=True,
                              stop=True).then_inc(expanded, 1)

                def contract(n):
                    e, i, s = n // PIECES, n % PIECES, n % 2
                    size, down = sizes[i], experts[e][2]
                    pe.wait_ge(multiplied, g * units + n + 2)
                    if i == 0:
                        pe.wait_ge(combined, g * E + 1 + max(e - 1, 0))
                    for t in range(GT):
                        last = pe.matmul(m.pT[:, e % 2, t * C:(t + 1) * C], hidden[0:size, s, t * P:(t + 1) * P],
                                         down(i), start=i == 0 and t == 0, stop=i == PIECES - 1,
                                         skip_group_check=True)
                    last.then_inc(contracted, 1)

                for n in range(units):
                    expand(n)
                    if n:
                        contract(n - 1)
                contract(units - 1)

        @ph.block.scalar
        def _(act):
            with act.Fori(0, GROUPS) as g:
                for n in range(units):
                    size, s = sizes[n % PIECES], n % 2
                    act.wait_ge(expanded, g * units + n + 1)
                    act.wait_ge(multiplied, g * units + 1 + max(n - 1, 0))
                    bias = 0.0 if biases is None else biases[1][0:size, n:n + 1]
                    act.activation(gated[0:size, s, 0:GROUP], prod[0:size, s, :], func,
                                   bias=bias).then_inc(activated, 1)

        @ph.block.vector
        def _(dve):
            opened(dve, multiplied, combined)
            if row_bias is not None:
                dve.tensor_tensor(x[:, :, :], x[:, :, :], row(row_bias, TILES), ALU.add).then_inc(biased, 1)
                dve.wait_ge(biased, 1)
            with dve.Fori(0, GROUPS) as g:
                def multiply(n):
                    size, s = sizes[n % PIECES], n % 2
                    dve.wait_ge(activated, g * units + n + 1)
                    dve.wait_ge(contracted, g * units + 1 + max(n - 1, 0))
                    if biases is None:
                        ins = dve.tensor_tensor(hidden[0:size, s, 0:GROUP], gated[0:size, s, 0:GROUP],
                                                prod[0:size, 2 + s, :], ALU.mult)
                    else:
                        ins = dve.scalar_tensor_tensor(out=hidden[0:size, s, 0:GROUP], in0=prod[0:size, 2 + s, :],
                                                       scalar=biases[0][0:size, n:n + 1],
                                                       in1=gated[0:size, s, 0:GROUP], op0=ALU.add, op1=ALU.mult)
                    ins.then_inc(multiplied, 1)

                def combine(e):
                    dve.wait_ge(contracted, g * units + (e + 1) * PIECES + 1)
                    dve.wait_ge(combined, g * E + e + 1)
                    here = x[:, ds(g * GT, GT), :]
                    if weighted[e] is None:
                        last = dve.tensor_tensor(here, here, m.pT[:, e % 2, :].rearrange("p (t c) -> p t c", c=C),
                                                 ALU.add)
                    else:
                        for t in range(GT):
                            tile = x[:, ds(g * GT + t, 1), :]
                            last = dve.scalar_tensor_tensor(
                                out=tile, in0=m.pT[:, e % 2, t * C:(t + 1) * C].unsqueeze(1),
                                scalar=m.weight[:, ds(g * GT + t, 1), weighted[e]:weighted[e] + 1], in1=tile,
                                op0=ALU.mult, op1=ALU.add)
                    last.then_inc(combined, 1)

                for n in range(units):
                    multiply(n)
                    if n >= PIECES and n % PIECES == 0:
                        combine(n // PIECES - 1)
                combine(E - 1)


def route_phase(nc, m, name, router, experts, keep, bias=None, softmax=True, eps=None):
    E = experts
    with Phase(nc, name + "_route") as ph:
        steps, scored, shifted, exped = ph.sem("steps"), ph.sem("scored"), ph.sem("shifted"), ph.sem("exped")
        p, wt = m.scores16[:, :, 0:E], m.weight[:, :, 0:E]
        logits = m.pG[:, 0:TILES * E].rearrange("p (t e) -> p t e", e=E)
        more = m.prob[:, :, :].rearrange("p s n -> p (s n)")[:, 0:TILES * E * E].rearrange(
            "p (t e f) -> p t e f", e=E, f=E)
        same = m.probT[:, :, :, :].rearrange("p s c q -> p (s c q)")[:, 0:TILES * E * E].rearrange(
            "p (t e f) -> p t e f", e=E, f=E)

        @ph.block.tensor
        def _(pe):
            for t in range(TILES):
                last = pe.matmul(m.pG[:, t * E:(t + 1) * E], m.hT[:, t * P:(t + 1) * P], router, start=True, stop=True)
            last.then_inc(scored, 1)

        @ph.block.scalar
        def _(act):
            if softmax:
                act.wait_ge(shifted, 1)
                act.activation(p, p, ACT.Exp).then_inc(exped, 1)

        @ph.block.vector
        def _(dve):
            st = Steps(dve, steps)
            dve.wait_ge(scored, 1)
            if bias is None:
                st.done(dve.tensor_copy(p, logits))
            else:
                st.done(dve.tensor_tensor(p, logits, row(bias, TILES), ALU.add))
            if softmax:
                st.done(dve.tensor_reduce(m.sum[:, :], p, AX_X, ALU.max))
                dve.tensor_tensor(p, p, each(m.sum[:, :], E), ALU.subtract).then_inc(shifted, 1)
                dve.wait_ge(exped, 1)
                st.done(dve.tensor_reduce(m.var[:, :], p, AX_X, ALU.add))
                st.done(dve.reciprocal(m.rstd[:, :], m.var[:, :]))
                st.done(dve.tensor_tensor(p, p, each(m.rstd[:, :], E), ALU.mult))
            other = p.unsqueeze(2).broadcast_to([P, TILES, E, E])
            before = m.k["before"].rearrange("p (e f) -> p e f", f=8)[:, 0:E, 0:E].unsqueeze(1).broadcast_to(
                [P, TILES, E, E])
            st.done(dve.tensor_tensor(more, other, each(p, E), ALU.is_gt))
            st.done(dve.tensor_tensor(same, other, each(p, E), ALU.is_equal))
            st.done(dve.tensor_tensor(same, same, before, ALU.mult))
            st.done(dve.tensor_tensor(more, more, same, ALU.add))
            st.done(dve.tensor_reduce(m.rank[:, :, 0:E], more, AX_X, ALU.add))
            if not softmax:
                st.done(dve.tensor_scalar(wt, m.rank[:, :, 0:E], keep - 0.5, None, ALU.is_lt))
                return
            st.done(dve.tensor_scalar(m.rank[:, :, 0:E], m.rank[:, :, 0:E], keep - 0.5, None, ALU.is_lt))
            st.done(dve.tensor_tensor(wt, m.rank[:, :, 0:E], p, ALU.mult))
            st.done(dve.tensor_reduce(m.sum[:, :], wt, AX_X, ALU.add))
            if eps is not None:
                st.done(dve.tensor_scalar(m.sum[:, :], m.sum[:, :], eps, None, ALU.add))
            st.done(dve.reciprocal(m.rstd[:, :], m.sum[:, :]))
            st.done(dve.tensor_tensor(wt, wt, each(m.rstd[:, :], E), ALU.mult))


def laid_side_by_side(w, hidden):
    n = len(pieces(hidden))

    def expert(e):
        def part(name):
            return lambda i: w[name][:, e * hidden + pieces(hidden)[i][0]:e * hidden + sum(pieces(hidden)[i])]

        def down(i):
            return w["down"][0:pieces(hidden)[i][1], (e * n + i) * C:(e * n + i + 1) * C]
        return part("gate"), part("up"), down
    return expert


def affine_phase(nc, m, name, src, dst, scale, shift, back=False, columns=None):
    with Phase(nc, name) as ph:
        steps, turned, copied = ph.sem("steps"), ph.sem("turned"), ph.sem("copied")
        norm = Normalization(ph)
        first = 4 if back else 0
        flat = wide(dst)

        @ph.block.vector
        def _(dve):
            st = Steps(dve, steps)
            if back:
                turn_out_dve(dve, m, flat, turned, copied)
                dve.wait_ge(copied, 4)
            norm.dve(dve, m, 1, src, dst, 1e-5)
            if scale is not None:
                norm.scale_dve(dve, m, 1, st, dst[:, :, :], scale, shift)
            for g in (1, 3):
                dve.wait_ge(turned, first + g + 1)
                if columns is None:
                    dve.tensor_copy(m.hT[:, g * 512:(g + 1) * 512], m.banks[:, g, :])
                else:
                    dve.tensor_scalar(m.hT[:, g * 512:(g + 1) * 512], m.banks[:, g, :], columns[0], columns[1],
                                      ALU.mult, ALU.add)

        @ph.block.scalar
        def _(act):
            if back:
                turn_out_act(act, m, flat, turned, copied)
            norm.act(act, m, 1, src, dst)
            for g in (0, 2):
                act.wait_ge(turned, first + g + 1)
                if columns is None:
                    act.activation(m.hT[:, g * 512:(g + 1) * 512], m.banks[:, g, :], ACT.Copy)
                else:
                    act.activation(m.hT[:, g * 512:(g + 1) * 512], m.banks[:, g, :], ACT.Identity,
                                   scale=columns[0], bias=columns[1])

        @ph.block.tensor
        def _(pe):
            if back:
                turn_pe(pe, m, m.hT[:, :].rearrange("p (t c) -> p t c", c=P), turned)
            if scale is None:
                norm.wait(pe, 1)
            else:
                pe.wait_ge(steps, 2)
            turn_pe(pe, m, dst, turned)


def shift_phase(nc, m, name, y, w):
    half = C // 2
    with Phase(nc, name) as ph:
        turned, cleared = ph.sem("turned"), ph.sem("cleared")
        shifted = m.hT[half:C, :].rearrange("p (b s) -> p b s", s=S)

        @ph.block.gpsimd
        def _(pool):
            pool.memset(shifted[:, :, 0:1], 0.0).then_inc(cleared, 1)
            pool.wait_ge(cleared, 1)
            if w is not None:
                for n, (scale, cos, sin) in enumerate(((w["qs_row"], "xq_cos", "xq_sin"),
                                                       (w["ks_row"], "xk_cos", "xk_sin"))):
                    c = w[cos].rearrange("p (t d) -> p t d", d=WIDE)
                    s = w[sin].rearrange("p (t d) -> p t d", d=WIDE)
                    at = slice(2 * n, 2 * n + 2)
                    h = WIDE // 2
                    pool.tensor_tensor(m.turn_cos[:, at, :], c, row(scale, QT), ALU.mult)
                    pool.tensor_tensor(m.turn_sin[:, at, 0:h], s[:, :, 0:h], row(scale[:, h:WIDE], QT), ALU.mult)
                    pool.tensor_tensor(m.turn_sin[:, at, h:WIDE], s[:, :, h:WIDE], row(scale[:, 0:h], QT), ALU.mult)

        @ph.block.tensor
        def _(pe):
            turn_pe(pe, m, y, turned)

        def move(g, copy):
            bank = m.banks[:, g, :].rearrange("p (b s) -> p b s", s=S)
            copy(m.hT[0:half, g * 512:(g + 1) * 512], m.banks[0:half, g, :])
            copy(shifted[:, 2 * g:2 * g + 2, 1:S], bank[half:C, :, 0:S - 1])

        @ph.block.scalar
        def _(act):
            for g in (0, 2):
                act.wait_ge(turned, g + 1)
                move(g, lambda dst, src: act.activation(dst, src, ACT.Copy))

        @ph.block.vector
        def _(dve):
            for g in (1, 3):
                dve.wait_ge(turned, g + 1)
                move(g, lambda dst, src: dve.tensor_copy(dst, src))


def local_phase(nc, m, name, w, y, fetch=None):
    CH, W = CHUNKS_L0F, CHUNKS_L0F * P
    h = WIDE // 2
    with Phase(nc, name) as ph:
        a = Attention(ph, L0F_HEADS, WIDE, S, w["scale"], mask=lambda t: w["band"][:, t * S:(t + 1) * S])
        copied = ph.sem("copied")
        rooted = ph.sem("rooted")
        bounded = ph.sem("bounded")
        inv_ready = ph.sem("inv_ready")
        o_copied = ph.sem("o_copied")
        o_turned = ph.sem("o_turned")
        oT_ready = ph.sem("oT_ready")
        out_mm = ph.sem("out_mm")
        added = ph.sem("added")
        qk_mm = ph.sem("qk_mm")
        values_mm = ph.sem("values_mm")
        split_off = ph.sem("split_off")
        values_ready = ph.sem("values_ready")
        summed = ph.sem("summed")
        rotated = ph.sem("rotated")
        joined = ph.sem("joined")
        scaled = ph.sem("scaled")
        qk_turned = ph.sem("qk_turned")
        queries_ready = ph.sem("queries_ready")
        keys_ready = ph.sem("keys_ready")
        flat_q, flat_k, flat_v = (t[:, :, :].rearrange("p c n -> p (c n)") for t in (m.qT, m.kT, m.v))
        qT = flat_q.rearrange("p (two c n) -> p two c n", two=2, n=S)
        kT = flat_k[:, 0:2048].rearrange("p (two c n) -> p two c n", two=2, n=S)
        v = flat_v[:, 0:2048].rearrange("p (two t n) -> p two t n", two=2, n=W)
        raw = flat_v[:, 2048:4096].rearrange("p (t a n) -> p t a n", t=QT, n=W)
        squares = flat_k[:, 2048:3072]
        oT = flat_k[:, 3072:4096].rearrange("p (t n) -> p t n", n=W)
        swapped = m.key_mask[:, :].bitcast(F32).rearrange("p (t a n) -> p t a n", t=QT, n=W)
        rotating = wide(m.h).rearrange("p (t a n) -> p t a n", t=QT, n=W)
        o = wide(m.o).rearrange("p (two t n) -> p two t n", two=2, n=W)
        o_all = wide(m.o).rearrange("p (two n) -> p two n", two=2)
        free = max(width(XW["L0x"]), width(XW["L1x"]))
        o_flat = m.xw[:, free:free + QT * W]
        o_now = o_flat.rearrange("p (t n) -> p t n", n=W)
        bankq, bankk, bankv, G = m.banks[:, 1, :], m.banks[:, 3, :], m.pT[:, 1, :], m.pG
        a.queries = lambda b, j: qT[:, ds(b & 1, 1), ds(j, 1), :].rearrange("p two c n -> p (two c) n")
        a.keys = lambda b, j: kT[:, ds(b & 1, 1), ds(j, 1), :]
        a.values = lambda b, c, head: v[:, ds(b & 1, 1), c, ds(head * WIDE, WIDE)]
        fetch_sync(ph, fetch)

        def done(b, t, back=0):
            return 2 * b + (t + 3 - back)

        def batch_done(b, back=0):
            return b + (2 - back)

        def by_head(ap):
            return ap.rearrange("p a (h d) -> p a h d", d=WIDE)

        @ph.block.gpsimd
        def _(pool):
            opened(pool, a.head_ready, copied, o_copied)
            opened(pool, joined, scaled, by=2)
            one = m.ones[:, 0:1]

            def copy_in(b):
                pool.wait_ge(values_mm, done(b, 0, 1))
                pool.tensor_tensor(m.x_now[:, :], m.hT[:, ds(batch_of(b) * S, S)], one.broadcast_to([P, S]),
                                   ALU.mult).then_inc(copied, 1)

            def join(b, t):
                pool.wait_ge(rotated, done(b, t))
                pool.tensor_tensor(rotating[:, t], rotating[:, t], swapped[:, t], ALU.add).then_inc(joined, 1)

            def divide(b, t):
                pool.wait_ge(inv_ready, batch_done(b))
                pool.wait_ge(joined, done(b, t))
                heads = rotating[:, t].rearrange("p a (h d) -> p (a h) d", d=WIDE)
                inverse = m.inv_norm[:, 2 * t:2 * t + 2, :].rearrange("p a h -> p (a h)")
                pool.tensor_tensor(heads, heads, each(inverse, WIDE), ALU.mult).then_inc(scaled, 1)

            def copy_o(b):
                pool.wait_ge(a.normed, a.count(b, a.H))
                pool.wait_ge(o_turned, batch_done(b, 1))
                pool.tensor_tensor(o_flat.unsqueeze(1), o_all[:, ds(b & 1, 1), :],
                                   one.unsqueeze(1).broadcast_to([P, 1, QT * W]), ALU.mult).then_inc(o_copied, 1)

            def after(b, i, previous):
                if i == 4:
                    for step in (join, divide):
                        for t in range(QT):
                            step(b + 1, t)
                if i == 6:
                    if previous is not None:
                        copy_o(previous)
                    copy_in(b + 2)

            copy_in(0)
            for t in range(QT):
                join(0, t)
                divide(0, t)
            copy_in(1)
            a.all_batches(pool, queries_slot(pool, m, a), lambda b: pool.wait_ge(queries_ready, done(b, 1)), after,
                          lambda: copy_o(B - 1))

        @ph.block.tensor
        def _(pe):
            opened(pe, a.scored, a.turned, a.weighed)
            opened(pe, o_turned, out_mm)
            opened(pe, qk_mm, values_mm, qk_turned, by=2)

            def multiply_qk(b, t):
                pe.wait_ge(copied, batch_done(b))
                pe.wait_ge(split_off, done(b, t, 1))
                if t == 0:
                    pe.wait_ge(queries_ready, done(b, t, 1))
                    pe.wait_ge(keys_ready, done(b, t, 1))
                for n, bank in enumerate((bankq, bankk)):
                    last = pe.matmul(bank, m.x_now[:, t * P:(t + 1) * P], w["wqkv"][:, n * W:(n + 1) * W],
                                     start=True, stop=True)
                last.then_inc(qk_mm, 1)

            def multiply_v(b, t):
                pe.wait_ge(values_ready, done(b, t, 1))
                pe.matmul(bankv, m.x_now[:, t * P:(t + 1) * P], w["wqkv"][:, 2 * W:3 * W], start=True,
                          stop=True).then_inc(values_mm, 1)

            def turn_qk(b, t):
                pe.wait_ge(scaled, done(b, t))
                if t == 0:
                    pe.wait_ge(split_off, done(b, 1))
                else:
                    pe.wait_ge(queries_ready, done(b, 0))
                    pe.wait_ge(keys_ready, done(b, 0))
                for n, bank in enumerate((bankq, bankk)):
                    for c in range(CH):
                        last = pe.transpose(bank[:, c * P:(c + 1) * P], rotating[:, t, n, c * P:(c + 1) * P],
                                            m.k["ident"])
                last.then_inc(qk_turned, 1)

            def turn_o(b, values):
                pe.wait_ge(o_copied, batch_done(b))
                pe.wait_ge(added, batch_done(b, 1))
                pe.wait_ge(values_ready, done(values, 1))
                for t, bank in enumerate((G, bankv)):
                    for c in range(CH):
                        last = pe.transpose(bank[:, c * P:(c + 1) * P], o_now[:, t, c * P:(c + 1) * P],
                                            m.k["ident"])
                last.then_inc(o_turned, 1)

            def put_out(b):
                pe.wait_ge(oT_ready, batch_done(b))
                for t in range(QT):
                    for c in range(CH):
                        last = pe.matmul(G[:, t * P:(t + 1) * P], oT[:, t, c * P:(c + 1) * P],
                                         w["wo"][:, c * C:(c + 1) * C], start=c == 0, stop=c == CH - 1)
                last.then_inc(out_mm, 1)

            def after(b, i, previous):
                if i in (0, 1):
                    multiply_qk(b + 1, i)
                if i in (2, 3):
                    multiply_v(b + 1, i - 2)
                if i in (5, 6):
                    turn_qk(b + 1, i - 5)
                if i == 6 and previous is not None:
                    turn_o(previous, b + 1)
                if i == 7 and previous is not None:
                    put_out(previous)

            def ready(b):
                pe.wait_ge(keys_ready, done(b, 1))
                pe.wait_ge(values_ready, done(b, 1))

            def end():
                turn_o(B - 1, B)
                put_out(B - 1)

            for step in (multiply_qk, multiply_v, turn_qk):
                for t in range(QT):
                    step(0, t)
            a.all_batches(pe, attention_pe(pe, m, a), ready, after, end)

        @ph.block.scalar
        def _(act):
            opened(act, a.exped, a.high_copied)
            opened(act, oT_ready, rooted)
            opened(act, split_off, values_ready, keys_ready, by=2)

            def split(b, t):
                act.wait_ge(qk_mm, done(b, t))
                act.wait_ge(rotated, done(b, t, 2))
                act.wait_ge(summed, done(b, t, 1))
                for n, bank in enumerate((bankq, bankk)):
                    act.activation(raw[:, t, n, :], bank, ACT.Copy)
                    last = act.activation(squares[:, n * W:(n + 1) * W], bank, ACT.Square)
                last.then_inc(split_off, 1)

            def root(b):
                act.wait_ge(summed, done(b, 1))
                act.wait_ge(scaled, done(b, 0, 1))
                act.activation(m.inv_norm[:, :, :], m.norm[:, :, :], ACT.Sqrt).then_inc(rooted, 1)

            def copy_values(b, t):
                act.wait_ge(values_mm, done(b, t))
                act.activation(v[:, ds(b & 1, 1), t, :], bankv.unsqueeze(1), ACT.Copy).then_inc(values_ready, 1)

            def copy_keys(b, t):
                act.wait_ge(qk_turned, done(b, t))
                act.activation(kT[:, ds(b & 1, 1), :, t * P:(t + 1) * P].rearrange("p two c n -> p (two c) n"),
                               bankk.rearrange("p (c n) -> p c n", n=P), ACT.Copy).then_inc(keys_ready, 1)

            def copy_oT(b):
                act.wait_ge(o_turned, batch_done(b))
                act.activation(oT[:, 0, :], G[:, :], ACT.Copy)
                act.activation(oT[:, 1, :], bankv, ACT.Copy).then_inc(oT_ready, 1)

            def after(b, i, previous):
                if i in (0, 1):
                    split(b + 1, i)
                if i in (2, 3):
                    copy_values(b + 1, i - 2)
                if i == 3:
                    root(b + 1)
                if i in (5, 6):
                    copy_keys(b + 1, i - 5)
                if i == 6 and previous is not None:
                    copy_oT(previous)

            for t in range(QT):
                split(0, t)
            root(0)
            for step in (copy_values, copy_keys):
                for t in range(QT):
                    step(0, t)
            a.all_batches(act, attention_act(act, m, a), None, after, lambda: copy_oT(B - 1))

        @ph.block.vector
        def _(dve):
            opened(dve, a.topped, a.normed, a.low_copied, a.inverted, bounded, inv_ready, added)
            opened(dve, summed, rotated, queries_ready, by=2)

            def rotate(b, t):
                dve.wait_ge(split_off, done(b, t))
                dve.wait_ge(joined, done(b, t, 2))
                dve.wait_ge(qk_turned, done(b, t, 2))
                qk, sw = by_head(raw[:, t]), by_head(swapped[:, t])
                at = slice(t, 4, 2)
                cos = m.turn_cos[:, at, :].unsqueeze(2).broadcast_to([P, 2, L0F_HEADS, WIDE])
                sin = m.turn_sin[:, at, :].unsqueeze(2).broadcast_to([P, 2, L0F_HEADS, WIDE])
                dve.tensor_tensor(by_head(rotating[:, t]), qk, cos, ALU.mult)
                dve.tensor_tensor(sw[:, :, :, 0:h], qk[:, :, :, h:WIDE], sin[:, :, :, 0:h], ALU.mult)
                dve.tensor_tensor(sw[:, :, :, h:WIDE], qk[:, :, :, 0:h], sin[:, :, :, h:WIDE],
                                  ALU.mult).then_inc(rotated, 1)

            def measure(b, t):
                dve.wait_ge(inv_ready, batch_done(b, 1))
                dve.wait_ge(split_off, done(b, t))
                dve.tensor_reduce(m.norm[:, 2 * t:2 * t + 2, :].rearrange("p a h -> p (a h)"),
                                  squares.rearrange("p (n d) -> p n d", d=WIDE), AX_X, ALU.add).then_inc(summed, 1)

            def invert(b):
                dve.wait_ge(rooted, batch_done(b))
                dve.tensor_scalar(m.norm[:, :, :], m.inv_norm[:, :, :], 1e-12, None, ALU.max).then_inc(bounded, 1)
                dve.wait_ge(bounded, batch_done(b))
                dve.reciprocal(m.inv_norm[:, :, :], m.norm[:, :, :]).then_inc(inv_ready, 1)

            def copy_queries(b, t):
                dve.wait_ge(qk_turned, done(b, t))
                dve.tensor_copy(qT[:, ds(b & 1, 1), :, t * P:(t + 1) * P].rearrange("p two c n -> p (two c) n"),
                                bankq.rearrange("p (c n) -> p c n", n=P)).then_inc(queries_ready, 1)

            def add_out(b):
                dve.wait_ge(out_mm, batch_done(b))
                here = y[:, ds(b * QT, QT), :]
                dve.tensor_tensor(here, here, G[:, 0:S].rearrange("p (t c) -> p t c", c=C), ALU.add).then_inc(added, 1)

            def after(b, i, previous):
                if i in (1, 2):
                    measure(b + 1, i - 1)
                    rotate(b + 1, i - 1)
                if i == 3:
                    invert(b + 1)
                if i in (5, 6):
                    copy_queries(b + 1, i - 5)
                if i == 7 and previous is not None:
                    add_out(previous)

            for t in range(QT):
                measure(0, t)
                rotate(0, t)
            invert(0)
            for t in range(QT):
                copy_queries(0, t)
            slot = attention_dve(dve, m, a, lambda b, t, head, _: o[:, ds(b & 1, 1), t, ds(head * WIDE, WIDE)])
            a.all_batches(dve, slot, None, after, lambda: add_out(B - 1))


def place_mask_phase(nc, m, name, allowed):
    with Phase(nc, name) as ph:
        @ph.block.vector
        def _(dve):
            dve.tensor_copy(m.allowed[:, :, :].rearrange("p t k -> p (t k)"), allowed)
            dve.tensor_copy(m.identb[:, :], m.k["ident"])


def add_phase(nc, m, name):
    with Phase(nc, name) as ph:
        @ph.block.vector
        def _(dve):
            dve.tensor_tensor(wide(m.x), wide(m.x), wide(m.xn), ALU.add)


def l0_ffn(nc, m, w, fetch):
    prepare(nc, m, "L0f")
    for d in range(2):
        wd = {n[:-1]: v for n, v in w.items() if n.endswith(str(d))}
        wd.update({n: w[n] for n in ("scale", "band", "xq_cos", "xq_sin", "xk_cos", "xk_sin")})
        shift_phase(nc, m, f"L0f{d}_shift", m.xn, wd)
        local_phase(nc, m, f"L0f{d}_attend", wd, m.xn, fetch if d == 0 else None)
        shift_phase(nc, m, f"L0f{d}_shift2", m.xn, None)
        affine_phase(nc, m, f"L0f{d}_norm", m.o, m.o, None, None, back=True, columns=(wd["g"], wd["b"]))
        cut = pieces(L0F_HID)
        value = lambda i: wd["w1"][:, cut[i][0]:sum(cut[i])]
        gate = lambda i: wd["w1"][:, L0F_HID + cut[i][0]:L0F_HID + sum(cut[i])]
        down = lambda i: wd["w2"][0:cut[i][1], i * C:(i + 1) * C]
        moe_phase(nc, m, f"L0f{d}_glu", m.xn, [(gate, value, down)], [n for _, n in cut], ACT.Gelu, [None],
                  biases=(wd["b1"][:, 0:3], wd["b1"][:, 3:6]), row_bias=wd["b2_row"])
    add_phase(nc, m, "L0f_add")


def select_phase(nc, m, w, sel, selT):
    with Phase(nc, "L2x_select") as ph:
        steps, diagonal, spread, own_read, picked, turned, copied, queries, taken = (ph.sem(n) for n in (
            "steps", "diagonal", "spread", "own_read", "picked", "turned", "copied", "queries", "taken"))
        more = m.kT[:, :, :].rearrange("p c n -> p (c n)").rearrange("p (b t j) -> p b t j", b=B, t=QT)
        same = m.v[:, :, :].rearrange("p c n -> p (c n)").rearrange("p (b t j) -> p b t j", b=B, t=QT)
        every = m.banks.rearrange("p a n -> p (a n)").rearrange("p (b j) -> p b j", j=S)
        ident = m.k["ident"].unsqueeze(1).broadcast_to([P, TILES, P])

        @ph.block.gpsimd
        def _(pool):
            pool.wait_ge(picked, 1)
            clear_stacks(pool, m)

        @ph.block.tensor
        def _(pe):
            pe.wait_ge(diagonal, 1)
            for g in range(4):
                last = pe.matmul(m.banks[:, g, :], m.ones[:, :], wide(m.h)[:, g * 512:(g + 1) * 512], start=True,
                                 stop=True)
            last.then_inc(spread, 1)
            pe.wait_ge(picked, 1)
            turn_pe(pe, m, sel, turned, rows=L2_CAP)
            pe.wait_ge(copied, 4)
            for g in range(4):
                for t in range(4):
                    last = pe.matmul(m.banks[:, g, t * P:(t + 1) * P], m.hT[:, (4 * g + t) * P:(4 * g + t + 1) * P],
                                     w["wq"], start=True, stop=True)
            last.then_inc(queries, 1)

        @ph.block.vector
        def _(dve):
            st = Steps(dve, steps)
            st.done(dve.tensor_tensor(m.h[:, :, :], m.xn[:, :, :], row(w["router_row"], TILES), ALU.mult))
            st.done(dve.tensor_reduce(m.route[:, :], m.h[:, :, :], AX_X, ALU.add))
            dve.tensor_tensor(m.h[:, :, :], ident, each(m.route[:, :], P), ALU.mult).then_inc(diagonal, 1)
            dve.wait_ge(spread, 1)
            st.done(dve.tensor_tensor(m.o[:, :, :], m.banks.rearrange("p a (t c) -> p (a t) c", c=P), ident,
                                      ALU.mult))
            st.done(dve.tensor_reduce(m.own[:, :], m.o[:, :, :], AX_X, ALU.add))
            own = each(m.own[:, :].rearrange("p (b t) -> p b t", t=QT), S)
            for b in range(2):
                at = slice(4 * b, 4 * b + 4)
                other = every[:, at, :].unsqueeze(2).broadcast_to([P, 4, QT, S])
                mine = own[:, at]
                for n in range(4):
                    st.done(dve.tensor_tensor(more[:, 4 * b + n], other[:, n], mine[:, n], ALU.is_gt))
                    st.done(dve.tensor_tensor(same[:, 4 * b + n], other[:, n], mine[:, n], ALU.is_equal))
            earlier = w["earlier"].rearrange("p (t j) -> p t j", t=QT).unsqueeze(1).broadcast_to([P, B, QT, S])
            st.done(dve.tensor_tensor(same, same, earlier, ALU.mult))
            st.done(dve.tensor_tensor(more, more, same, ALU.add))
            st.done(dve.tensor_reduce(m.own[:, :].rearrange("p (b t) -> p b t", t=QT), more, AX_X, ALU.add))
            dve.tensor_tensor(sel, row(w["slot"], TILES), each(m.own[:, :], L2_CAP), ALU.is_equal).then_inc(picked, 1)
            turn_out_dve(dve, m, selT, turned, copied, rows=L2_CAP)
            dve.wait_ge(queries, 1)
            rope = w["l2_ropeq"].rearrange("p (n) -> p n").unsqueeze(1).broadcast_to([P, B, QT * C])
            dve.tensor_tensor(wide(m.h).rearrange("p (b n) -> p b n", b=B),
                              m.banks.rearrange("p a (b n) -> p (a b) n", b=2), rope, ALU.mult)

        @ph.block.scalar
        def _(act):
            turn_out_act(act, m, selT, turned, copied, rows=L2_CAP)


def chosen_phase(nc, m, w, sel, selT, fetch):
    with Phase(nc, "L2x_attend") as ph:
        a = Attention(ph, L2_HEADS, C // L2_HEADS, SK, q_rows=L2_CAP, tiles=1)
        p = Preparation(ph, a, SK + L2_CAP)
        scattered, placed, blanked, fetched = (ph.sem(n) for n in ("scattered", "placed", "blanked", "fetched"))
        G, free = m.pG, m.banks[:, 1, :]

        @ph.block.sync
        def _(sp):
            narrow_sync(sp, m, a, p)

        @ph.block.gpsimd
        def _(pool):
            pool.dma_start(*fetch).then_inc(fetched, 16)
            pool.memset(m.prob[L2_CAP:P, :, :], 0.0).then_inc(blanked, 1)
            pool.wait_ge(blanked, 1)
            narrow_pool(pool, m, a, p, ((m.ctx_now[:, :], m.ctxT, SK), (m.x_now[:, :], wide(m.h), S)))
            pool.wait_ge(fetched, 16)

        @ph.block.tensor
        def _(pe):
            def piece(n, b):
                pe.wait_ge(p.taken, 3 * b + n + 1)
                if n == 0:
                    last = pe.matmul(G[:, :], w["wk"], m.ctxT[:, ds(batch_of(b) * SK, SK)], start=True, stop=True)
                if n == 1:
                    pe.wait_ge(p.copied, b + 2)
                    for t in range(QT):
                        last = pe.matmul(G[:, 0:L2_CAP], m.x_now[:, t * P:(t + 1) * P],
                                         sel[:, ds(batch_of(b) * QT + t, 1), :], start=t == 0, stop=t == QT - 1)
                if n == 2:
                    for t in range(KT):
                        last = pe.matmul(G[:, t * P:(t + 1) * P], m.ctx_now[:, t * P:(t + 1) * P], w["wv"],
                                         start=True, stop=True)
                last.then_inc(p.made, 1)

            def scatter(b):
                pe.wait_ge(a.normed, a.count(b, a.H))
                pe.wait_ge(placed, b + 1)
                pe.matmul(free[:, 0:S], m.o_now[0:L2_CAP, :], selT[0:L2_CAP, ds(b * S, S)], start=True,
                          stop=True).then_inc(scattered, 1)

            pe.wait_ge(blanked, 1)
            opened(pe, scattered)
            narrow_pe(pe, m, a, p, piece, scatter)

        @ph.block.scalar
        def _(act):
            opened(act, a.exped, a.high_copied, placed)

            def piece(n, b):
                if n == 2:
                    act.wait_ge(p.made, 3 * b + 3)
                    two = b & 1
                    act.activation(m.v_narrow[:, ds(two, 1), :, :].rearrange("p a t c -> p (a t) c"),
                                   G[:, :].rearrange("p (t c) -> p t c", c=C), ACT.Copy).then_inc(p.taken, 1)

            p.first(piece)

            def place(b):
                act.wait_ge(scattered, b + 2)
                act.activation(wide(m.o)[:, ds(b * S, S)], free[:, 0:S], ACT.Copy).then_inc(placed, 1)

            a.all_batches(act, attention_act(act, m, a), None, p.after(piece, place), lambda: place(B - 1))

        @ph.block.vector
        def _(dve):
            opened(dve, a.topped, a.normed, a.low_copied, a.inverted, p.taken)

            def piece(n, b):
                if n == 0:
                    dve.wait_ge(p.made, 3 * b + 1)
                    dve.tensor_tensor(m.qk[:, 0:SK], G[:, :], w["l2_ropek"], ALU.mult).then_inc(p.taken, 1)
                if n == 1:
                    dve.wait_ge(p.made, 3 * b + 2)
                    dve.tensor_copy(m.qk[:, SK:SK + L2_CAP], G[:, 0:L2_CAP]).then_inc(p.taken, 1)

            p.first(piece)
            slot = attention_dve(dve, m, a, lambda b, t, h, _: m.o_now[0:L2_CAP, ds(h * a.dh, a.dh)])
            a.all_batches(dve, slot, None, p.after(piece, lambda b: dve.wait_ge(scattered, b + 2)))


def chosen_finish(nc, m, w):
    with Phase(nc, "L2x_finish") as ph:
        steps, projected = ph.sem("steps"), ph.sem("projected")

        @ph.block.tensor
        def _(pe):
            for g in range(4):
                for t in range(4):
                    at = (4 * g + t) * P
                    last = pe.matmul(m.banks[:, g, t * P:(t + 1) * P], wide(m.o)[:, at:at + P], w["wo"], start=True,
                                     stop=True)
                last.then_inc(projected, 1)

        @ph.block.vector
        def _(dve):
            st = Steps(dve, steps)
            for g in range(4):
                at = slice(4 * g, 4 * g + 4)
                dve.wait_ge(projected, g + 1)
                st.done(dve.tensor_tensor(m.h[:, at, :], m.banks[:, g, :].rearrange("p (t c) -> p t c", c=C),
                                          each(m.route[:, at], C), ALU.mult))
                st.done(dve.tensor_tensor(m.x[:, at, :], m.x[:, at, :], m.h[:, at, :], ALU.add))


def wide_cross_phase(nc, m, w, fetch):
    CH = CHUNKS_L3
    with Phase(nc, "L3x_attend") as ph:
        mask_now = wide(m.o)[:, 4 * C:4 * C + SK]
        a = Attention(ph, L3_HEADS, WIDE, SK, w["scale"], mask=lambda t: mask_now)
        a.mask_by_batch = True
        copied = ph.sem("copied")
        biased = ph.sem("biased")
        weights_ready = ph.sem("weights_ready")
        keys_mm, queries_mm, values_mm = (ph.sem(n) for n in ("keys_mm", "queries_mm", "values_mm"))
        keys_taken = ph.sem("keys_taken")
        queries_taken = ph.sem("queries_taken")
        values_taken = ph.sem("values_taken")
        o_turned = ph.sem("o_turned")
        oT_ready = ph.sem("oT_ready")
        out_mm = ph.sem("out_mm")
        added = ph.sem("added")
        G = m.pG[:, :]
        spare = m.sel[:, :, :].rearrange("p t c -> p (t c)")
        w_now = spare[:, 0:4 * P].rearrange("p (two n c) -> p two n c", two=2, n=2)
        oT = spare[:, 4 * P:4 * P + 2 * S].rearrange("p (two q) -> p two q", two=2)
        o = m.o[:, 0:4, :].rearrange("p (two t) c -> p two t c", two=2)
        wqk = m.xw[:, 0:2 * CH * C].rearrange("p (n c) -> p n c", n=2)
        a.queries = lambda b, j: m.qT[:, ds(j, 1), :]
        a.keys = lambda b, j: m.kT[:, ds(j, 1), :]
        a.values = lambda b, c, head: m.v[:, c, ds(head * WIDE, WIDE)]
        fetch_sync(ph, fetch)

        def done(b, c, back=0):
            return b * CH + (c + (2 - back))

        def weighed(b, j, previous):
            if isinstance(j, int) and j < 2:
                return None if previous is None else (previous, j + CH - 2)
            return b, j - 2

        def emptied(b, i, j, previous):
            if isinstance(i, int) and i >= a.H or isinstance(j, int) and j < 2 and previous is None:
                return None
            return (b, j + CH - 2) if isinstance(j, int) and j < 2 else (b + 1, j - 2)

        def starting(i):
            return not (isinstance(i, int) and i >= a.H)

        @ph.block.gpsimd
        def _(pool):
            opened(pool, a.head_ready, weights_ready)
            one = m.ones[:, 0:1]

            def copy_context(b):
                pool.tensor_tensor(m.ctx_now[:, :], m.ctxT[:, ds(batch_of(b) * SK, SK)], one.broadcast_to([P, SK]),
                                   ALU.mult).then_inc(copied, 1)

            def copy_weights(b, j, parity):
                if not isinstance(b, int) or b > 0 or j >= 2:
                    pool.wait_ge(queries_mm, done(b, j, 2))
                pool.tensor_tensor(w_now[:, parity], wqk[:, :, ds(j * P, P)],
                                   one.unsqueeze(2).broadcast_to([P, 2, P]), ALU.mult).then_inc(weights_ready, 1)

            def before(b, j):
                pool.wait_ge(queries_taken, done(b, j))

            def more(b, place, j):
                if isinstance(j, int) and j == 0:
                    pool.wait_ge(a.topped, a.count(b, 0))
                    pool.tensor_tensor(mask_now, m.key_mask[:, ds(b * SK, SK)], one.broadcast_to([P, SK]),
                                       ALU.mult).then_inc(a.mask_ready, 1)
                copy_weights(b + 1, j, place // 2)
                if isinstance(j, int) and j == 1:
                    pool.wait_ge(values_mm, done(b, CH - 1))
                    copy_context(b + 1)

            copy_context(0)
            for c in range(CH):
                copy_weights(0, c, c % 2)
            a.all_batches(pool, queries_slot(pool, m, a, before, more))

        @ph.block.tensor
        def _(pe):
            opened(pe, a.scored, a.turned, a.weighed, keys_mm, queries_mm, values_mm, o_turned, out_mm)

            def keys(b, j, parity, bank):
                pe.wait_ge(weights_ready, done(b, j))
                pe.matmul(bank, w_now[:, parity, 1, :], m.ctxT[:, ds(batch_of(b) * SK, SK)], start=True,
                          stop=True).then_inc(keys_mm, 1)

            def queries(b, j, parity, bank):
                pe.matmul(bank[:, 0:S], w_now[:, parity, 0, :], m.hT[:, ds(batch_of(b) * S, S)], start=True,
                          stop=True).then_inc(queries_mm, 1)

            def values(b, c, bank):
                pe.wait_ge(copied, b + 1)
                for t in range(KT):
                    last = pe.matmul(bank[:, t * P:(t + 1) * P], m.ctx_now[:, t * P:(t + 1) * P],
                                     w["wv"][:, ds(c * P, P)], start=True, stop=True)
                last.then_inc(values_mm, 1)

            def put_out(b, c, parity):
                pe.wait_ge(oT_ready, done(b, c))
                for t in range(QT):
                    last = pe.matmul(G[:, t * P:(t + 1) * P], oT[:, parity, t * P:(t + 1) * P],
                                     w["wo"][:, ds(c * C, C)], start=True, stop=True)
                last.then_inc(out_mm, 1)

            def more(k, b, i, place, j, previous):
                parity, chunk = place // 2, weighed(b, j, previous)
                if place % 2 == 0:
                    new = emptied(b, i, j, previous)
                    if k == 1 and new is not None:
                        pe.wait_ge(queries_taken, done(b + 1, j, 1))
                        values(*new, G)
                    if k == 2 and chunk is not None:
                        if new is not None:
                            pe.wait_ge(values_taken, done(*new))
                        pe.wait_ge(a.normed, a.count(b, 2 * j - 2, previous))
                        if not starting(i):
                            pe.wait_ge(queries_taken, done(b + 1, CH - 1))
                            pe.wait_ge(added, done(*chunk, 1))
                        for t in range(QT):
                            last = pe.transpose(G[:, t * P:(t + 1) * P], o[:, parity, t, :], m.k["ident"])
                        last.then_inc(o_turned, 1)
                else:
                    if k == 0 and chunk is not None:
                        put_out(*chunk, parity)
                    if k == 1 and starting(i):
                        if chunk is not None:
                            pe.wait_ge(added, done(*chunk))
                        else:
                            pe.wait_ge(queries_taken, done(b + 1, j, 1))
                        keys(b + 1, j, parity, G)
                    if k == 2 and starting(i):
                        pe.wait_ge(keys_taken, done(b + 1, j))
                        queries(b + 1, j, parity, G)

            for c in range(CH):
                pe.wait_ge(keys_taken, done(0, c, 1))
                keys(0, c, c % 2, m.banks[:, 0, :])
                pe.wait_ge(queries_taken, done(0, c, 1))
                queries(0, c, c % 2, m.banks[:, 1, :])
                pe.wait_ge(values_taken, done(0, c, 1))
                values(0, c, G)
            pe.wait_ge(keys_taken, done(0, CH - 1))
            pe.wait_ge(queries_taken, done(0, CH - 1))
            pe.wait_ge(values_taken, done(0, CH - 1))
            a.all_batches(pe, attention_pe(pe, m, a, more), end=lambda: put_out(B - 1, CH - 1, (CH - 1) % 2))

        @ph.block.scalar
        def _(act):
            opened(act, a.exped, a.high_copied, keys_taken, oT_ready)

            def take_keys(b, j, bank):
                act.wait_ge(keys_mm, done(b, j))
                act.activation(m.kT[:, ds(j, 1), :], bank.unsqueeze(1), ACT.Identity,
                               bias=w["bk"][:, ds(j, 1)]).then_inc(keys_taken, 1)

            def more(k, b, i, place, j, previous):
                if k == 1 and place % 2 == 1 and starting(i):
                    take_keys(b + 1, j, G)
                chunk = weighed(b, j, previous)
                if k == 2 and place % 2 == 0 and chunk is not None:
                    act.wait_ge(o_turned, done(*chunk))
                    act.activation(oT[:, place // 2, :], G[:, 0:S], ACT.Copy).then_inc(oT_ready, 1)

            for c in range(CH):
                take_keys(0, c, m.banks[:, 0, :])
            a.all_batches(act, attention_act(act, m, a, more))

        @ph.block.vector
        def _(dve):
            opened(dve, a.topped, a.normed, a.low_copied, a.inverted, queries_taken, values_taken, added)
            dve.tensor_tensor(m.x[:, :, :], m.x[:, :, :], row(w["bo_row"], TILES), ALU.add).then_inc(biased, 1)

            def take_queries(b, j, bank):
                dve.wait_ge(queries_mm, done(b, j))
                dve.tensor_scalar(m.qT[:, ds(j, 1), :], bank[:, 0:S].unsqueeze(1), w["bq"][:, ds(j, 1)], None,
                                  ALU.add).then_inc(queries_taken, 1)

            def take_values(b, c):
                dve.wait_ge(values_mm, done(b, c))
                dve.tensor_tensor(m.v[:, :, ds(c * P, P)], G[:, :].rearrange("p (t c) -> p t c", c=P),
                                  row(w["bv_row"][:, ds(c * P, P)], KT), ALU.add).then_inc(values_taken, 1)

            def add(b, c):
                dve.wait_ge(out_mm, done(b, c))
                dve.wait_ge(added, done(b, c, 1))
                here = m.x[:, ds(b * QT, QT), :]
                dve.tensor_tensor(here, here, G[:, 0:S].rearrange("p (t c) -> p t c", c=C), ALU.add).then_inc(added, 1)

            def more(k, b, i, place, j, previous):
                chunk = weighed(b, j, previous)
                if place % 2 == 0:
                    new = emptied(b, i, j, previous)
                    if k == 1 and new is not None:
                        take_values(*new)
                else:
                    if k == 0 and chunk is not None:
                        add(*chunk)
                    if k == 2 and starting(i):
                        take_queries(b + 1, j, G)

            for c in range(CH):
                take_queries(0, c, m.banks[:, 1, :])
                take_values(0, c)
            dve.wait_ge(biased, 1)
            slot = attention_dve(dve, m, a, lambda b, t, head, place: o[:, place // 2, t, ds(place % 2 * WIDE, WIDE)],
                                 more)
            a.all_batches(dve, slot, end=lambda: add(B - 1, CH - 1))


def conv_phase(nc, m, w):
    with Phase(nc, "L3f_conv") as ph:
        steps = ph.sem("steps")
        src = m.hT[:, :].rearrange("p (b s) -> p b s", s=S)
        dst = wide(m.h).rearrange("p (b s) -> p b s", s=S)

        @ph.block.vector
        def _(dve):
            st = Steps(dve, steps)
            st.done(dve.tensor_scalar(dst, src, w["conv"][:, 2:3], None, ALU.mult))
            for back in (1, 2):
                st.done(dve.scalar_tensor_tensor(out=dst[:, :, back:S], in0=src[:, :, 0:S - back],
                                                 scalar=w["conv"][:, 2 - back:3 - back], in1=dst[:, :, back:S],
                                                 op0=ALU.mult, op1=ALU.add))


def causal_phase(nc, m, w):
    with Phase(nc, "L3f_attend") as ph:
        a = Attention(ph, L3F_HEADS, C // L3F_HEADS, S)
        a.causal = True
        a.warm = WARM
        p = Preparation(ph, a, 2 * S)
        crossed = ph.sem("crossed")
        G, x = m.pG, wide(m.h)

        @ph.block.sync
        def _(sp):
            narrow_sync(sp, m, a, p)

        @ph.block.gpsimd
        def _(pool):
            narrow_pool(pool, m, a, p, ((m.x_now[:, :], x, S),))

        @ph.block.tensor
        def _(pe):
            def piece(n, b):
                pe.wait_ge(p.taken, 3 * b + n + 1)
                if n < 2:
                    for i, name in enumerate((("wk", "wq"), ("wkr", "wqr"))[n]):
                        last = pe.matmul(G[:, i * S:(i + 1) * S], w[name], x[:, ds(batch_of(b) * S, S)], start=True,
                                         stop=True)
                if n == 2:
                    pe.wait_ge(p.copied, b + 2)
                    for t in range(QT):
                        last = pe.matmul(G[:, t * P:(t + 1) * P], m.x_now[:, t * P:(t + 1) * P], w["wv"],
                                         start=True, stop=True)
                last.then_inc(p.made, 1)

            narrow_pe(pe, m, a, p, piece)

        @ph.block.scalar
        def _(act):
            opened(act, a.exped, a.high_copied)

            def piece(n, b):
                if n == 2:
                    act.wait_ge(p.made, 3 * b + 3)
                    two = b & 1
                    act.activation(m.v_narrow[:, ds(two, 1), 0:QT, :].rearrange("p a t c -> p (a t) c"),
                                   G[:, 0:S].rearrange("p (t c) -> p t c", c=C), ACT.Copy).then_inc(p.taken, 1)

            p.first(piece)
            a.all_batches(act, attention_act(act, m, a), None, p.after(piece))

        @ph.block.vector
        def _(dve):
            opened(dve, a.topped, a.normed, a.low_copied, a.inverted, p.taken)

            def piece(n, b):
                if n == 0:
                    dve.wait_ge(p.made, 3 * b + 1)
                    dve.tensor_tensor(m.qk[:, 0:2 * S], G[:, :], w["l3f_cos"], ALU.mult).then_inc(p.taken, 1)
                if n == 1:
                    dve.wait_ge(p.made, 3 * b + 2)
                    dve.tensor_tensor(m.qk_rest[:, 0:2 * S], G[:, :], w["l3f_sin"], ALU.mult).then_inc(crossed, 1)
                    dve.wait_ge(crossed, b + 1)
                    dve.tensor_tensor(m.qk[:, 0:2 * S], m.qk[:, 0:2 * S], m.qk_rest[:, 0:2 * S],
                                      ALU.add).then_inc(p.taken, 1)

            p.first(piece)
            slot = attention_dve(dve, m, a, lambda b, t, h, _: m.o[:, ds(b * QT + t, 1), ds(h * a.dh, a.dh)])
            a.all_batches(dve, slot, None, p.after(piece))


def l3_ffn(nc, m, w):
    place_mask_phase(nc, m, "L3f_mask", w["causal"])
    prepare(nc, m, "L3f", clear=True)
    affine_phase(nc, m, "L3f_norm1", m.xn, m.o, w["g1_row"], w["b1_row"])
    conv_phase(nc, m, w)
    causal_phase(nc, m, w)
    xattn_finish(nc, m, "L3f", w, m.xn, bias=False)
    affine_phase(nc, m, "L3f_norm2", m.xn, m.o, w["g2_row"], w["b2_row"])
    route_phase(nc, m, "L3f", w["router"], L3F_EXPERTS, 1, softmax=False)
    cut = pieces(L3F_HID)

    def expert(e):
        at = 2 * L3F_HID * e
        gate = lambda i: w["wv2"][:, at + i * P:at + (i + 1) * P]
        value = lambda i: w["wv2"][:, at + L3F_HID + i * P:at + L3F_HID + (i + 1) * P]
        down = lambda i: w["down"][:, (e * len(cut) + i) * C:(e * len(cut) + i + 1) * C]
        return gate, value, down

    moe_phase(nc, m, "L3f_moe", m.xn, [expert(e) for e in range(L3F_EXPERTS)], [n for _, n in cut], ACT.Silu,
              list(range(L3F_EXPERTS)))
    add_phase(nc, m, "L3f_add")


def store_phase(nc, m, out):
    with Phase(nc, "store") as ph:
        stored = ph.sem("stored")

        @ph.block.sync
        def _(sp):
            sp.dma_start(out.rearrange("(t p) c -> p t c", p=P), m.x[:, :, :]).then_inc(stored, 16)
            sp.wait_ge(stored, 16)


def build(nc, x, ctxT, mask_f, mask_b, wx, wf, const, out):
    with ExitStack() as ctx:
        m = Memory(nc, ctx)
        load_phase(nc, m, x, ctxT, wx, const)
        k = m.k

        def weights_f(name):
            return m.fw[:, 0:width(FW[name])], wf[name]

        def weights_x(name):
            return m.xw[:, 0:width(XW[name])], wx[name]

        w = views(m.xw, XW["L0x"])
        prepare(nc, m, "L0x", clear=True)
        cross_phase(nc, m, "L0x", w, L0_HEADS, with_q=True, fetch=weights_f("L0f"))
        l0_xattn_finish(nc, m, w)
        l0_ffn(nc, m, views(m.fw, FW["L0f"]), weights_x("L1x"))
        w = views(m.xw, XW["L1x"])
        prepare(nc, m, "L1x", clear=True)
        key_mask_phase(nc, m, "L1x", mask_f, False)
        cross_phase(nc, m, "L1x", w, L1_HEADS, mask=True, fetch=weights_f("L1f"))
        xattn_finish(nc, m, "L1x", w, m.x)
        w = views(m.fw, FW["L1f"])
        prepare(nc, m, "L1f")
        route_phase(nc, m, "L1f", w["router"], L1F_EXPERTS, 2, bias=w["rb_row"])
        moe_phase(nc, m, "L1f", m.x, [laid_side_by_side(w, L1F_HID)(e) for e in range(1 + L1F_EXPERTS)],
                  [n for _, n in pieces(L1F_HID)], ACT.Silu, [None, *range(L1F_EXPERTS)],
                  fetch=weights_x("L2x"))
        w = views(m.xw, XW["L2x"])
        sel = m.sel[:, :, :]
        selT = wide(m.xn)
        prepare(nc, m, "L2x")
        select_phase(nc, m, w, sel, selT)
        chosen_phase(nc, m, w, sel, selT, weights_f("L2f"))
        chosen_finish(nc, m, w)
        w = views(m.fw, FW["L2f"])
        prepare(nc, m, "L2f")
        route_phase(nc, m, "L2f", w["router"], L2F_EXPERTS, 2, eps=1e-20)
        moe_phase(nc, m, "L2f", m.x, [laid_side_by_side(w, L2F_HID)(e) for e in range(1 + L2F_EXPERTS)],
                  [n for _, n in pieces(L2F_HID)], ACT.Silu, [None, *range(L2F_EXPERTS)],
                  fetch=weights_x("L3x"))
        w = views(m.xw, XW["L3x"])
        prepare(nc, m, "L3x")
        key_mask_phase(nc, m, "L3x", mask_b, True)
        wide_cross_phase(nc, m, w, weights_f("L3f"))
        l3_ffn(nc, m, views(m.fw, FW["L3f"]))
        store_phase(nc, m, out)


def kernel(**inputs):
    import numpy as np
    import concourse.bacc as bacc
    from concourse import mybir as mb
    from concourse.bass_utils import run_bass_kernel_spmd

    a = {n: np.asarray(v) for n, v in inputs.items()}

    def rows(v):
        return np.broadcast_to(v.reshape(1, -1), (P, v.size))

    def tall(v):
        n = -(-v.shape[0] // P)
        v = np.concatenate([v, np.zeros((n * P - v.shape[0], v.shape[1]), v.dtype)])
        return v.reshape(n, P, -1).transpose(1, 0, 2).reshape(P, -1)

    def chunks(v):
        n = -(-v.size // P)
        return np.concatenate([v, np.zeros(n * P - v.size, v.dtype)]).reshape(n, P).T

    L0x = {n: a["L0_xattn_" + n] for n in ("Wq", "Wk", "Wv", "Wo", "bq", "bk", "bv", "bo", "g0", "b0", "g1", "b1")}
    L1x = {n: a["L1_xattn_" + n] for n in ("Wq", "Wk", "Wv", "Wo", "bq", "bk", "bv", "bo")}
    L2x = {n: a["L2_xattn_" + n] for n in ("router_w", "q_w", "kv_w", "out_w")}
    L3x = {n: a["L3_xattn_" + n] for n in ("Wq", "Wk", "Wv", "Wo", "bq", "bk", "bv", "bo")}
    L0f = {n: a["L0_ffn_" + n] for n in ("wqkv", "q_scale", "k_scale", "wo", "ln_g", "ln_b", "w1", "b1", "w2", "b2")}
    L1f = {n: a["L1_ffn_" + n] for n in ("sg", "su", "sd", "rg", "ru", "rd", "wr", "rb")}
    L2f = {n: a["L2_ffn_" + n] for n in ("Wr", "Wg", "Wu", "Wd", "Sg", "Su", "Sd")}
    L3f = {n: a["L3_ffn_" + n] for n in ("ln1_w", "ln1_b", "ln2_w", "ln2_b", "conv_w", "attn_w", "proj_w",
                                         "router_w", "expert_wv", "expert_proj")}
    by16 = np.arange(C).reshape(8, 1, 16).transpose(1, 2, 0).reshape(-1)
    by8 = np.arange(C).reshape(8, 2, 8).transpose(1, 2, 0).reshape(-1)
    hd = C // L3F_HEADS
    f = np.float32
    part = np.arange(P)
    head_rows = lambda n, s: (part[:, None] // (P // n) == np.arange(n)[None]) * f(s)
    place = np.arange(S)
    q_at, k_at = place[:, None], place[None, :]
    tile2 = lambda t: t.reshape(QT, P, -1).transpose(1, 0, 2).reshape(P, -1)
    masked = f(-1e30)
    freq4 = np.exp(np.linspace(0.0, -1.0, 4, dtype=f) * np.log(f(10000.0))).astype(f)

    def l2_rope(n):
        angle = np.arange(n, dtype=f)[:, None] * freq4
        return np.tile(np.concatenate([np.sin(angle), np.cos(angle)], axis=-1), (1, L2_HEADS))

    inv = (f(1.0) / f(10000.0) ** (np.arange(0, hd, 2, dtype=f) / f(hd))).astype(f)
    ang = place.astype(f)[:, None] * inv
    l3_cos = np.tile(np.cos(ang), (1, 2 * L3F_HEADS)).T
    l3_sin = np.tile(np.concatenate([-np.sin(ang), np.sin(ang)], axis=-1), (1, L3F_HEADS)).T
    half = np.arange(0, WIDE, 2, dtype=f)
    ang = place.astype(f)[:, None] * (f(1.0) / f(10000.0) ** (half / f(WIDE)))[None]
    base = (half + f(0.4 * WIDE)) / f(1.4 * WIDE)
    grow = base[None] ** ((place - S // 2).astype(f) / f(32.0))[:, None]
    both = lambda t: np.concatenate([t, t], axis=-1)
    signed = lambda t: np.concatenate([-t, t], axis=-1)
    thin = lambda t: np.asarray(t, dtype=f)
    consts = [np.eye(P), rows(np.arange(8)[None] < np.arange(8)[:, None])]
    band = tile2(np.where((k_at <= q_at) & (k_at >= q_at - 64), f(0), masked))
    causal = tile2(np.where(k_at <= q_at, f(0), masked))
    local_tables = [np.tile(head_rows(2, 8.0), (1, CHUNKS_L0F)), band, tile2(both(np.cos(ang) * grow)),
                    tile2(signed(np.sin(ang) * grow)), tile2(both(np.cos(ang) / grow)),
                    tile2(signed(np.sin(ang) / grow))]
    causal_tables = [causal, l3_cos[by8], l3_cos[by8] / np.sqrt(f(8)), l3_sin[by8], l3_sin[by8] / np.sqrt(f(8))]
    chosen_tables = [tile2((l2_rope(S) / np.sqrt(f(8)))[:, by8]), l2_rope(SK).T[by8], rows(np.arange(L2_CAP)),
                     tile2(k_at < q_at)]

    packs = {
        "x_L0x": [L0x["Wq"].T[:, by16], L0x["Wq"].T, L0x["Wk"].T[:, by16], L0x["Wv"].T, L0x["Wo"].T,
                  chunks(L0x["bq"][by16]), chunks(L0x["bk"][by16]),
                  *(rows(L0x[n]) for n in ("bq", "bv", "bo", "g0", "b0", "g1", "b1"))],
        "x_L1x": [L1x["Wq"].T[:, by8], L1x["Wk"].T[:, by8], L1x["Wv"].T, L1x["Wo"].T, chunks(L1x["bq"][by8]),
                  chunks(L1x["bk"][by8]),
                  rows(L1x["bv"]), rows(L1x["bo"])],
        "x_L2x": [L2x["q_w"].T[:, by8], L2x["kv_w"][:C].T[:, by8], L2x["kv_w"][C:].T, L2x["out_w"].T, rows(L2x["router_w"]),
                  *chosen_tables],
        "x_L3x": [L3x["Wq"], L3x["Wk"], L3x["Wv"], tall(L3x["Wo"]), chunks(L3x["bq"]), chunks(L3x["bk"]),
                  rows(L3x["bv"]), rows(L3x["bo"]), np.tile(head_rows(2, 1 / 8.0), (1, CHUNKS_L3))],
        "f_L1f": [*(L1f[s].T for s in ("sg",)), *(w.T for w in L1f["rg"]), L1f["su"].T, *(w.T for w in L1f["ru"]),
                  tall(L1f["sd"].T), *(tall(w.T) for w in L1f["rd"]), L1f["wr"].T, rows(L1f["rb"])],
        "f_L2f": [L2f["Sg"], *L2f["Wg"], L2f["Su"], *L2f["Wu"], tall(L2f["Sd"]), *(tall(w) for w in L2f["Wd"]),
                  L2f["Wr"]],
    }
    depth = []
    for d in (0, 1):
        b1 = L0f["b1"][d]
        depth += [L0f["wqkv"][d], tall(L0f["wo"][d]), L0f["w1"][d], tall(L0f["w2"][d]), rows(L0f["q_scale"][d]),
                  rows(L0f["k_scale"][d]), chunks(L0f["ln_g"][d]), chunks(L0f["ln_b"][d]),
                  chunks(b1[:L0F_HID]), chunks(b1[L0F_HID:]), rows(L0f["b2"][d])]
    packs["f_L0f"] = depth + local_tables
    swap = np.arange(C).reshape(L3F_HEADS, 2, hd // 2)[:, ::-1].reshape(-1)
    wq, wk, wv = np.split(L3f["attn_w"], 3, axis=1)
    packs["f_L3f"] = [*L3f["expert_wv"], *(tall(w) for w in L3f["expert_proj"]), wq[:, by8], wq[:, swap][:, by8],
                      wk[:, by8], wk[:, swap][:, by8],
                      wv, L3f["proj_w"], L3f["conv_w"].reshape(C, 3), rows(L3f["ln1_w"]), rows(L3f["ln1_b"]),
                      rows(L3f["ln2_w"]), rows(L3f["ln2_b"]), L3f["router_w"], *causal_tables]

    arrays = {n: np.ascontiguousarray(np.concatenate([thin(v) for v in p], axis=1)) for n, p in packs.items()}
    arrays["const"] = np.ascontiguousarray(np.concatenate([thin(v) for v in consts], axis=1))
    arrays["x"] = np.ascontiguousarray(a["x"].reshape(TOK, C))
    arrays["ctxT"] = np.ascontiguousarray(a["ctx_1024"].reshape(B * SK, C).T)
    arrays["mask_f"] = np.ascontiguousarray(a["mask_BxS2_ff1"].reshape(1, B * SK))
    arrays["mask_b"] = np.ascontiguousarray(a["mask_BxS2_bf1"].reshape(1, B * SK)).view(np.uint8)

    nc = bacc.Bacc("TRN2", target_bir_lowering=False, num_devices=1)
    d = {n: nc.dram_tensor("in_" + n, v.shape, mb.dt.from_np(v.dtype), kind="ExternalInput").ap() for n, v in arrays.items()}
    out = nc.dram_tensor("out_0", (TOK, C), mb.dt.float32, kind="ExternalOutput").ap()
    build(nc, d["x"], d["ctxT"], d["mask_f"], d["mask_b"], {n[2:]: d[n] for n in d if n.startswith("x_")},
          {n[2:]: d[n] for n in d if n.startswith("f_")}, d["const"], out)
    got = run_bass_kernel_spmd(nc, [{"in_" + n: v for n, v in arrays.items()}], core_ids=[0]).results[0]["out_0"]
    return got.reshape(B, S, C)
```
